# Optimizing a Trainium2 kernel written in Bass

```python
import numpy as np
import jax
import jax.numpy as jnp

def _softmax(x, axis=-1):
    return jax.nn.softmax(x, axis=axis)

def _gelu(x):
    return jax.nn.gelu(x, approximate=True)

def _silu(x):
    return jax.nn.silu(x)

def _sigmoid(x):
    return jax.nn.sigmoid(x)

def _layernorm(x, axis=-1, eps=1e-05):
    m = jnp.mean(x, axis=axis, keepdims=True)
    v = jnp.var(x, axis=axis, keepdims=True)
    return (x - m) / jnp.sqrt(v + eps)

def _scatter_add(tgt, idx, src, axis=0):
    return tgt.at[idx].add(src)

def _segment_sum(src, seg, n):
    return jax.ops.segment_sum(src, seg, n)
kernel_name = 'mk_gnn_ffn_d1_gnn_r8_fdf1f8'

def setup_inputs(seed: int=0):
    np.random.seed(seed)
    _w = jnp.asarray

    def _rec_inputs():
        import jax
        import jax.numpy as jnp
        _gk = jax.random.key(seed)
        x = -0.0002117 + 1 * jax.random.normal(jax.random.fold_in(_gk, 1), (12500, 256), jnp.float32)
        _s = jax.random.randint(jax.random.fold_in(_gk, 2), (100000,), 0, 12500, jnp.int32)
        _d = jax.random.randint(jax.random.fold_in(_gk, 3), (100000,), 0, 12500, jnp.int32)
        _loop = jnp.arange(12500, dtype=jnp.int32)
        src = jnp.concatenate([_s, _d, _loop])
        dst = jnp.concatenate([_d, _s, _loop])
        _o = jnp.argsort(dst, stable=True)
        src = src[_o]
        dst = dst[_o]
        edge_weight = jax.random.uniform(jax.random.fold_in(_gk, 12), (212500,), jnp.float32, 0.0, 1)
        return (x, src, dst, edge_weight)
    x, src, dst, edge_weight = _rec_inputs()

    def _L0_gnn_setup():
        import jax, jax.numpy as jnp
        import numpy as np
        N_NODES = 12500
        N_EDGES = 400000
        IN_C = 256
        OUT_C = 256
        key = jax.random.key(seed)
        k1, k2, k3, k4, k5 = jax.random.split(key, 5)
        limit = float(np.sqrt(6.0 / (IN_C + OUT_C)))
        W = jax.random.uniform(k2, (IN_C, OUT_C), jnp.float32, -limit, limit)
        return {'x': jax.random.normal(k1, (N_NODES, IN_C), jnp.float32), 'W': W, 'bias': jnp.zeros((OUT_C,), jnp.float32), 'edge_row': jax.random.randint(k3, (N_EDGES,), 0, N_NODES, jnp.int32), 'edge_col': jax.random.randint(k4, (N_EDGES,), 0, N_NODES, jnp.int32), 'edge_val': jax.random.uniform(k5, (N_EDGES,), jnp.float32)}
    _L0_gnn_all = _L0_gnn_setup()
    _L0_gnn_in = {k: v for k, v in _L0_gnn_all.items() if k in ('W', 'bias')}
    del _L0_gnn_all

    def _L0_ffn_setup():
        import jax, jax.numpy as jnp
        import numpy as np
        B, S, D = (8, 512, 256)
        H = 4 * D
        CAPACITY = 0.5
        key = jax.random.key(seed)
        ks = jax.random.split(key, 6)
        x = jax.random.normal(ks[0], (B, S, D), dtype=jnp.float32)
        attention_mask = jnp.zeros((B, 1, 1, S), dtype=jnp.float32)
        wr = jax.random.normal(ks[1], (D, 1), dtype=jnp.float32) * 0.02
        br = jnp.zeros((1,), dtype=jnp.float32)
        w1 = jax.random.normal(ks[2], (D, H), dtype=jnp.float32) * 0.02
        b1 = jnp.zeros((H,), dtype=jnp.float32)
        w2 = jax.random.normal(ks[3], (H, D), dtype=jnp.float32) * 0.02
        b2 = jnp.zeros((D,), dtype=jnp.float32)
        return {'x': x, 'attention_mask': attention_mask, 'wr': wr, 'br': br, 'w1': w1, 'b1': b1, 'w2': w2, 'b2': b2}
    _L0_ffn_all = _L0_ffn_setup()
    _L0_ffn_in = {k: v for k, v in _L0_ffn_all.items() if k in ('attention_mask', 'wr', 'br', 'w1', 'b1', 'w2', 'b2')}
    del _L0_ffn_all
    return {'x': x, 'src': src, 'dst': dst, 'edge_weight': edge_weight, 'L0_gnn_W': _L0_gnn_in['W'], 'L0_gnn_bias': _L0_gnn_in['bias'], 'L0_ffn_attention_mask': _L0_ffn_in['attention_mask'], 'L0_ffn_wr': _L0_ffn_in['wr'], 'L0_ffn_br': _L0_ffn_in['br'], 'L0_ffn_w1': _L0_ffn_in['w1'], 'L0_ffn_b1': _L0_ffn_in['b1'], 'L0_ffn_w2': _L0_ffn_in['w2'], 'L0_ffn_b2': _L0_ffn_in['b2']}

def reference(x, src, dst, edge_weight, L0_gnn_W, L0_gnn_bias, L0_ffn_attention_mask, L0_ffn_wr, L0_ffn_br, L0_ffn_w1, L0_ffn_b1, L0_ffn_w2, L0_ffn_b2):
    import jax
    import jax.numpy as jnp

    def _L0_gnn_ref(x, W, bias, edge_row, edge_col, edge_val):
        import jax, jax.numpy as jnp
        import numpy as np
        N_NODES = 12500
        N_EDGES = 400000
        IN_C = 256
        OUT_C = 256
        h = x @ W
        msgs = h[edge_col] * edge_val[:, None]
        agg = jax.ops.segment_sum(msgs, edge_row, num_segments=N_NODES)
        return agg + bias

    def _L0_ffn_ref(x, attention_mask, wr, br, w1, b1, w2, b2):
        import jax, jax.numpy as jnp
        import numpy as np
        B, S, D = (8, 512, 256)
        H = 4 * D
        CAPACITY = 0.5
        b, s, d = x.shape
        weights = (jnp.einsum('bsd,do->bso', x, wr) + br)[..., 0]
        k = max(1, int(CAPACITY * s))
        kk = k - 1 if k > 1 else 1
        _, idx = jax.lax.top_k(weights, k)
        sel_idx = idx[:, :kk]
        sel = jnp.take_along_axis(x, sel_idx[:, :, None], axis=1)
        h = jax.nn.gelu(jnp.einsum('bkd,dh->bkh', sel, w1) + b1)
        y = jnp.einsum('bkh,hd->bkd', h, w2) + b2
        w_sel = jnp.take_along_axis(weights, sel_idx, axis=1)
        y = y * w_sel[..., None]
        batch_idx = jnp.arange(b)[:, None]
        processed = jnp.zeros_like(x).at[batch_idx, sel_idx].set(y)
        return processed + x
    x = x + _L0_gnn_ref(_layernorm(x, axis=-1), L0_gnn_W, L0_gnn_bias, src, dst, edge_weight)
    x = x + _L0_ffn_ref(_layernorm(x, axis=-1)[None], L0_ffn_attention_mask, L0_ffn_wr, L0_ffn_br, L0_ffn_w1, L0_ffn_b1, L0_ffn_w2, L0_ffn_b2)[0]
    return x

_drawn_inputs = setup_inputs


def setup_inputs(seed=0):
    import zlib

    import numpy as np

    out = dict(_drawn_inputs(seed))
    spreads = {'L0_gnn_bias': (0.0, 0.1), 'L0_ffn_b1': (0.0, 0.8), 'L0_ffn_b2': (0.0, 0.8)}
    factors = {'L0_ffn_wr': 6.09, 'L0_ffn_w1': 6.145, 'L0_ffn_w2': 5.744}
    for name, (base, spread) in spreads.items():
        noise = np.random.default_rng([zlib.crc32(name.encode()), seed]).standard_normal(out[name].shape)
        drawn = base * np.exp(spread * noise) if base else spread * noise
        out[name] = jnp.asarray(drawn.astype(out[name].dtype))
    for name, factor in factors.items():
        out[name] = (out[name] * factor).astype(out[name].dtype)
    return out
```

```python
from contextlib import ExitStack

import concourse.bass as bass
from concourse import mybir

P = 128
F32 = mybir.dt.float32
BF16 = mybir.dt.bfloat16
I32 = mybir.dt.int32
ALU = mybir.AluOpType
ACT = mybir.ActivationFunctionType
AX = mybir.AxisListType

EPS = 1e-5
TABLES = 4
ZERO_DMAS = 4
EDGES_PER_SUPER = 1024
CH = EDGES_PER_SUPER // P
SUPERS = 2
BATCH = 4
TG = 4
NFIELD = 5
SRC, REL, WGT, SPARE, DST = range(NFIELD)


class Steps:

    def __init__(self, engine, sem):
        self.engine, self.sem, self.base, self.k = engine, sem, 0, 0

    def rebase(self, base):
        self.base, self.k = base, 0

    def wait(self, instruction):
        instruction.then_inc(self.sem, 1)
        self.k += 1
        self.engine.wait_ge(self.sem, self.base + self.k)


def wait_if(engine, sem, value):
    if not isinstance(value, int) or value > 0:
        engine.wait_ge(sem, value)


def build_constants(nc, k, sem):
    g = nc.gpsimd
    st = Steps(g, sem)
    st.wait(g.memset(k["ident"][:], 0.0))
    st.wait(g.affine_select(out=k["ident"][:], in_=k["ident"][:], compare_op=ALU.not_equal, fill=1.0,
                            base=0, pattern=[[-1, P]], channel_multiplier=1))
    st.wait(g.memset(k["lower"][:], 1.0))
    st.wait(g.affine_select(out=k["lower"][:], in_=k["lower"][:], compare_op=ALU.is_gt, fill=0.0,
                            base=0, pattern=[[-1, P]], channel_multiplier=1))
    st.wait(g.memset(k["before"][:], 1.0))
    st.wait(g.affine_select(out=k["before"][:], in_=k["before"][:], compare_op=ALU.is_gt, fill=0.0,
                            base=0, pattern=[[1, P]], channel_multiplier=-1))
    st.wait(g.memset(k["ones"][:], 1.0))
    st.wait(g.iota(k["row"][:], pattern=[[1, P]], base=0, channel_multiplier=0,
                   allow_small_or_imprecise_dtypes=True))
    st.wait(g.iota(k["col"][:], pattern=[[0, 1]], base=0, channel_multiplier=1,
                   allow_small_or_imprecise_dtypes=True))
    st.wait(g.memset(k["eps"][:], EPS))
    st.wait(g.memset(k["zero"][:], 0.0))
    return st.k


def build(nc, x, src, dst, wgt, W, bias, wr, br, w1, b1, w2, b2, out):
    N, D = x.shape
    E = src.shape[0]
    H = w1.shape[1]
    KD, KH = D // P, H // P
    NT = -(-N // P)
    LAST = N - (NT - 1) * P
    GROUPS = NT // TG
    TAIL = NT - GROUPS * TG
    S = -(-E // EDGES_PER_SUPER)
    S += S % SUPERS
    Q = S // SUPERS
    OVER = S * EDGES_PER_SUPER - E
    BATCHES = SUPERS * CH // BATCH
    NCH = SUPERS * CH
    KEPT = max(1, int(0.5 * N)) - 1
    SLOTS = -(-KEPT // P)
    SG = SLOTS // TG
    STAIL = SLOTS - SG * TG
    assert Q <= P and OVER < EDGES_PER_SUPER and GROUPS % 2 == 0 and TAIL and SG % 2 == 0 and STAIL == 1
    ROWS = P * ZERO_DMAS * (-(-(NT * P + P) // (P * ZERO_DMAS)))

    h_dram = nc.dram_tensor("h_rows", [N, D], F32, kind="Internal").ap()
    xn_dram = nc.dram_tensor("xn_rows", [NT * P, D], F32, kind="Internal").ap()
    tables = [nc.dram_tensor(f"aggregate{i}", [ROWS, D], F32, kind="Internal").ap() for i in range(TABLES)]

    def tile_rows(a, g, tiles=TG):
        return a[bass.ds(g * (TG * P), tiles * P), :].rearrange("(t p) d -> p t d", p=P)

    with ExitStack() as whole:
        def sb(ctx, name, shape, dt=F32):
            return ctx.enter_context(nc.sbuf_tensor(name, shape, dt))

        def sem(name):
            return whole.enter_context(nc.semaphore(name))

        consts = {
            "ident": sb(whole, "ident", [P, P]),
            "lower": sb(whole, "lower", [P, P]),
            "before": sb(whole, "before", [P, P], BF16),
            "ones": sb(whole, "ones", [P, P]),
            "row": sb(whole, "row", [P, P]),
            "col": sb(whole, "col", [P, 1]),
            "eps": sb(whole, "eps", [P, 1]),
            "zero": sb(whole, "zero", [P, 5 * D]),
        }
        ident, lower, before, ones = (consts[n] for n in ("ident", "lower", "before", "ones"))
        row, col, zero = (consts[n] for n in ("row", "col", "zero"))
        w1_sb = sb(whole, "w1_sb", [P, KD, H])
        w2_sb = sb(whole, "w2_sb", [P, KH, D])
        b1_sb = sb(whole, "b1_sb", [P, KH])
        b2_sb = sb(whole, "b2_sb", [P, D])
        wr_sb = sb(whole, "wr_sb", [P, D])
        br_sb = sb(whole, "br_sb", [P, 1])
        bias_sb = sb(whole, "bias_sb", [P, D])

        consts_ready = sem("consts_ready")
        weights_loaded = sem("weights_loaded")
        table_cleared = [sem(f"table_cleared{i}") for i in range(TABLES)]
        table_added = [sem(f"table_added{i}") for i in range(TABLES)]
        CONSTS = 11

        held = sem("held")

        def hold(engine):
            engine.sem_inc(held, 1)

        eps = consts["eps"]

        with ExitStack() as edge_ctx:
            edges = sb(edge_ctx, "edges", [P, Q + 1, SUPERS, NFIELD, CH])
            window_row = sb(edge_ctx, "window_row", [1, Q, SUPERS], I32)
            flag = sb(edge_ctx, "flag", [1, 1], I32)
            project(nc, locals())
            edge_sums(nc, locals())
        with ExitStack() as late:
            base = sb(late, "base", [P, NT, D])
            kept_row = sb(late, "kept_row", [P, SLOTS], I32)
            wts = sb(late, "wts", [P, NT])
            base_stored = sem("base_stored")
            combine(nc, locals())
            choose(nc, locals())
            ffn(nc, locals())


def project(nc, v):
    hold = v['hold']
    (x, src, dst, wgt, W, h_dram, consts, edges, window_row, flag, tables, table_cleared, table_added, sem, sb) = (
        v[n] for n in "x src dst wgt W h_dram consts edges window_row flag tables table_cleared table_added sem sb".split())
    N, D, Q, OVER, KD, GROUPS, TAIL, LAST, ROWS = (v[n] for n in "N D Q OVER KD GROUPS TAIL LAST ROWS".split())
    ident, zero, col = consts["ident"], consts["zero"], consts["col"]
    consts_ready, weights_loaded = v["consts_ready"], v["weights_loaded"]
    tile_rows = v["tile_rows"]
    E1 = EDGES_PER_SUPER
    with ExitStack() as c:
        def ps(name, shape):
            return c.enter_context(nc.psum_tensor(name, shape, F32))

        W_sb = sb(c, "W_sb", [P, KD, D])
        src_i = sb(c, "src_i", [Q, SUPERS, E1], I32)
        dst_i = sb(c, "dst_i", [Q, SUPERS, E1], I32)
        lists = [sb(c, n, [Q, SUPERS, E1]) for n in ("src_f", "rel_f", "wgt_f", "dst_f")]
        src_f, rel_f, wgt_f, dst_f = lists
        fields = (SRC, REL, WGT, DST)
        lo = sb(c, "lo", [Q, SUPERS])
        hi = sb(c, "hi", [Q, SUPERS])
        spread = sb(c, "spread", [Q, SUPERS])
        first = sb(c, "first", [Q, SUPERS])
        wide = sb(c, "wide", [Q, SUPERS])
        wide_row = sb(c, "wide_row", [1, SUPERS, Q])
        any_wide = sb(c, "any_wide", [1, 1])
        spare = sb(c, "spare", [P, 1])
        x_in = sb(c, "x_in", [P, 2, TG, D])
        stats = sb(c, "stats", [P, TG, 6])
        mv = sb(c, "mv", [P, TG, 2])
        std = sb(c, "std", [P, TG])
        xn = sb(c, "xn", [P, 2, TG, D])
        xnT = sb(c, "xnT", [P, 2, KD, TG * P])
        h_sb = sb(c, "h_sb", [P, 2, TG, D])
        turn_ps = [ps(f"turn_ps{i}", [P, 4, P]) for i in range(2)]
        xt_ps = ps("xt_ps", [P, KD, TG * P])
        h_ps = [ps(f"h_ps{i}", [P, TG, D]) for i in range(2)]

        edges_loaded = sem("edges_loaded")
        lists_ready = sem("lists_ready")
        turned = sem("turned")
        turn_copied = sem("turn_copied")
        meta_turned = sem("meta_turned")
        W_loaded = sem("W_loaded")
        x_loaded = [sem(f"x_loaded{i}") for i in range(2)]
        norm_done = sem("norm_done")
        x_turned = sem("x_turned")
        xt_copied = sem("xt_copied")
        h_done = sem("h_done")
        mv_ready = sem("mv_ready")
        std_ready = sem("std_ready")
        h_copied = sem("h_copied")
        h_stored = [sem(f"h_stored{i}") for i in range(2)]
        dve_step = sem("project_dve_step")
        NTURN = len(lists) * SUPERS * (CH // 4)
        NG = GROUPS + 1
        EDGE_DMAS = 12

        block = c.enter_context(nc.Block())

        @block.gpsimd
        def _(pool):
            n = build_constants(nc, consts, consts_ready)
            assert n == v["CONSTS"]

        @block.sync
        def _(sp):
            sp.dma_start(W_sb[:], W.rearrange("(k p) n -> p k n", p=P)).then_inc(W_loaded, 16)
            for a, t in ((src, src_i), (dst, dst_i), (wgt, wgt_f)):
                sp.dma_start(t[0:1, 0, :], a[0:E1].rearrange("(o e) -> o e", o=1)).then_inc(edges_loaded, 16)
                sp.dma_start(t[0:1, 1, :], a[E1 - OVER:2 * E1 - OVER].rearrange("(o e) -> o e", o=1)).then_inc(edges_loaded, 16)
                for q0, q1 in ((1, 8), (8, Q)):
                    sp.dma_start(t[q0:q1, :, :], a[q0 * SUPERS * E1 - OVER:q1 * SUPERS * E1 - OVER]
                                 .rearrange("(q g e) -> q g e", g=SUPERS, e=E1)).then_inc(edges_loaded, 16)

            def load(i, b, tiles=TG):
                g = 2 * i + b
                wait_if(sp, norm_done, g - 1)
                if tiles == TG:
                    sp.dma_start(x_in[:, b, :, :], tile_rows(x, g)).then_inc(x_loaded[b], 16)
                else:
                    n0 = GROUPS * TG * P
                    sp.dma_start(x_in[:, b, 0:tiles - 1, :], x[n0:n0 + (tiles - 1) * P, :]
                                 .rearrange("(t p) d -> p t d", p=P)).then_inc(x_loaded[b], 16)
                    sp.dma_start(x_in[0:LAST, b, tiles - 1, :], x[N - LAST:N, :]).then_inc(x_loaded[b], 16)

            def store(i, b, tiles=TG):
                g = 2 * i + b
                sp.wait_ge(h_copied, g + 1)
                if tiles == TG:
                    sp.dma_start(tile_rows(h_dram, g), h_sb[:, b, :, :]).then_inc(h_stored[b], 16)
                else:
                    n0 = GROUPS * TG * P
                    sp.dma_start(h_dram[n0:n0 + (tiles - 1) * P, :].rearrange("(t p) d -> p t d", p=P),
                                 h_sb[:, b, 0:tiles - 1, :]).then_inc(h_stored[b], 16)
                    sp.dma_start(h_dram[N - LAST:N, :], h_sb[0:LAST, b, tiles - 1, :]).then_inc(h_stored[b], 16)

            load(0, 0)
            load(0, 1)
            with sp.Fori(1, GROUPS // 2) as i:
                for b in range(2):
                    load(i, b)
                    store(i - 1, b)
            load(GROUPS // 2, 0, TAIL)
            store(GROUPS // 2 - 1, 0)
            store(GROUPS // 2 - 1, 1)
            store(GROUPS // 2, 0, TAIL)
            sp.wait_ge(h_stored[0], 16 * (GROUPS // 2 + 2))
            sp.wait_ge(h_stored[1], 16 * (GROUPS // 2))

        @block.scalar
        def _(act):
            act.wait_ge(consts_ready, v["CONSTS"])
            per = ROWS // P // ZERO_DMAS
            runs = 5
            assert per % runs == 0
            for z in range(ZERO_DMAS):
                for t in range(TABLES):
                    to = tables[t].rearrange("(z p r) d -> z p (r d)", z=ZERO_DMAS, p=P)[z]
                    to = to.rearrange("p (n m) -> p n m", m=runs * D)
                    act.dma_start(to, zero[:].unsqueeze(1).to_broadcast([P, per // runs, runs * D])).then_inc(table_cleared[t], 16)
            for a, t in ((v["w1"].rearrange("(k p) n -> p k n", p=P), v["w1_sb"]),
                         (v["w2"].rearrange("(k p) n -> p k n", p=P), v["w2_sb"]),
                         (v["b2"].partition_broadcast(P), v["b2_sb"]),
                         (v["wr"].rearrange("n o -> (n o)").partition_broadcast(P), v["wr_sb"]),
                         (v["br"].partition_broadcast(P), v["br_sb"]),
                         (v["bias"].partition_broadcast(P), v["bias_sb"])):
                act.dma_start(t[:], a).then_inc(weights_loaded, 16)
            with nc.allow_non_contiguous_dma(reason="the bias of the first product, once"):
                act.dma_start(v["b1_sb"][:], v["b1"].rearrange("(c p) -> p c", p=P)).then_inc(weights_loaded, 16)

            for n in range(NTURN):
                f, g, half = n // (SUPERS * 2), n // 2 % SUPERS, n % 2
                act.wait_ge(turned, n + 1)
                act.activation(edges[:, 0:Q, g, fields[f], 4 * half:4 * half + 4],
                               turn_ps[n % 2][:, :, 0:Q].rearrange("p k q -> p q k"), ACT.Copy).then_inc(turn_copied, 1)

            def xt_copy(i, b, tiles=TG):
                g = 2 * i + b
                act.wait_ge(mv_ready, g + 1)
                act.activation(std[:, 0:tiles], mv[:, 0:tiles, 1], ACT.Sqrt, bias=v["eps"][:]).then_inc(std_ready, 1)
                act.wait_ge(x_turned, g + 1)
                wait_if(act, h_done, g - 1)
                act.activation(xnT[:, b, :, 0:tiles * P], xt_ps[:, :, 0:tiles * P], ACT.Copy).then_inc(xt_copied, 1)

            def h_copy(i, b, tiles=TG, first=False):
                g = 2 * i + b
                act.wait_ge(h_done, g + 1)
                wait_if(act, h_stored[b], 16 * i)
                act.activation(h_sb[:, b, 0:tiles, :], h_ps[b][:, 0:tiles, :], ACT.Copy).then_inc(h_copied, 1)

            xt_copy(0, 0)
            xt_copy(0, 1)
            h_copy(0, 0)
            with act.Fori(1, GROUPS // 2) as i:
                xt_copy(i, 0)
                h_copy(i - 1, 1)
                xt_copy(i, 1)
                h_copy(i, 0)
            xt_copy(GROUPS // 2, 0, TAIL)
            h_copy(GROUPS // 2 - 1, 1)
            h_copy(GROUPS // 2, 0, TAIL)

        @block.vector
        def _(dve):
            st = Steps(dve, dve_step)
            vec = nc.vector
            dve.wait_ge(edges_loaded, 16 * EDGE_DMAS)
            vec.memset(wgt_f[0:1, 0, E1 - OVER:E1], 0.0)
            vec.tensor_copy(src_f[:], src_i[:])
            vec.memset(edges[:, Q, :, :, :], 0.0)
            dve.wait_ge(consts_ready, v["CONSTS"])
            vec.tensor_scalar(spare[:], col[:], float(N), None, ALU.add)
            st.wait(vec.tensor_copy(dst_f[:], dst_i[:]))
            vec.tensor_reduce(lo[:], dst_f[:], op=ALU.min, axis=AX.X)
            st.wait(vec.tensor_reduce(hi[:], dst_f[:], op=ALU.max, axis=AX.X))
            st.wait(vec.tensor_scalar(first[:], lo[:], float(N - P), None, ALU.min))
            for g in range(SUPERS):
                vec.tensor_scalar(rel_f[:, g, :], dst_f[:, g, :], first[:, g:g + 1], None, ALU.subtract)
            st.wait(vec.tensor_tensor(spread[:], hi[:], first[:], ALU.subtract))
            vec.tensor_scalar(wide[:], spread[:], float(P), None, ALU.is_ge).then_inc(lists_ready, 1)
            dve.wait_ge(meta_turned, 1)
            vec.tensor_copy(window_row[0:1, :, :].rearrange("o q g -> o g q"), turn_ps[0][0:1, 0:SUPERS, 0:Q])
            st.wait(vec.tensor_copy(wide_row[:], turn_ps[1][0:1, 0:SUPERS, 0:Q]))
            st.wait(vec.tensor_reduce(any_wide[:], wide_row[:].rearrange("o g q -> o (g q)"), op=ALU.max, axis=AX.X))
            vec.tensor_copy(flag[:], any_wide[:])
            dve.wait_ge(turn_copied, NTURN)
            for g in range(SUPERS):
                vec.tensor_scalar(edges[:, 0:Q, g, SPARE, :], edges[:, 0:Q, g, SRC, :], -1.0, spare[:], ALU.mult, ALU.add)
            per_group = 0

            def norm(i, b, tiles=TG):
                g = 2 * i + b
                dve.wait_ge(x_loaded[b], 16 * (i + 1) if tiles == TG else 16 * (i + 2))
                for t in range(tiles):
                    last = vec.bn_stats(stats[:, t, :], x_in[:, b, t, :])
                st.wait(last)
                hold(dve)
                for t in range(tiles):
                    last = vec.bn_aggr(mv[:, t, :], stats[:, t, :])
                last.then_inc(mv_ready, 1)
                dve.wait_ge(std_ready, g + 1)
                st.wait(vec.reciprocal(std[:, 0:tiles], std[:, 0:tiles]))
                wait_if(dve, x_turned, g - 1)
                for t in range(tiles):
                    last = vec.tensor_scalar(xn[:, b, t, :], x_in[:, b, t, :], mv[:, t, 0:1], std[:, t:t + 1],
                                             ALU.subtract, ALU.mult)
                last.then_inc(norm_done, 1)

            norm(0, 0)
            norm(0, 1)
            before_loop, a_step = st.k, 2 * 2
            with dve.Fori(1, GROUPS // 2) as i:
                st.rebase(before_loop + (i - 1) * a_step)
                norm(i, 0)
                norm(i, 1)
            st.rebase(before_loop + (GROUPS // 2 - 1) * a_step)
            norm(GROUPS // 2, 0, TAIL)

        @block.tensor
        def _(pe):
            t = nc.tensor
            pe.wait_ge(consts_ready, v["CONSTS"])
            pe.wait_ge(lists_ready, 1)
            for g in range(SUPERS):
                t.transpose(turn_ps[0][0:1, g, 0:Q], first[:, g:g + 1], ident[0:Q, 0:Q])
                last = t.transpose(turn_ps[1][0:1, g, 0:Q], wide[:, g:g + 1], ident[0:Q, 0:Q])
            last.then_inc(meta_turned, 1)
            pe.wait_ge(dve_step, 6)
            for n in range(NTURN):
                f, g, half = n // (SUPERS * 2), n // 2 % SUPERS, n % 2
                wait_if(pe, turn_copied, n - 1)
                for k in range(4):
                    e0 = (4 * half + k) * P
                    last = t.transpose(turn_ps[n % 2][:, k, 0:Q], lists[f][:, g, e0:e0 + P], ident[0:Q, 0:Q])
                last.then_inc(turned, 1)
            pe.wait_ge(W_loaded, 16)

            def turn(i, b, tiles=TG):
                g = 2 * i + b
                pe.wait_ge(norm_done, g + 1)
                wait_if(pe, xt_copied, g)
                for j in range(tiles):
                    for k in range(KD):
                        last = t.transpose(xt_ps[:, k, j * P:(j + 1) * P], xn[:, b, j, k * P:(k + 1) * P], ident[:])
                last.then_inc(x_turned, 1)

            def product(i, b, tiles=TG):
                g = 2 * i + b
                pe.wait_ge(xt_copied, g + 1)
                wait_if(pe, h_copied, g - 1)
                for j in range(tiles):
                    for k in range(KD):
                        last = t.matmul(h_ps[b][:, j, :], lhsT=xnT[:, b, k, j * P:(j + 1) * P], rhs=W_sb[:, k, :],
                                        start=(k == 0), stop=(k == KD - 1))
                last.then_inc(h_done, 1)

            turn(0, 0)
            turn(0, 1)
            product(0, 0)
            with pe.Fori(1, GROUPS // 2) as i:
                turn(i, 0)
                product(i - 1, 1)
                turn(i, 1)
                product(i, 0)
            turn(GROUPS // 2, 0, TAIL)
            product(GROUPS // 2 - 1, 1)
            product(GROUPS // 2, 0, TAIL)


def edge_sums(nc, v):
    hold = v['hold']
    (h_dram, consts, edges, window_row, flag, tables, table_cleared, table_added, sem, sb) = (
        v[n] for n in "h_dram consts edges window_row flag tables table_cleared table_added sem sb".split())
    N, D, Q, NCH, BATCHES, ROWS = (v[n] for n in "N D Q NCH BATCHES ROWS".split())
    ident, lower, row = consts["ident"], consts["lower"], consts["row"]
    PER_SUPER = CH // BATCH
    with ExitStack() as c:
        def ps(name, shape):
            return c.enter_context(nc.psum_tensor(name, shape, F32))

        cur = sb(c, "cur", [P, SUPERS, NFIELD, CH])
        same = sb(c, "same", [P, 2, BATCH, P])
        earlier = sb(c, "earlier", [P, BATCH, P])
        dups = sb(c, "dups", [P, BATCH])
        moved = sb(c, "moved", [P, BATCH])
        pick = sb(c, "pick", [P, 2, BATCH, P])
        mix_sb = sb(c, "mix_sb", [P, 2, BATCH, P])
        window = sb(c, "window", [P, SUPERS, D])
        gathered = sb(c, "gathered", [P, SUPERS, CH, D])
        target = sb(c, "target", [P, SUPERS, CH], I32)
        put_row = sb(c, "put_row", [P, NCH], I32)
        msg = sb(c, "msg", [P, 2 * BATCH, D])
        src_ps = [ps(f"src_ps{i}", [P, BATCH, P]) for i in range(2)]
        mix_ps = [ps(f"mix_ps{i}", [P, BATCH, P]) for i in range(2)]
        msg_ps = [ps(f"msg_ps{i}", [P, 2, D]) for i in range(4)]

        cur_ready = sem("cur_ready")
        src_turned = sem("src_turned")
        picked = sem("picked")
        rows_ready = sem("rows_ready")
        mix_done = sem("mix_done")
        mix_copied = sem("mix_copied")
        msg_done = sem("msg_done")
        msg_copied = sem("msg_copied")
        window_loaded = [sem(f"window_loaded{i}") for i in range(SUPERS)]
        target_ready = sem("target_ready")
        rows_gathered = [sem(f"rows_gathered{i}") for i in range(SUPERS)]
        edge_step = sem("edge_dve_step")

        block = c.enter_context(nc.Block())

        def steps(engine, body):
            body(0)
            with engine.Fori(1, Q) as q:
                body(q)

        def vector_body(dve, general):
            vec = nc.vector
            st = Steps(dve, edge_step)


            def body(q):
                for g in range(SUPERS):
                    dve.wait_ge(cur_ready, SUPERS * q + g + 1)
                    wait_if(dve, picked, PER_SUPER * (SUPERS * q + g))
                    wait_if(dve, rows_ready, PER_SUPER * (SUPERS * q + g))
                    nq, ng = (q, 1) if g == 0 else (q + 1, 0)
                    vec.tensor_copy(cur[:, ng, :, :], edges[:, bass.ds(nq, 1), ng, :, :]
                                    .rearrange("p o f k -> p (o f) k")).then_inc(cur_ready, 1)
                    if general:
                        wait_if(dve, rows_gathered[g], 16 * CH * q)
                        vec.tensor_copy(target[:, g, :], cur[:, g, DST, :]).then_inc(target_ready, 1)
                    for hb in range(PER_SUPER):
                        t = BATCHES * q + PER_SUPER * g + hb
                        r = hb % 2
                        k0 = hb * BATCH
                        dve.wait_ge(src_turned, t + 1)
                        if not general:
                            wait_if(dve, mix_done, t - 1)
                        s4 = cur[:, g, SRC, k0:k0 + BATCH]
                        st.wait(vec.tensor_tensor(same[:, r, :, :], src_ps[r][:],
                                                  s4.unsqueeze(2).to_broadcast([P, BATCH, P]), ALU.is_equal))
                        st.wait(vec.tensor_tensor(earlier[:], same[:, r, :, :],
                                                  lower[:].unsqueeze(1).to_broadcast([P, BATCH, P]), ALU.mult))
                        st.wait(vec.tensor_reduce(dups[:], earlier[:], op=ALU.add, axis=AX.X))
                        st.wait(vec.scalar_tensor_tensor(out=moved[:], in0=dups[:], scalar=1.0,
                                                         in1=cur[:, g, SPARE, k0:k0 + BATCH], op0=ALU.min, op1=ALU.mult))
                        slot = g * CH + k0
                        for j in range(TABLES):
                            value = 16 * (t + 1 - BATCHES)
                            if not (isinstance(q, int)):
                                dve.wait_ge(table_added[j], value)
                        vec.tensor_tensor(put_row[:, slot:slot + BATCH], moved[:], s4, ALU.add).then_inc(rows_ready, 1)
                        if general:
                            wait_if(dve, msg_done, 2 * t - 2)
                        for k in range(BATCH):
                            last = vec.tensor_scalar(
                                pick[:, r, k, :], src_ps[r][:, k, :] if general else row[:],
                                cur[:, g, SRC if general else REL, k0 + k:k0 + k + 1],
                                cur[:, g, WGT, k0 + k:k0 + k + 1], ALU.is_equal, ALU.mult)
                        last.then_inc(picked, 1)

            a_step = 4 * BATCHES
            vec.tensor_copy(cur[:, 0, :, :], edges[:, 0, 0, :, :]).then_inc(cur_ready, 1)
            first = st.k
            body(0)
            assert st.k == first + a_step
            with dve.Fori(1, Q) as q:
                st.rebase(first + q * a_step)
                body(q)

        @block.vector
        def _(dve):
            wide = dve.value_load(flag[0:1, 0:1], min_val=0, max_val=1)
            with dve.If(wide):
                vector_body(dve, True)
            with dve.Else():
                vector_body(dve, False)

        def tensor_body(pe, general):
            t_ = nc.tensor

            def sources(q, bt):
                t, g, hb = BATCHES * q + bt, bt // PER_SUPER, bt % PER_SUPER
                pe.wait_ge(cur_ready, SUPERS * q + g + 1)
                wait_if(pe, picked, t - 1)
                for k in range(BATCH):
                    col_ap = cur[:, g, SRC, hb * BATCH + k:hb * BATCH + k + 1]
                    last = t_.transpose(src_ps[bt % 2][:, k, :], col_ap.to_broadcast([P, P]), ident[:])
                last.then_inc(src_turned, 1)

            def mix(t, bt):
                pe.wait_ge(picked, t + 1)
                wait_if(pe, mix_copied, t - 1)
                for k in range(BATCH):
                    last = t_.matmul(mix_ps[bt % 2][:, k, :], lhsT=pick[:, bt % 2, k, :], rhs=same[:, bt % 2, k, :],
                                     start=True, stop=True)
                last.then_inc(mix_done, 1)

            def message(t, q, bt):
                g, hb = bt // PER_SUPER, bt % PER_SUPER
                if general:
                    pe.wait_ge(picked, t + 1)
                    pe.wait_ge(rows_gathered[g], 16 * CH * (q + 1))
                else:
                    pe.wait_ge(mix_copied, t + 1)
                    pe.wait_ge(window_loaded[g], 16 * (q + 1))
                for half in range(2):
                    wait_if(pe, msg_copied, 2 * t + half - 3)
                    for k in range(2):
                        kk = 2 * half + k
                        last = t_.matmul(msg_ps[(2 * bt + half) % 4][:, k, :],
                                         lhsT=pick[:, bt % 2, kk, :] if general else mix_sb[:, bt % 2, kk, :],
                                         rhs=gathered[:, g, hb * BATCH + kk, :] if general else window[:, g, :],
                                         start=True, stop=True)
                    last.then_inc(msg_done, 1)

            def body(q):
                first = isinstance(q, int)
                for bt in range(BATCHES):
                    t = BATCHES * q + bt
                    sources(q, bt)
                    if general:
                        if not (first and bt < 1):
                            message(t - 1, q if bt >= 1 else q - 1, (bt - 1) % BATCHES)
                        continue
                    if not (first and bt < 1):
                        mix(t - 1, (bt - 1) % BATCHES)
                    if not (first and bt < 2):
                        message(t - 2, q if bt >= 2 else q - 1, (bt - 2) % BATCHES)

            steps(pe, body)
            end = BATCHES * Q
            if general:
                message(end - 1, Q - 1, BATCHES - 1)
            else:
                mix(end - 1, BATCHES - 1)
                message(end - 2, Q - 1, BATCHES - 2)
                message(end - 1, Q - 1, BATCHES - 1)

        @block.tensor
        def _(pe):
            wide = pe.value_load(flag[0:1, 0:1], min_val=0, max_val=1)
            with pe.If(wide):
                tensor_body(pe, True)
            with pe.Else():
                tensor_body(pe, False)

        def scalar_body(act, general):
            def mix_copy(t, bt):
                act.wait_ge(mix_done, t + 1)
                wait_if(act, msg_done, 2 * t - 2)
                act.activation(mix_sb[:, bt % 2, :, :], mix_ps[bt % 2][:], ACT.Copy).then_inc(mix_copied, 1)

            def msg_copy(t, q, bt):
                for half in range(2):
                    act.wait_ge(msg_done, 2 * t + half + 1)
                    if not (isinstance(t, int) and t < 2):
                        for j in (2 * half, 2 * half + 1):
                            act.wait_ge(table_added[j], 16 * (t - 1))
                    k0 = (bt % 2) * BATCH + 2 * half
                    act.activation(msg[:, k0:k0 + 2, :], msg_ps[(2 * bt + half) % 4][:], ACT.Copy).then_inc(msg_copied, 1)

            def body(q):
                first = isinstance(q, int)
                for bt in range(BATCHES):
                    t = BATCHES * q + bt
                    if general:
                        msg_copy(t, q, bt)
                        continue
                    mix_copy(t, bt)
                    if not (first and bt < 1):
                        msg_copy(t - 1, q, (bt - 1) % BATCHES)

            steps(act, body)
            if not general:
                msg_copy(BATCHES * Q - 1, Q - 1, BATCHES - 1)

        @block.scalar
        def _(act):
            wide = act.value_load(flag[0:1, 0:1], min_val=0, max_val=1)
            with act.If(wide):
                scalar_body(act, True)
            with act.Else():
                scalar_body(act, False)

        @block.sync
        def _(sp):
            wide = sp.value_load(flag[0:1, 0:1], min_val=0, max_val=1)
            with sp.If(wide):
                sp.nop()
            with sp.Else():
                def body(q):
                    for g in range(SUPERS):
                        wait_if(sp, msg_done, 2 * PER_SUPER * (SUPERS * (q - 1) + g + 1))
                        r0 = sp.value_load(window_row[0:1, bass.ds(q, 1), g], min_val=0, max_val=N - P)
                        sp.dma_start(window[:, g, :], h_dram[bass.ds(r0, P), :]).then_inc(window_loaded[g], 16)

                steps(sp, body)

        def add_to_table(pool, q, bt):
            t = BATCHES * q + bt
            pool.wait_ge(rows_ready, t + 1)
            for j in range(BATCH):
                if j % 2 == 0:
                    pool.wait_ge(msg_copied, 2 * t + j // 2 + 1)
                if isinstance(t, int) and t == 0:
                    pool.wait_ge(table_cleared[j], 16 * ZERO_DMAS)
                wait_if(pool, table_added[j], 16 * t)
                slot = bt * BATCH + j
                hold(pool)
                pool.indirect_dma_start(
                    out=tables[j], out_offset=bass.IndirectOffsetOnAxis(ap=put_row[:, slot:slot + 1], axis=0),
                    in_=msg[:, (bt % 2) * BATCH + j, :], in_offset=None,
                    compute_op=ALU.add).then_inc(table_added[j], 16)

        def gather_rows(pool, q, g):
            pool.wait_ge(target_ready, SUPERS * q + g + 1)
            wait_if(pool, msg_done, 2 * PER_SUPER * (SUPERS * (q - 1) + g + 1))
            for k in range(CH):
                hold(pool)
                pool.indirect_dma_start(
                    out=gathered[:, g, k, :], out_offset=None, in_=h_dram,
                    in_offset=bass.IndirectOffsetOnAxis(ap=target[:, g, k:k + 1], axis=0)).then_inc(rows_gathered[g], 16)

        @block.gpsimd
        def _(pool):
            wide = pool.value_load(flag[0:1, 0:1], min_val=0, max_val=1)
            with pool.If(wide):
                def general_body(q):
                    for g in range(SUPERS):
                        gather_rows(pool, q, g)
                        for hb in range(PER_SUPER):
                            if g == 0 and not isinstance(q, int):
                                add_to_table(pool, q - 1, (SUPERS - 1) * PER_SUPER + hb)
                            elif g > 0:
                                add_to_table(pool, q, (g - 1) * PER_SUPER + hb)

                steps(pool, general_body)
                for hb in range(PER_SUPER):
                    add_to_table(pool, Q - 1, (SUPERS - 1) * PER_SUPER + hb)
            with pool.Else():
                def body(q):
                    for bt in range(BATCHES):
                        add_to_table(pool, q, bt)

                steps(pool, body)
            for j in range(TABLES):
                pool.wait_ge(table_added[j], 16 * BATCHES * Q)


def combine(nc, v):
    hold = v['hold']
    (x, xn_dram, tables, sem, sb, base, wts, wr_sb, br_sb, bias_sb, tile_rows) = (
        v[n] for n in "x xn_dram tables sem sb base wts wr_sb br_sb bias_sb tile_rows".split())
    N, D, GROUPS, TAIL, LAST, NT = (v[n] for n in "N D GROUPS TAIL LAST NT".split())
    with ExitStack() as c:
        parts = sb(c, "parts", [P, 2, TABLES, TG, D])
        xb = sb(c, "xb", [P, 2, TG, D])
        xn = sb(c, "xn1", [P, 2, TG, D])
        stats = sb(c, "stats1", [P, TG, 6])
        mv = sb(c, "mv1", [P, TG, 2])
        std = sb(c, "std1", [P, TG])
        junk = sb(c, "junk", [P, TG, D])
        wcur = sb(c, "wcur", [P, TG])
        loaded = [sem(f"parts_loaded{i}") for i in range(2)]
        pool_added = sem("pool_added")
        parts_used = sem("parts_used")
        xn_ready = sem("xn_ready")
        xn_stored = [sem(f"xn_stored{i}") for i in range(2)]
        step = sem("combine_dve_step")
        mv_ready = sem("mv1_ready")
        std_ready = sem("std1_ready")
        block = c.enter_context(nc.Block())

        @block.sync
        def _(sp):
            def load(i, b, tiles=TG):
                g = 2 * i + b
                wait_if(sp, parts_used, g - 1)
                for j in range(TABLES):
                    sp.dma_start(parts[:, b, j, 0:tiles, :], tile_rows(tables[j], g, tiles)).then_inc(loaded[b], 16)
                if tiles == TG:
                    sp.dma_start(xb[:, b, :, :], tile_rows(x, g)).then_inc(loaded[b], 16)
                else:
                    n0 = GROUPS * TG * P
                    sp.dma_start(xb[:, b, 0:tiles - 1, :], x[n0:n0 + (tiles - 1) * P, :]
                                 .rearrange("(t p) d -> p t d", p=P)).then_inc(loaded[b], 16)
                    sp.dma_start(xb[0:LAST, b, tiles - 1, :], x[N - LAST:N, :]).then_inc(loaded[b], 16)

            def store(i, b, tiles=TG):
                g = 2 * i + b
                sp.wait_ge(xn_ready, g + 1)
                sp.dma_start(tile_rows(xn_dram, g, tiles), xn[:, b, 0:tiles, :]).then_inc(xn_stored[b], 16)

            load(0, 0)
            load(0, 1)
            with sp.Fori(1, GROUPS // 2) as i:
                for b in range(2):
                    load(i, b)
                    store(i - 1, b)
            load(GROUPS // 2, 0, TAIL)
            store(GROUPS // 2 - 1, 0)
            store(GROUPS // 2 - 1, 1)
            store(GROUPS // 2, 0, TAIL)
            sp.wait_ge(xn_stored[0], 16 * (GROUPS // 2 + 1))
            sp.wait_ge(xn_stored[1], 16 * (GROUPS // 2))

        def landed(engine, i, b, tiles):
            engine.wait_ge(loaded[b], 16 * (TABLES + 1) * (i + 1) + (0 if tiles == TG else 16))

        @block.scalar
        def _(act):
            def root(g, tiles=TG):
                act.wait_ge(mv_ready, g + 1)
                act.activation(std[:, 0:tiles], mv[:, 0:tiles, 1], ACT.Sqrt, bias=v["eps"][:]).then_inc(std_ready, 1)

            root(0)
            with act.Fori(1, GROUPS) as g:
                root(g)
            root(GROUPS, TAIL)

        @block.gpsimd
        def _(pool):
            def add(i, b, tiles=TG):
                landed(pool, i, b, tiles)
                nc.gpsimd.tensor_tensor(parts[:, b, 2, 0:tiles, :], parts[:, b, 2, 0:tiles, :],
                                        parts[:, b, 3, 0:tiles, :], ALU.add)
                nc.gpsimd.tensor_tensor(xb[:, b, 0:tiles, :], xb[:, b, 0:tiles, :],
                                        bias_sb[:].unsqueeze(1).to_broadcast([P, tiles, D]), ALU.add).then_inc(pool_added, 1)

            pool.wait_ge(v["weights_loaded"], 16 * 7)
            add(0, 0)
            add(0, 1)
            with pool.Fori(1, GROUPS // 2) as i:
                add(i, 0)
                add(i, 1)
            add(GROUPS // 2, 0, TAIL)

        @block.vector
        def _(dve):
            vec = nc.vector
            st = Steps(dve, step)
            dve.wait_ge(v["weights_loaded"], 16 * 7)
            vec.memset(wts[:], float("-inf"))

            def group(i, b, tiles=TG):
                g = 2 * i + b
                landed(dve, i, b, tiles)
                p = parts[:, b, :, 0:tiles, :]
                st.wait(vec.tensor_tensor(p[:, 0], p[:, 0], p[:, 1], ALU.add))
                dve.wait_ge(pool_added, g + 1)
                st.wait(vec.tensor_tensor(p[:, 0], p[:, 0], p[:, 2], ALU.add))
                st.wait(vec.tensor_tensor(p[:, 0], p[:, 0], xb[:, b, 0:tiles, :], ALU.add))
                for t in range(tiles):
                    last = vec.bn_stats(stats[:, t, :], p[:, 0, t, :])
                st.wait(last)
                hold(dve)
                for t in range(tiles):
                    last = vec.bn_aggr(mv[:, t, :], stats[:, t, :])
                last.then_inc(mv_ready, 1)
                dve.wait_ge(std_ready, g + 1)
                st.wait(vec.reciprocal(std[:, 0:tiles], std[:, 0:tiles]))
                wait_if(dve, xn_stored[b], 16 * i)
                for t in range(tiles):
                    last = vec.tensor_scalar(xn[:, b, t, :], p[:, 0, t, :], mv[:, t, 0:1], std[:, t:t + 1],
                                             ALU.subtract, ALU.mult)
                last.then_inc(xn_ready, 1)
                dve.wait_ge(xn_ready, g + 1)
                for t in range(tiles):
                    last = vec.tensor_tensor_reduce(out=junk[:, t, :], in0=xn[:, b, t, :], in1=wr_sb[:], scale=1.0, scalar=0.0,
                                                    op0=ALU.mult, op1=ALU.add, accum_out=wcur[:, t:t + 1])
                st.wait(last)
                if tiles == TG:
                    vec.tensor_scalar(wts[:, bass.ds(g * TG, TG)], wcur[:], br_sb[:], None, ALU.add)
                else:
                    vec.tensor_scalar(wts[:, NT - tiles:NT - 1], wcur[:, 0:tiles - 1], br_sb[:], None, ALU.add)
                    vec.tensor_scalar(wts[0:LAST, NT - 1:NT], wcur[0:LAST, tiles - 1:tiles], br_sb[0:LAST, :], None, ALU.add)
                vec.tensor_tensor(base[:, bass.ds(g * TG, tiles), :], p[:, 0], xn[:, b, 0:tiles, :], ALU.add).then_inc(parts_used, 1)

            group(0, 0)
            group(0, 1)
            first = st.k
            a_step = first
            with dve.Fori(1, GROUPS // 2) as i:
                st.rebase(i * a_step)
                group(i, 0)
                group(i, 1)
            st.rebase((GROUPS // 2) * a_step)
            group(GROUPS // 2, 0, TAIL)


def choose(nc, v):
    (out, sem, sb, base, wts, kept_row, consts) = (v[n] for n in "out sem sb base wts kept_row consts".split())
    N, D, NT, LAST, KEPT, SLOTS, base_stored = (v[n] for n in "N D NT LAST KEPT SLOTS base_stored".split())
    before, ones, row, col = (consts[n] for n in ("before", "ones", "row", "col"))
    BITS = 16
    PART = 14
    assert NT % PART == 0
    with ExitStack() as c:
        def ps(name, shape):
            return c.enter_context(nc.psum_tensor(name, shape, F32))

        half_i = [sb(c, f"half_i{i}", [P, NT], I32) for i in range(2)]
        key = [sb(c, f"key{i}", [P, NT]) for i in range(2)]
        neg = sb(c, "neg", [P, NT])
        tmp = sb(c, "tmp", [P, NT])
        junk = sb(c, "junk2", [P, NT])
        cand = sb(c, "cand", [P, 1])
        weight_of_bit = sb(c, "weight_of_bit", [P, 2])
        cnt = sb(c, "cnt", [P, 1])
        up = sb(c, "up", [P, 1])
        top = sb(c, "top", [P, 1])
        tied_left = sb(c, "tied_left", [P, 1])
        above = sb(c, "above", [P, NT], BF16)
        tied = sb(c, "tied", [P, NT], BF16)
        chosen = sb(c, "chosen", [P, NT], BF16)
        ones_b = sb(c, "ones_b", [P, P], BF16)
        total_b = sb(c, "total_b", [NT, P], BF16)
        rank = sb(c, "rank", [P, NT])
        rank_i = sb(c, "rank_i", [P, NT], I32)
        part_i = [sb(c, f"part_i{i}", [P, NT], I32) for i in range(2)]
        part = [sb(c, f"part{i}", [P, NT]) for i in range(2)]
        in_slot = sb(c, "in_slot", [P, 2, PART, P], BF16)
        in_tile = sb(c, "in_tile", [P, 2, PART, SLOTS], BF16)
        number = sb(c, "number", [P, 2, PART, 2, SLOTS], BF16)
        number_f = sb(c, "number_f", [P, 2, SLOTS])
        tot_ps = ps("tot_ps", [P, 1])
        all_ps = ps("all_ps", [P, NT])
        col_ps = ps("col_ps", [NT, 1])
        rank_ps = ps("rank_ps", [P, NT])
        num_ps = ps("num_ps", [P, 2, SLOTS])
        step = sem("choose_dve_step")
        counted = sem("counted")
        totalled = sem("totalled")
        ready = sem("mask_ready")
        summed = sem("mask_summed")
        spread = sem("totals_spread")
        ranked = sem("ranked")
        hot = sem("hot_ready")
        packed = sem("packed")
        block = c.enter_context(nc.Block())

        @block.sync
        def _(sp):
            sp.dma_start(out[0:N - LAST, :].rearrange("(t p) d -> p t d", p=P), base[:, 0:NT - 1, :]).then_inc(base_stored, 16)
            sp.dma_start(out[N - LAST:N, :], base[0:LAST, NT - 1, :]).then_inc(base_stored, 16)
            sp.wait_ge(base_stored, 32)

        @block.tensor
        def _(pe):
            t = nc.tensor

            def total(n):
                pe.wait_ge(counted, n + 1)
                t.matmul(tot_ps[:], lhsT=ones[:], rhs=cnt[:], start=True, stop=True).then_inc(totalled, 1)

            with pe.Fori(0, 2 * BITS) as n:
                total(n)
            pe.wait_ge(ready, 1)
            t.matmul(all_ps[:], lhsT=ones_b[:], rhs=above[:], start=True, stop=True)
            for n, mask in enumerate((tied, chosen)):
                pe.wait_ge(ready, n + 1)
                t.matmul(col_ps[:], lhsT=mask[:], rhs=ones_b[:, 0:1], start=True, stop=True).then_inc(summed, 1)
                pe.wait_ge(spread, n + 1)
                t.matmul(rank_ps[:], lhsT=before[:], rhs=mask[:], start=True, stop=False)
                t.matmul(rank_ps[:], lhsT=total_b[:], rhs=before[0:NT, 0:NT], start=False, stop=True).then_inc(ranked, 1)
            for n in range(NT // PART):
                pe.wait_ge(hot, n + 1)
                for j in range(PART):
                    last = t.matmul(num_ps[:], lhsT=in_slot[:, n % 2, j, :], rhs=number[:, n % 2, j, :, :],
                                    start=(n == 0 and j == 0), stop=(n == NT // PART - 1 and j == PART - 1))
                last.then_inc(packed, 1)

        @block.vector
        def _(dve):
            vec = nc.vector
            st = Steps(dve, step)
            bits = wts[:].bitcast(I32)
            vec.memset(ones_b[:], 1.0)
            vec.tensor_scalar(half_i[0][:], bits, 16, None, ALU.logical_shift_right)
            st.wait(vec.tensor_scalar(half_i[1][:], bits, 0xFFFF, None, ALU.bitwise_and))
            vec.tensor_copy(key[1][:], half_i[1][:])
            st.wait(vec.tensor_copy(key[0][:], half_i[0][:]))
            vec.tensor_scalar(neg[:], key[0][:], 32768.0, None, ALU.is_ge)
            st.wait(vec.tensor_scalar(tmp[:], key[0][:], -2.0, 32767.0, ALU.mult, ALU.add))
            st.wait(vec.tensor_tensor(tmp[:], tmp[:], neg[:], ALU.mult))
            st.wait(vec.scalar_tensor_tensor(out=key[0][:], in0=key[0][:], scalar=32768.0, in1=tmp[:], op0=ALU.add, op1=ALU.add))
            st.wait(vec.tensor_scalar(tmp[:], key[1][:], -2.0, 65535.0, ALU.mult, ALU.add))
            st.wait(vec.tensor_tensor(tmp[:], tmp[:], neg[:], ALU.mult))
            st.wait(vec.tensor_tensor(key[1][:], key[1][:], tmp[:], ALU.add))
            for half in range(2):
                if half:
                    st.wait(vec.tensor_scalar(top[:], cand[:], 0.5, None, ALU.subtract))
                    st.wait(vec.tensor_scalar(tmp[:], key[0][:], top[:], 65536.0, ALU.subtract, ALU.mult))
                    st.wait(vec.tensor_tensor(key[1][:], key[1][:], tmp[:], ALU.add))
                vec.memset(cand[:], float(1 << (BITS - 1)))
                vec.memset(weight_of_bit[:, 0:1], float(1 << (BITS - 1)))
                st.wait(vec.memset(weight_of_bit[:, 1:2], float(1 << (BITS - 2))))
                first = st.base + st.k
                with dve.Fori(0, BITS) as i:
                    st.rebase(first + i * 3)
                    vec.tensor_scalar(junk[:], key[half][:], cand[:], 0.0, ALU.is_ge, ALU.add,
                                      accum_out=cnt[:]).then_inc(counted, 1)
                    dve.wait_ge(totalled, i + (BITS * half + 1))
                    st.wait(vec.tensor_scalar(up[:], tot_ps[:], float(KEPT), weight_of_bit[:, 0:1], ALU.is_ge, ALU.mult))
                    st.wait(vec.scalar_tensor_tensor(out=cand[:], in0=cand[:], scalar=weight_of_bit[:, 1:2], in1=up[:],
                                                     op0=ALU.subtract, op1=ALU.add))
                    st.wait(vec.tensor_scalar(weight_of_bit[:], weight_of_bit[:], 0.5, None, ALU.mult))
                st.rebase(first + BITS * 3)
            st.wait(vec.tensor_scalar(top[:], cand[:], 0.5, None, ALU.subtract))
            vec.tensor_scalar(above[:], key[1][:], top[:], None, ALU.is_gt)
            vec.tensor_scalar(tied[:], key[1][:], top[:], None, ALU.is_equal).then_inc(ready, 1)

            def spread_totals(n):
                dve.wait_ge(summed, n + 1)
                vec.tensor_copy(total_b[:], col_ps[:].to_broadcast([NT, P])).then_inc(spread, 1)
                dve.wait_ge(ranked, n + 1)

            spread_totals(0)
            st.wait(vec.tensor_reduce(cnt[:], all_ps[:], op=ALU.add, axis=AX.X))
            st.wait(vec.tensor_scalar(tied_left[:], cnt[:], -1.0, float(KEPT), ALU.mult, ALU.add))
            st.wait(vec.tensor_scalar(tmp[:], rank_ps[:], tied_left[:], None, ALU.is_lt))
            st.wait(vec.tensor_tensor(tmp[:], tmp[:], tied[:], ALU.mult))
            vec.tensor_tensor(chosen[:], tmp[:], above[:], ALU.add).then_inc(ready, 1)
            spread_totals(1)
            st.wait(vec.scalar_tensor_tensor(out=rank[:], in0=rank_ps[:], scalar=1.0, in1=chosen[:], op0=ALU.add, op1=ALU.mult))
            st.wait(vec.tensor_scalar(rank_i[:], rank[:], -1.0, None, ALU.add))
            vec.tensor_scalar(part_i[0][:], rank_i[:], 7, None, ALU.arith_shift_right)
            st.wait(vec.tensor_scalar(part_i[1][:], rank_i[:], P - 1, None, ALU.bitwise_and))
            vec.tensor_copy(part[0][:], part_i[0][:])
            st.wait(vec.tensor_copy(part[1][:], part_i[1][:]))
            for n in range(NT // PART):
                r, t0 = n % 2, n * PART
                wait_if(dve, packed, n - 1)
                st.wait(vec.tensor_tensor(in_tile[:, r, :, :], part[0][:, t0:t0 + PART].unsqueeze(2).to_broadcast([P, PART, SLOTS]),
                                          row[:, 0:SLOTS].unsqueeze(1).to_broadcast([P, PART, SLOTS]), ALU.is_equal))
                for j in range(PART):
                    vec.tensor_scalar(number[:, r, j, 0, :], in_tile[:, r, j, :], float(t0 + j), None, ALU.mult)
                vec.tensor_scalar(number[:, r, :, 1, :], in_tile[:, r, :, :], col[:], None, ALU.mult)
                vec.tensor_tensor(in_slot[:, r, :, :], part[1][:, t0:t0 + PART].unsqueeze(2).to_broadcast([P, PART, P]),
                                  row[:].unsqueeze(1).to_broadcast([P, PART, P]), ALU.is_equal).then_inc(hot, 1)
            dve.wait_ge(packed, NT // PART)
            st.wait(vec.tensor_copy(number_f[:], num_ps[:]))
            vec.scalar_tensor_tensor(out=kept_row[:], in0=number_f[:, 0, :], scalar=float(P), in1=number_f[:, 1, :],
                                     op0=ALU.mult, op1=ALU.add)


def ffn(nc, v):
    hold = v['hold']
    (out, xn_dram, sem, sb, kept_row, consts, w1_sb, w2_sb, b1_sb, b2_sb, wr_sb, br_sb) = (
        v[n] for n in "out xn_dram sem sb kept_row consts w1_sb w2_sb b1_sb b2_sb wr_sb br_sb".split())
    N, D, NT, KD, KH, KEPT, SLOTS, SG = (v[n] for n in "N D NT KD KH KEPT SLOTS SG".split())
    ident = consts["ident"]
    LAST_SLOTS = KEPT - (SLOTS - 1) * P
    with ExitStack() as c:
        def ps(name, shape):
            return c.enter_context(nc.psum_tensor(name, shape, F32))

        ids = sb(c, "ids", [P, 2, TG], I32)
        xg = sb(c, "xg", [P, 2, TG, D])
        xgT = sb(c, "xgT", [P, 2, KD, TG * P])
        hidden = sb(c, "hidden", [P, KH, TG * P])
        route = sb(c, "route", [P, 2, TG])
        route_in = sb(c, "route_in", [P, 2, TG])
        junk = sb(c, "junk3", [P, TG, D])
        y1 = sb(c, "y1", [P, TG, D])
        y = sb(c, "y", [P, 2, TG, D])
        xt_ps = ps("xgt_ps", [P, KD, TG * P])
        up_ps = [ps(f"up_ps{i}", [P, TG * P]) for i in range(2)]
        y_ps = [ps(f"y_ps{i}", [P, TG, D]) for i in range(2)]
        ids_ready = sem("ids_ready")
        xg_loaded = [sem(f"xg_loaded{i}") for i in range(2)]
        xg_turned = sem("xg_turned")
        xgT_ready = sem("xgT_ready")
        routed = sem("routed")
        up_done = sem("up_done")
        gelu_done = sem("gelu_done")
        down_done = sem("down_done")
        y_ready = sem("y_ready")
        y_added = [sem(f"y_added{i}") for i in range(2)]
        step = sem("ffn_dve_step")
        block = c.enter_context(nc.Block())
        HALF = SG // 2

        @block.gpsimd
        def _(pool):
            def gather(i, b, tiles=TG):
                g = 2 * i + b
                pool.wait_ge(ids_ready, g + 1)
                wait_if(pool, xg_turned, g - 1)
                wait_if(pool, routed, g - 1)
                for k in range(tiles):
                    hold(pool)
                    pool.indirect_dma_start(
                        out=xg[:, b, k, :], out_offset=None, in_=xn_dram,
                        in_offset=bass.IndirectOffsetOnAxis(ap=ids[:, b, k:k + 1], axis=0)).then_inc(xg_loaded[b], 16)

            def add(i, b, tiles=TG):
                g = 2 * i + b
                pool.wait_ge(y_ready, g + 1)
                for k in range(tiles):
                    n = P if tiles == TG else LAST_SLOTS
                    hold(pool)
                    pool.indirect_dma_start(
                        out=out, out_offset=bass.IndirectOffsetOnAxis(ap=ids[0:n, b, k:k + 1], axis=0),
                        in_=y[0:n, b, k, :], in_offset=None,
                        compute_op=ALU.add).then_inc(y_added[b], 16)

            gather(0, 0)
            gather(0, 1)
            with pool.Fori(1, HALF) as i:
                for b in range(2):
                    add(i - 1, b)
                    gather(i, b)
            add(HALF - 1, 0)
            gather(HALF, 0, 1)
            add(HALF - 1, 1)
            add(HALF, 0, 1)
            pool.wait_ge(y_added[0], 16 * (TG * HALF + 1))
            pool.wait_ge(y_added[1], 16 * TG * HALF)

        @block.vector
        def _(dve):
            vec = nc.vector
            st = Steps(dve, step)

            def take_ids(i, b, tiles=TG):
                g = 2 * i + b
                wait_if(dve, y_added[b], 16 * TG * i)
                vec.tensor_copy(ids[:, b, 0:tiles], kept_row[:, bass.ds(g * TG, tiles)]).then_inc(ids_ready, 1)

            def turn(i, b, tiles=TG):
                g = 2 * i + b
                dve.wait_ge(xg_turned, g + 1)
                vec.tensor_copy(xgT[:, b, :, 0:tiles * P], xt_ps[:, :, 0:tiles * P]).then_inc(xgT_ready, 1)
                for k in range(tiles):
                    last = vec.tensor_tensor_reduce(out=junk[:, k, :], in0=xg[:, b, k, :], in1=wr_sb[:], scale=1.0, scalar=0.0,
                                                    op0=ALU.mult, op1=ALU.add, accum_out=route_in[:, b, k:k + 1])
                st.wait(last)
                vec.tensor_scalar(route[:, b, 0:tiles], route_in[:, b, 0:tiles], br_sb[:], None, ALU.add).then_inc(routed, 1)

            def scale(i, b, tiles=TG):
                g = 2 * i + b
                dve.wait_ge(down_done, g + 1)
                wait_if(dve, y_ready, g)
                st.wait(vec.tensor_tensor(y1[:, 0:tiles, :], y_ps[b][:, 0:tiles, :],
                                          b2_sb[:].unsqueeze(1).to_broadcast([P, tiles, D]), ALU.add))
                for k in range(tiles):
                    last = vec.tensor_scalar(y[:, b, k, :], y1[:, k, :], route[:, b, k:k + 1], None, ALU.mult)
                last.then_inc(y_ready, 1)

            take_ids(0, 0)
            take_ids(0, 1)
            turn(0, 0)
            turn(0, 1)
            first = st.k
            with dve.Fori(1, HALF) as i:
                st.rebase(first + (i - 1) * 4)
                for b in range(2):
                    scale(i - 1, b)
                    take_ids(i, b)
                    turn(i, b)
            st.rebase(first + (HALF - 1) * 4)
            scale(HALF - 1, 0)
            take_ids(HALF, 0, 1)
            turn(HALF, 0, 1)
            scale(HALF - 1, 1)
            scale(HALF, 0, 1)

        @block.tensor
        def _(pe):
            t = nc.tensor

            def turn(i, b, tiles=TG):
                g = 2 * i + b
                pe.wait_ge(xg_loaded[b], 16 * (TG * i + tiles))
                wait_if(pe, xgT_ready, g)
                for j in range(tiles):
                    for k in range(KD):
                        last = t.transpose(xt_ps[:, k, j * P:(j + 1) * P], xg[:, b, j, k * P:(k + 1) * P], ident[:])
                last.then_inc(xg_turned, 1)

            def up(i, b, tiles=TG):
                g = 2 * i + b
                pe.wait_ge(xgT_ready, g + 1)
                for m in range(KH):
                    wait_if(pe, gelu_done, KH * g + m - 1)
                    for k in range(KD):
                        last = t.matmul(up_ps[m % 2][:, 0:tiles * P], lhsT=w1_sb[:, k, m * P:(m + 1) * P],
                                        rhs=xgT[:, b, k, 0:tiles * P], start=(k == 0), stop=(k == KD - 1))
                    last.then_inc(up_done, 1)

            def down(i, b, tiles=TG):
                g = 2 * i + b
                pe.wait_ge(gelu_done, KH * (g + 1))
                wait_if(pe, y_ready, g - 1)
                for j in range(tiles):
                    for m in range(KH):
                        last = t.matmul(y_ps[b][:, j, :], lhsT=hidden[:, m, j * P:(j + 1) * P], rhs=w2_sb[:, m, :],
                                        start=(m == 0), stop=(m == KH - 1))
                last.then_inc(down_done, 1)

            turn(0, 0)
            up(0, 0)
            turn(0, 1)
            down(0, 0)
            with pe.Fori(1, HALF) as i:
                up(i - 1, 1)
                turn(i, 0)
                down(i - 1, 1)
                up(i, 0)
                turn(i, 1)
                down(i, 0)
            up(HALF - 1, 1)
            turn(HALF, 0, 1)
            down(HALF - 1, 1)
            up(HALF, 0, 1)
            down(HALF, 0, 1)

        @block.scalar
        def _(act):
            def gelu(i, b, tiles=TG):
                g = 2 * i + b
                wait_if(act, down_done, g)
                for m in range(KH):
                    act.wait_ge(up_done, KH * g + m + 1)
                    act.activation(hidden[:, m, 0:tiles * P], up_ps[m % 2][:, 0:tiles * P], ACT.Gelu_apprx_tanh,
                                   bias=b1_sb[:, m:m + 1]).then_inc(gelu_done, 1)

            gelu(0, 0)
            gelu(0, 1)
            with act.Fori(1, HALF) as i:
                gelu(i, 0)
                gelu(i, 1)
            gelu(HALF, 0, 1)


_INS = ["x", "src", "dst", "edge_weight", "L0_gnn_W", "L0_gnn_bias", "L0_ffn_wr", "L0_ffn_br", "L0_ffn_w1",
        "L0_ffn_b1", "L0_ffn_w2", "L0_ffn_b2"]
_OUTS = [((12500, 256), "float32")]


def kernel(**inputs):
    import numpy as _np
    import concourse.bacc as _bacc
    from concourse import mybir as _mybir
    from concourse.bass_utils import run_bass_kernel_spmd as _run

    nc = _bacc.Bacc("TRN2", target_bir_lowering=False, num_devices=1)
    arrays, args = {}, []
    for name in _INS:
        a = _np.ascontiguousarray(inputs[name])
        arrays[f"in_{name}"] = a
        args.append(nc.dram_tensor(f"in_{name}", a.shape, _mybir.dt.from_np(a.dtype), kind="ExternalInput").ap())
    for i, (shape, dtype) in enumerate(_OUTS):
        args.append(nc.dram_tensor(f"out_{i}", shape, _mybir.dt.from_np(_np.dtype(dtype)), kind="ExternalOutput").ap())
    build(nc, *args)
    r = _run(nc, [arrays], core_ids=[0])
    return r.results[0]["out_0"]
```

```python
from contextlib import ExitStack

import concourse.bass as bass
from concourse import mybir

P = 128
F32 = mybir.dt.float32
F32R = mybir.dt.float32r
BF16 = mybir.dt.bfloat16
I32 = mybir.dt.int32
ALU = mybir.AluOpType
ACT = mybir.ActivationFunctionType
AX = mybir.AxisListType

EPS = 1e-5
TABLES = 4
CLEAR_ROWS = 11
EDGES_PER_SUPER = 1024
CH = EDGES_PER_SUPER // P
SUPERS = 2
BATCH = 4
TG = 4
NFIELD = 5
SRC, REL, WGT, SPARE, DST = range(NFIELD)


PAIRS = ((0, 0), (0, 1), (1, 0))


class Steps:

    def __init__(self, engine, sem):
        self.engine, self.sem, self.base, self.k = engine, sem, 0, 0

    def rebase(self, base):
        self.base, self.k = base, 0

    def wait(self, instruction):
        instruction.then_inc(self.sem, 1)
        self.k += 1
        self.engine.wait_ge(self.sem, self.base + self.k)


def wait_if(engine, sem, value):
    if not isinstance(value, int) or value > 0:
        engine.wait_ge(sem, value)


def build_constants(nc, k, sem):
    g = nc.gpsimd
    st = Steps(g, sem)
    st.wait(g.memset(k["ident"][:], 0.0))
    st.wait(g.affine_select(out=k["ident"][:], in_=k["ident"][:], compare_op=ALU.not_equal, fill=1.0,
                            base=0, pattern=[[-1, P]], channel_multiplier=1))
    st.wait(g.memset(k["lower"][:], 1.0))
    st.wait(g.affine_select(out=k["lower"][:], in_=k["lower"][:], compare_op=ALU.is_gt, fill=0.0,
                            base=0, pattern=[[-1, P]], channel_multiplier=1))
    st.wait(g.memset(k["before"][:], 1.0))
    st.wait(g.affine_select(out=k["before"][:], in_=k["before"][:], compare_op=ALU.is_gt, fill=0.0,
                            base=0, pattern=[[1, P]], channel_multiplier=-1))
    st.wait(g.memset(k["ones"][:], 1.0))
    st.wait(g.iota(k["row"][:], pattern=[[1, P]], base=0, channel_multiplier=0,
                   allow_small_or_imprecise_dtypes=True))
    st.wait(g.iota(k["col"][:], pattern=[[0, 1]], base=0, channel_multiplier=1,
                   allow_small_or_imprecise_dtypes=True))
    st.wait(g.memset(k["eps"][:], EPS))
    st.wait(g.memset(k["zero"][:], 0.0))
    return st.k


def build(nc, x, src, dst, wgt, W, bias, wr, br, w1, b1, w2, b2, out):
    N, D = x.shape
    E = src.shape[0]
    H = w1.shape[1]
    KD, KH = D // P, H // P
    NT = -(-N // P)
    LAST = N - (NT - 1) * P
    GROUPS = NT // TG
    TAIL = NT - GROUPS * TG
    S = -(-E // EDGES_PER_SUPER)
    S += S % SUPERS
    Q = S // SUPERS
    OVER = S * EDGES_PER_SUPER - E
    BATCHES = SUPERS * CH // BATCH
    NCH = SUPERS * CH
    KEPT = max(1, int(0.5 * N)) - 1
    SLOTS = -(-KEPT // P)
    SG = SLOTS // TG
    STAIL = SLOTS - SG * TG
    assert Q <= P and OVER < EDGES_PER_SUPER and GROUPS % 2 == 0 and TAIL and SG % 2 == 0 and STAIL == 1
    CLEARS = GROUPS // 2
    CLEAR_P = 96
    ROWS = CLEARS * CLEAR_P * CLEAR_ROWS
    assert ROWS >= N + P and ROWS >= NT * P

    h_dram = nc.dram_tensor("h_rows", [N, D], F32, kind="Internal").ap()
    xn_dram = nc.dram_tensor("xn_rows", [NT * P, D], F32, kind="Internal").ap()
    tables = [nc.dram_tensor(f"aggregate{i}", [ROWS, D], F32, kind="Internal").ap() for i in range(TABLES)]

    def tile_rows(a, g, tiles=TG):
        return a[bass.ds(g * (TG * P), tiles * P), :].rearrange("(t p) d -> p t d", p=P)

    with ExitStack() as whole:
        def sb(ctx, name, shape, dt=F32):
            return ctx.enter_context(nc.sbuf_tensor(name, shape, dt))

        def sem(name):
            return whole.enter_context(nc.semaphore(name))

        consts = {
            "ident": sb(whole, "ident", [P, P]),
            "lower": sb(whole, "lower", [P, P]),
            "before": sb(whole, "before", [P, P], BF16),
            "ones": sb(whole, "ones", [P, P]),
            "row": sb(whole, "row", [P, P]),
            "col": sb(whole, "col", [P, 1]),
            "eps": sb(whole, "eps", [P, 1]),
            "zero": sb(whole, "zero", [P, CLEAR_ROWS * D]),
        }
        ident, lower, before, ones = (consts[n] for n in ("ident", "lower", "before", "ones"))
        row, col, zero = (consts[n] for n in ("row", "col", "zero"))
        w1_parts = sb(whole, "w1_parts", [P, 2, KD, H], F32R)
        w2_parts = sb(whole, "w2_parts", [P, 2, KH, D], F32R)
        b1_sb = sb(whole, "b1_sb", [P, KH])
        b2_sb = sb(whole, "b2_sb", [P, D])
        wr_sb = sb(whole, "wr_sb", [P, D])
        br_sb = sb(whole, "br_sb", [P, 1])
        bias_sb = sb(whole, "bias_sb", [P, D])

        consts_ready = sem("consts_ready")
        weights_loaded = sem("weights_loaded")
        table_cleared = [sem(f"table_cleared{i}") for i in range(TABLES)]
        table_added = [sem(f"table_added{i}") for i in range(TABLES)]
        CONSTS = 11

        held = sem("held")

        def hold(engine):
            engine.sem_inc(held, 1)

        eps = consts["eps"]

        with ExitStack() as edge_ctx:
            edges = sb(edge_ctx, "edges", [P, Q + 1, SUPERS, NFIELD, CH])
            window_row = sb(edge_ctx, "window_row", [1, Q, SUPERS], I32)
            flag = sb(edge_ctx, "flag", [1, 1], I32)
            project(nc, locals())
            edge_sums(nc, locals())
        with ExitStack() as late:
            kept_row = sb(late, "kept_row", [P, (SG + 2) * TG], I32)
            base_stored = sem("base_stored")
            with ExitStack() as middle:
                base = sb(middle, "base", [P, NT, D])
                wts = sb(middle, "wts", [P, NT])
                combine(nc, locals())
                choose(nc, locals())
            ffn(nc, locals())


def project(nc, v):
    hold = v['hold']
    (x, src, dst, wgt, W, h_dram, consts, edges, window_row, flag, tables, table_cleared, table_added, sem, sb) = (
        v[n] for n in "x src dst wgt W h_dram consts edges window_row flag tables table_cleared table_added sem sb".split())
    N, D, Q, OVER, KD, GROUPS, TAIL, LAST, ROWS = (v[n] for n in "N D Q OVER KD GROUPS TAIL LAST ROWS".split())
    ident, zero, col = consts["ident"], consts["zero"], consts["col"]
    consts_ready, weights_loaded = v["consts_ready"], v["weights_loaded"]
    tile_rows = v["tile_rows"]
    E1 = EDGES_PER_SUPER
    with ExitStack() as c:
        def ps(name, shape):
            return c.enter_context(nc.psum_tensor(name, shape, F32))

        W_sb = sb(c, "W_sb", [P, KD, D])
        src_i = sb(c, "src_i", [Q, SUPERS, E1], I32)
        dst_i = sb(c, "dst_i", [Q, SUPERS, E1], I32)
        lists = [sb(c, n, [Q, SUPERS, E1]) for n in ("src_f", "rel_f", "wgt_f", "dst_f")]
        src_f, rel_f, wgt_f, dst_f = lists
        fields = (SRC, REL, WGT, DST)
        lo = sb(c, "lo", [Q, SUPERS])
        hi = sb(c, "hi", [Q, SUPERS])
        spread = sb(c, "spread", [Q, SUPERS])
        first = sb(c, "first", [Q, SUPERS])
        wide = sb(c, "wide", [Q, SUPERS])
        wide_row = sb(c, "wide_row", [1, SUPERS, Q])
        any_wide = sb(c, "any_wide", [1, 1])
        spare = sb(c, "spare", [P, 1])
        x_in = sb(c, "x_in", [P, 2, TG, D])
        stats = sb(c, "stats", [P, TG, 6])
        mv = sb(c, "mv", [P, TG, 2])
        std = sb(c, "std", [P, TG])
        xn = sb(c, "xn", [P, 2, TG, D])
        xnT = sb(c, "xnT", [P, 2, KD, TG * P])
        h_sb = sb(c, "h_sb", [P, 2, TG, D])
        w1_sb = sb(c, "w1_sb", [P, KD, v["H"]])
        w2_sb = sb(c, "w2_sb", [P, v["KH"], D])
        turn_ps = [ps(f"turn_ps{i}", [P, 4, P]) for i in range(2)]
        xt_ps = ps("xt_ps", [P, KD, TG * P])
        h_ps = [ps(f"h_ps{i}", [P, TG, D]) for i in range(2)]

        edges_loaded = sem("edges_loaded")
        lists_ready = sem("lists_ready")
        turned = sem("turned")
        turn_copied = sem("turn_copied")
        meta_turned = sem("meta_turned")
        W_loaded = sem("W_loaded")
        x_loaded = [sem(f"x_loaded{i}") for i in range(2)]
        norm_done = sem("norm_done")
        x_turned = sem("x_turned")
        xt_copied = sem("xt_copied")
        h_done = sem("h_done")
        mv_ready = sem("mv_ready")
        split_step = sem("split_step")
        std_ready = sem("std_ready")
        h_copied = sem("h_copied")
        h_stored = [sem(f"h_stored{i}") for i in range(2)]
        dve_step = sem("project_dve_step")
        NTURN = len(lists) * SUPERS * (CH // 4)
        NG = GROUPS + 1
        EDGE_DMAS = 12

        block = c.enter_context(nc.Block())

        @block.gpsimd
        def _(pool):
            n = build_constants(nc, consts, consts_ready)
            assert n == v["CONSTS"]
            pool.wait_ge(weights_loaded, 16 * 7)
            for n, (w, parts) in enumerate(((w1_sb, v["w1_parts"]), (w2_sb, v["w2_parts"]))):
                nc.gpsimd.tensor_copy(parts[:, 0, :, :], w[:]).then_inc(split_step, 1)
                pool.wait_ge(split_step, n + 1)
                nc.gpsimd.tensor_tensor(parts[:, 1, :, :], w[:], parts[:, 0, :, :].bitcast(F32), ALU.subtract)

        @block.sync
        def _(sp):
            sp.dma_start(W_sb[:], W.rearrange("(k p) n -> p k n", p=P)).then_inc(W_loaded, 16)
            for a, t in ((src, src_i), (dst, dst_i), (wgt, wgt_f)):
                sp.dma_start(t[0:1, 0, :], a[0:E1].rearrange("(o e) -> o e", o=1)).then_inc(edges_loaded, 16)
                sp.dma_start(t[0:1, 1, :], a[E1 - OVER:2 * E1 - OVER].rearrange("(o e) -> o e", o=1)).then_inc(edges_loaded, 16)
                for q0, q1 in ((1, 8), (8, Q)):
                    sp.dma_start(t[q0:q1, :, :], a[q0 * SUPERS * E1 - OVER:q1 * SUPERS * E1 - OVER]
                                 .rearrange("(q g e) -> q g e", g=SUPERS, e=E1)).then_inc(edges_loaded, 16)

            def load(i, b, tiles=TG):
                g = 2 * i + b
                wait_if(sp, norm_done, g - 1)
                if tiles == TG:
                    sp.dma_start(x_in[:, b, :, :], tile_rows(x, g)).then_inc(x_loaded[b], 16)
                else:
                    n0 = GROUPS * TG * P
                    sp.dma_start(x_in[:, b, 0:tiles - 1, :], x[n0:n0 + (tiles - 1) * P, :]
                                 .rearrange("(t p) d -> p t d", p=P)).then_inc(x_loaded[b], 16)
                    sp.dma_start(x_in[0:LAST, b, tiles - 1, :], x[N - LAST:N, :]).then_inc(x_loaded[b], 16)

            def store(i, b, tiles=TG):
                g = 2 * i + b
                sp.wait_ge(h_copied, g + 1)
                if tiles == TG:
                    sp.dma_start(tile_rows(h_dram, g), h_sb[:, b, :, :]).then_inc(h_stored[b], 16)
                else:
                    n0 = GROUPS * TG * P
                    sp.dma_start(h_dram[n0:n0 + (tiles - 1) * P, :].rearrange("(t p) d -> p t d", p=P),
                                 h_sb[:, b, 0:tiles - 1, :]).then_inc(h_stored[b], 16)
                    sp.dma_start(h_dram[N - LAST:N, :], h_sb[0:LAST, b, tiles - 1, :]).then_inc(h_stored[b], 16)

            load(0, 0)
            load(0, 1)
            with sp.Fori(1, GROUPS // 2) as i:
                for b in range(2):
                    load(i, b)
                    store(i - 1, b)
            load(GROUPS // 2, 0, TAIL)
            store(GROUPS // 2 - 1, 0)
            store(GROUPS // 2 - 1, 1)
            store(GROUPS // 2, 0, TAIL)
            sp.wait_ge(h_stored[0], 16 * (GROUPS // 2 + 2))
            sp.wait_ge(h_stored[1], 16 * (GROUPS // 2))

        @block.scalar
        def _(act):
            act.wait_ge(consts_ready, v["CONSTS"])

            def clear(i):
                rows = v["CLEAR_P"] * CLEAR_ROWS
                for t in range(TABLES):
                    act.dma_start(tables[t][bass.ds(i * rows, rows), :].rearrange("(p r) d -> p (r d)", r=CLEAR_ROWS),
                                  zero[0:v["CLEAR_P"], :]).then_inc(table_cleared[t], 16)

            clear(0)
            for a, t in ((v["w1"].rearrange("(k p) n -> p k n", p=P), w1_sb),
                         (v["w2"].rearrange("(k p) n -> p k n", p=P), w2_sb),
                         (v["b2"].partition_broadcast(P), v["b2_sb"]),
                         (v["wr"].rearrange("n o -> (n o)").partition_broadcast(P), v["wr_sb"]),
                         (v["br"].partition_broadcast(P), v["br_sb"]),
                         (v["bias"].partition_broadcast(P), v["bias_sb"])):
                act.dma_start(t[:], a).then_inc(weights_loaded, 16)
            with nc.allow_non_contiguous_dma(reason="the bias of the first product, once"):
                act.dma_start(v["b1_sb"][:], v["b1"].rearrange("(c p) -> p c", p=P)).then_inc(weights_loaded, 16)

            for n in range(NTURN):
                f, g, half = n // (SUPERS * 2), n // 2 % SUPERS, n % 2
                act.wait_ge(turned, n + 1)
                act.activation(edges[:, 0:Q, g, fields[f], 4 * half:4 * half + 4],
                               turn_ps[n % 2][:, :, 0:Q].rearrange("p k q -> p q k"), ACT.Copy).then_inc(turn_copied, 1)

            def xt_copy(i, b, tiles=TG):
                g = 2 * i + b
                act.wait_ge(mv_ready, g + 1)
                act.activation(std[:, 0:tiles], mv[:, 0:tiles, 1], ACT.Sqrt, bias=v["eps"][:]).then_inc(std_ready, 1)
                act.wait_ge(x_turned, g + 1)
                wait_if(act, h_done, g - 1)
                act.activation(xnT[:, b, :, 0:tiles * P], xt_ps[:, :, 0:tiles * P], ACT.Copy).then_inc(xt_copied, 1)

            def h_copy(i, b, tiles=TG, first=False):
                g = 2 * i + b
                act.wait_ge(h_done, g + 1)
                wait_if(act, h_stored[b], 16 * i)
                act.activation(h_sb[:, b, 0:tiles, :], h_ps[b][:, 0:tiles, :], ACT.Copy).then_inc(h_copied, 1)

            xt_copy(0, 0)
            xt_copy(0, 1)
            h_copy(0, 0)
            with act.Fori(1, GROUPS // 2) as i:
                xt_copy(i, 0)
                clear(i)
                h_copy(i - 1, 1)
                xt_copy(i, 1)
                h_copy(i, 0)
            xt_copy(GROUPS // 2, 0, TAIL)
            h_copy(GROUPS // 2 - 1, 1)
            h_copy(GROUPS // 2, 0, TAIL)

        @block.vector
        def _(dve):
            st = Steps(dve, dve_step)
            vec = nc.vector
            dve.wait_ge(edges_loaded, 16 * EDGE_DMAS)
            vec.memset(wgt_f[0:1, 0, E1 - OVER:E1], 0.0)
            vec.tensor_copy(src_f[:], src_i[:])
            vec.memset(edges[:, Q, :, :, :], 0.0)
            dve.wait_ge(consts_ready, v["CONSTS"])
            vec.tensor_scalar(spare[:], col[:], float(N), None, ALU.add)
            st.wait(vec.tensor_copy(dst_f[:], dst_i[:]))
            vec.tensor_reduce(lo[:], dst_f[:], op=ALU.min, axis=AX.X)
            st.wait(vec.tensor_reduce(hi[:], dst_f[:], op=ALU.max, axis=AX.X))
            st.wait(vec.tensor_scalar(first[:], lo[:], float(N - P), None, ALU.min))
            for g in range(SUPERS):
                vec.tensor_scalar(rel_f[:, g, :], dst_f[:, g, :], first[:, g:g + 1], None, ALU.subtract)
            st.wait(vec.tensor_tensor(spread[:], hi[:], first[:], ALU.subtract))
            vec.tensor_scalar(wide[:], spread[:], float(P), None, ALU.is_ge).then_inc(lists_ready, 1)
            dve.wait_ge(meta_turned, 1)
            vec.tensor_copy(window_row[0:1, :, :].rearrange("o q g -> o g q"), turn_ps[0][0:1, 0:SUPERS, 0:Q])
            st.wait(vec.tensor_copy(wide_row[:], turn_ps[1][0:1, 0:SUPERS, 0:Q]))
            st.wait(vec.tensor_reduce(any_wide[:], wide_row[:].rearrange("o g q -> o (g q)"), op=ALU.max, axis=AX.X))
            vec.tensor_copy(flag[:], any_wide[:])
            dve.wait_ge(turn_copied, NTURN)
            for g in range(SUPERS):
                vec.tensor_scalar(edges[:, 0:Q, g, SPARE, :], edges[:, 0:Q, g, SRC, :], -1.0, spare[:], ALU.mult, ALU.add)
            per_group = 0

            def norm(i, b, tiles=TG):
                g = 2 * i + b
                dve.wait_ge(x_loaded[b], 16 * (i + 1) if tiles == TG else 16 * (i + 2))
                for t in range(tiles):
                    last = vec.bn_stats(stats[:, t, :], x_in[:, b, t, :])
                st.wait(last)
                hold(dve)
                for t in range(tiles):
                    last = vec.bn_aggr(mv[:, t, :], stats[:, t, :])
                last.then_inc(mv_ready, 1)
                dve.wait_ge(std_ready, g + 1)
                st.wait(vec.reciprocal(std[:, 0:tiles], std[:, 0:tiles]))
                wait_if(dve, x_turned, g - 1)
                for t in range(tiles):
                    last = vec.tensor_scalar(xn[:, b, t, :], x_in[:, b, t, :], mv[:, t, 0:1], std[:, t:t + 1],
                                             ALU.subtract, ALU.mult)
                last.then_inc(norm_done, 1)

            norm(0, 0)
            norm(0, 1)
            before_loop, a_step = st.k, 2 * 2
            with dve.Fori(1, GROUPS // 2) as i:
                st.rebase(before_loop + (i - 1) * a_step)
                norm(i, 0)
                norm(i, 1)
            st.rebase(before_loop + (GROUPS // 2 - 1) * a_step)
            norm(GROUPS // 2, 0, TAIL)

        @block.tensor
        def _(pe):
            t = nc.tensor
            pe.wait_ge(consts_ready, v["CONSTS"])
            pe.wait_ge(lists_ready, 1)
            for g in range(SUPERS):
                t.transpose(turn_ps[0][0:1, g, 0:Q], first[:, g:g + 1], ident[0:Q, 0:Q])
                last = t.transpose(turn_ps[1][0:1, g, 0:Q], wide[:, g:g + 1], ident[0:Q, 0:Q])
            last.then_inc(meta_turned, 1)
            pe.wait_ge(dve_step, 6)
            for n in range(NTURN):
                f, g, half = n // (SUPERS * 2), n // 2 % SUPERS, n % 2
                wait_if(pe, turn_copied, n - 1)
                for k in range(4):
                    e0 = (4 * half + k) * P
                    last = t.transpose(turn_ps[n % 2][:, k, 0:Q], lists[f][:, g, e0:e0 + P], ident[0:Q, 0:Q])
                last.then_inc(turned, 1)
            pe.wait_ge(W_loaded, 16)

            def turn(i, b, tiles=TG):
                g = 2 * i + b
                pe.wait_ge(norm_done, g + 1)
                wait_if(pe, xt_copied, g)
                for j in range(tiles):
                    for k in range(KD):
                        last = t.transpose(xt_ps[:, k, j * P:(j + 1) * P], xn[:, b, j, k * P:(k + 1) * P], ident[:])
                last.then_inc(x_turned, 1)

            def product(i, b, tiles=TG):
                g = 2 * i + b
                pe.wait_ge(xt_copied, g + 1)
                wait_if(pe, h_copied, g - 1)
                for j in range(tiles):
                    for k in range(KD):
                        last = t.matmul(h_ps[b][:, j, :], lhsT=xnT[:, b, k, j * P:(j + 1) * P], rhs=W_sb[:, k, :],
                                        start=(k == 0), stop=(k == KD - 1))
                last.then_inc(h_done, 1)

            turn(0, 0)
            turn(0, 1)
            product(0, 0)
            with pe.Fori(1, GROUPS // 2) as i:
                turn(i, 0)
                product(i - 1, 1)
                turn(i, 1)
                product(i, 0)
            turn(GROUPS // 2, 0, TAIL)
            product(GROUPS // 2 - 1, 1)
            product(GROUPS // 2, 0, TAIL)


def edge_sums(nc, v):
    hold = v['hold']
    (h_dram, consts, edges, window_row, flag, tables, table_cleared, table_added, sem, sb) = (
        v[n] for n in "h_dram consts edges window_row flag tables table_cleared table_added sem sb".split())
    N, D, Q, NCH, BATCHES, ROWS = (v[n] for n in "N D Q NCH BATCHES ROWS".split())
    ident, lower, row = consts["ident"], consts["lower"], consts["row"]
    PER_SUPER = CH // BATCH
    with ExitStack() as c:
        def ps(name, shape):
            return c.enter_context(nc.psum_tensor(name, shape, F32))

        cur = sb(c, "cur", [P, SUPERS, NFIELD, CH])
        same = sb(c, "same", [P, 2, BATCH, P])
        earlier = sb(c, "earlier", [P, BATCH, P])
        dups = sb(c, "dups", [P, BATCH])
        moved = sb(c, "moved", [P, BATCH])
        pick = sb(c, "pick", [P, 2, BATCH, P])
        mix_sb = sb(c, "mix_sb", [P, 2, BATCH, P])
        window = sb(c, "window", [P, SUPERS, D])
        gathered = sb(c, "gathered", [P, SUPERS, CH, D])
        target = sb(c, "target", [P, SUPERS, CH], I32)
        put_row = sb(c, "put_row", [P, NCH], I32)
        msg = sb(c, "msg", [P, 2 * BATCH, D])
        src_ps = [ps(f"src_ps{i}", [P, BATCH, P]) for i in range(2)]
        mix_ps = [ps(f"mix_ps{i}", [P, BATCH, P]) for i in range(2)]
        msg_ps = [ps(f"msg_ps{i}", [P, 2, D]) for i in range(4)]

        cur_ready = sem("cur_ready")
        src_turned = sem("src_turned")
        picked = sem("picked")
        rows_ready = sem("rows_ready")
        mix_done = sem("mix_done")
        mix_copied = sem("mix_copied")
        msg_done = sem("msg_done")
        msg_copied = sem("msg_copied")
        window_loaded = [sem(f"window_loaded{i}") for i in range(SUPERS)]
        target_ready = sem("target_ready")
        rows_gathered = [sem(f"rows_gathered{i}") for i in range(SUPERS)]
        edge_step = sem("edge_dve_step")

        block = c.enter_context(nc.Block())

        def steps(engine, body):
            body(0)
            with engine.Fori(1, Q) as q:
                body(q)

        def vector_body(dve, general):
            vec = nc.vector
            st = Steps(dve, edge_step)


            def body(q):
                for g in range(SUPERS):
                    dve.wait_ge(cur_ready, SUPERS * q + g + 1)
                    wait_if(dve, picked, PER_SUPER * (SUPERS * q + g))
                    wait_if(dve, rows_ready, PER_SUPER * (SUPERS * q + g))
                    nq, ng = (q, 1) if g == 0 else (q + 1, 0)
                    vec.tensor_copy(cur[:, ng, :, :], edges[:, bass.ds(nq, 1), ng, :, :]
                                    .rearrange("p o f k -> p (o f) k")).then_inc(cur_ready, 1)
                    if general:
                        wait_if(dve, rows_gathered[g], 16 * CH * q)
                        vec.tensor_copy(target[:, g, :], cur[:, g, DST, :]).then_inc(target_ready, 1)
                    for hb in range(PER_SUPER):
                        t = BATCHES * q + PER_SUPER * g + hb
                        r = hb % 2
                        k0 = hb * BATCH
                        dve.wait_ge(src_turned, t + 1)
                        if not general:
                            wait_if(dve, mix_done, t - 1)
                        s4 = cur[:, g, SRC, k0:k0 + BATCH]
                        st.wait(vec.tensor_tensor(same[:, r, :, :], src_ps[r][:],
                                                  s4.unsqueeze(2).to_broadcast([P, BATCH, P]), ALU.is_equal))
                        st.wait(vec.tensor_tensor(earlier[:], same[:, r, :, :],
                                                  lower[:].unsqueeze(1).to_broadcast([P, BATCH, P]), ALU.mult))
                        st.wait(vec.tensor_reduce(dups[:], earlier[:], op=ALU.add, axis=AX.X))
                        st.wait(vec.scalar_tensor_tensor(out=moved[:], in0=dups[:], scalar=1.0,
                                                         in1=cur[:, g, SPARE, k0:k0 + BATCH], op0=ALU.min, op1=ALU.mult))
                        slot = g * CH + k0
                        for j in range(TABLES):
                            value = 16 * (t + 1 - BATCHES)
                            if not (isinstance(q, int)):
                                dve.wait_ge(table_added[j], value)
                        vec.tensor_tensor(put_row[:, slot:slot + BATCH], moved[:], s4, ALU.add).then_inc(rows_ready, 1)
                        if general:
                            wait_if(dve, msg_done, 2 * t - 2)
                        for k in range(BATCH):
                            last = vec.tensor_scalar(
                                pick[:, r, k, :], src_ps[r][:, k, :] if general else row[:],
                                cur[:, g, SRC if general else REL, k0 + k:k0 + k + 1],
                                cur[:, g, WGT, k0 + k:k0 + k + 1], ALU.is_equal, ALU.mult)
                        last.then_inc(picked, 1)

            a_step = 4 * BATCHES
            vec.tensor_copy(cur[:, 0, :, :], edges[:, 0, 0, :, :]).then_inc(cur_ready, 1)
            first = st.k
            body(0)
            assert st.k == first + a_step
            with dve.Fori(1, Q) as q:
                st.rebase(first + q * a_step)
                body(q)

        @block.vector
        def _(dve):
            wide = dve.value_load(flag[0:1, 0:1], min_val=0, max_val=1)
            with dve.If(wide):
                vector_body(dve, True)
            with dve.Else():
                vector_body(dve, False)

        def tensor_body(pe, general):
            t_ = nc.tensor

            def sources(q, bt):
                t, g, hb = BATCHES * q + bt, bt // PER_SUPER, bt % PER_SUPER
                pe.wait_ge(cur_ready, SUPERS * q + g + 1)
                wait_if(pe, picked, t - 1)
                for k in range(BATCH):
                    col_ap = cur[:, g, SRC, hb * BATCH + k:hb * BATCH + k + 1]
                    last = t_.transpose(src_ps[bt % 2][:, k, :], col_ap.to_broadcast([P, P]), ident[:])
                last.then_inc(src_turned, 1)

            def mix(t, bt):
                pe.wait_ge(picked, t + 1)
                wait_if(pe, mix_copied, t - 1)
                for k in range(BATCH):
                    last = t_.matmul(mix_ps[bt % 2][:, k, :], lhsT=pick[:, bt % 2, k, :], rhs=same[:, bt % 2, k, :],
                                     start=True, stop=True)
                last.then_inc(mix_done, 1)

            def message(t, q, bt):
                g, hb = bt // PER_SUPER, bt % PER_SUPER
                if general:
                    pe.wait_ge(picked, t + 1)
                    pe.wait_ge(rows_gathered[g], 16 * CH * (q + 1))
                else:
                    pe.wait_ge(mix_copied, t + 1)
                    pe.wait_ge(window_loaded[g], 16 * (q + 1))
                for half in range(2):
                    wait_if(pe, msg_copied, 2 * t + half - 3)
                    for k in range(2):
                        kk = 2 * half + k
                        last = t_.matmul(msg_ps[(2 * bt + half) % 4][:, k, :],
                                         lhsT=pick[:, bt % 2, kk, :] if general else mix_sb[:, bt % 2, kk, :],
                                         rhs=gathered[:, g, hb * BATCH + kk, :] if general else window[:, g, :],
                                         start=True, stop=True)
                    last.then_inc(msg_done, 1)

            def body(q):
                first = isinstance(q, int)
                for bt in range(BATCHES):
                    t = BATCHES * q + bt
                    sources(q, bt)
                    if general:
                        if not (first and bt < 1):
                            message(t - 1, q if bt >= 1 else q - 1, (bt - 1) % BATCHES)
                        continue
                    if not (first and bt < 1):
                        mix(t - 1, (bt - 1) % BATCHES)
                    if not (first and bt < 2):
                        message(t - 2, q if bt >= 2 else q - 1, (bt - 2) % BATCHES)

            steps(pe, body)
            end = BATCHES * Q
            if general:
                message(end - 1, Q - 1, BATCHES - 1)
            else:
                mix(end - 1, BATCHES - 1)
                message(end - 2, Q - 1, BATCHES - 2)
                message(end - 1, Q - 1, BATCHES - 1)

        @block.tensor
        def _(pe):
            wide = pe.value_load(flag[0:1, 0:1], min_val=0, max_val=1)
            with pe.If(wide):
                tensor_body(pe, True)
            with pe.Else():
                tensor_body(pe, False)

        def scalar_body(act, general):
            def mix_copy(t, bt):
                act.wait_ge(mix_done, t + 1)
                wait_if(act, msg_done, 2 * t - 2)
                act.activation(mix_sb[:, bt % 2, :, :], mix_ps[bt % 2][:], ACT.Copy).then_inc(mix_copied, 1)

            def msg_copy(t, q, bt):
                for half in range(2):
                    act.wait_ge(msg_done, 2 * t + half + 1)
                    if not (isinstance(t, int) and t < 2):
                        for j in (2 * half, 2 * half + 1):
                            act.wait_ge(table_added[j], 16 * (t - 1))
                    k0 = (bt % 2) * BATCH + 2 * half
                    act.activation(msg[:, k0:k0 + 2, :], msg_ps[(2 * bt + half) % 4][:], ACT.Copy).then_inc(msg_copied, 1)

            def body(q):
                first = isinstance(q, int)
                for bt in range(BATCHES):
                    t = BATCHES * q + bt
                    if general:
                        msg_copy(t, q, bt)
                        continue
                    mix_copy(t, bt)
                    if not (first and bt < 1):
                        msg_copy(t - 1, q, (bt - 1) % BATCHES)

            steps(act, body)
            if not general:
                msg_copy(BATCHES * Q - 1, Q - 1, BATCHES - 1)

        @block.scalar
        def _(act):
            wide = act.value_load(flag[0:1, 0:1], min_val=0, max_val=1)
            with act.If(wide):
                scalar_body(act, True)
            with act.Else():
                scalar_body(act, False)

        @block.sync
        def _(sp):
            wide = sp.value_load(flag[0:1, 0:1], min_val=0, max_val=1)
            with sp.If(wide):
                sp.nop()
            with sp.Else():
                def body(q):
                    for g in range(SUPERS):
                        wait_if(sp, msg_done, 2 * PER_SUPER * (SUPERS * (q - 1) + g + 1))
                        r0 = sp.value_load(window_row[0:1, bass.ds(q, 1), g], min_val=0, max_val=N - P)
                        sp.dma_start(window[:, g, :], h_dram[bass.ds(r0, P), :]).then_inc(window_loaded[g], 16)

                steps(sp, body)

        def add_to_table(pool, q, bt):
            t = BATCHES * q + bt
            pool.wait_ge(rows_ready, t + 1)
            for j in range(BATCH):
                if j % 2 == 0:
                    pool.wait_ge(msg_copied, 2 * t + j // 2 + 1)
                if isinstance(t, int) and t == 0:
                    pool.wait_ge(table_cleared[j], 16 * v["CLEARS"])
                wait_if(pool, table_added[j], 16 * t)
                slot = bt * BATCH + j
                hold(pool)
                pool.indirect_dma_start(
                    out=tables[j], out_offset=bass.IndirectOffsetOnAxis(ap=put_row[:, slot:slot + 1], axis=0),
                    in_=msg[:, (bt % 2) * BATCH + j, :], in_offset=None,
                    compute_op=ALU.add).then_inc(table_added[j], 16)

        def gather_rows(pool, q, g):
            pool.wait_ge(target_ready, SUPERS * q + g + 1)
            wait_if(pool, msg_done, 2 * PER_SUPER * (SUPERS * (q - 1) + g + 1))
            for k in range(CH):
                hold(pool)
                pool.indirect_dma_start(
                    out=gathered[:, g, k, :], out_offset=None, in_=h_dram,
                    in_offset=bass.IndirectOffsetOnAxis(ap=target[:, g, k:k + 1], axis=0)).then_inc(rows_gathered[g], 16)

        @block.gpsimd
        def _(pool):
            wide = pool.value_load(flag[0:1, 0:1], min_val=0, max_val=1)
            with pool.If(wide):
                def general_body(q):
                    for g in range(SUPERS):
                        gather_rows(pool, q, g)
                        for hb in range(PER_SUPER):
                            if g == 0 and not isinstance(q, int):
                                add_to_table(pool, q - 1, (SUPERS - 1) * PER_SUPER + hb)
                            elif g > 0:
                                add_to_table(pool, q, (g - 1) * PER_SUPER + hb)

                steps(pool, general_body)
                for hb in range(PER_SUPER):
                    add_to_table(pool, Q - 1, (SUPERS - 1) * PER_SUPER + hb)
            with pool.Else():
                def body(q):
                    for bt in range(BATCHES):
                        add_to_table(pool, q, bt)

                steps(pool, body)
            for j in range(TABLES):
                pool.wait_ge(table_added[j], 16 * BATCHES * Q)


def combine(nc, v):
    hold = v['hold']
    (x, xn_dram, tables, sem, sb, base, wts, wr_sb, br_sb, bias_sb, tile_rows) = (
        v[n] for n in "x xn_dram tables sem sb base wts wr_sb br_sb bias_sb tile_rows".split())
    N, D, GROUPS, TAIL, LAST, NT = (v[n] for n in "N D GROUPS TAIL LAST NT".split())
    ident = v["consts"]["ident"]
    with ExitStack() as c:
        parts = sb(c, "parts", [P, 2, TABLES, TG, D])
        xb = sb(c, "xb", [P, 2, TG, D])
        x1 = sb(c, "x1", [P, 2, TG, D])
        xn = sb(c, "xn1", [P, 2, TG, D])
        stats = sb(c, "stats1", [P, TG, 6])
        mv = sb(c, "mv1", [P, TG, 2])
        std = sb(c, "std1", [P, TG])
        junk = sb(c, "junk", [P, TG, D])
        wcur = sb(c, "wcur", [P, TG])
        sum_ps = [c.enter_context(nc.psum_tensor(f"sum_ps{i}", [P, TG, D], F32)) for i in range(2)]
        parts_loaded = [sem(f"parts_loaded{i}") for i in range(2)]
        x_loaded = [sem(f"x1_loaded{i}") for i in range(2)]
        parts_summed = sem("parts_summed")
        bias_added = sem("bias_added")
        x1_ready = sem("x1_ready")
        xn_ready = sem("xn_ready")
        base_ready = sem("base_ready")
        dotted = sem("dotted")
        xn_stored = [sem(f"xn_stored{i}") for i in range(2)]
        step = sem("combine_dve_step")
        mv_ready = sem("mv1_ready")
        std_ready = sem("std1_ready")
        block = c.enter_context(nc.Block())

        @block.sync
        def _(sp):
            def load(i, b, tiles=TG):
                g = 2 * i + b
                wait_if(sp, parts_summed, g - 1)
                for j in range(TABLES):
                    sp.dma_start(parts[:, b, j, 0:tiles, :], tile_rows(tables[j], g, tiles)).then_inc(parts_loaded[b], 16)
                wait_if(sp, x1_ready, g - 1)
                if tiles == TG:
                    sp.dma_start(xb[:, b, :, :], tile_rows(x, g)).then_inc(x_loaded[b], 16)
                else:
                    n0 = GROUPS * TG * P
                    sp.dma_start(xb[:, b, 0:tiles - 1, :], x[n0:n0 + (tiles - 1) * P, :]
                                 .rearrange("(t p) d -> p t d", p=P)).then_inc(x_loaded[b], 16)
                    sp.dma_start(xb[0:LAST, b, tiles - 1, :], x[N - LAST:N, :]).then_inc(x_loaded[b], 16)

            load(0, 0)
            load(0, 1)
            with sp.Fori(1, GROUPS // 2) as i:
                load(i, 0)
                load(i, 1)
            load(GROUPS // 2, 0, TAIL)

        @block.tensor
        def _(pe):
            def add_tables(i, b, tiles=TG):
                g = 2 * i + b
                pe.wait_ge(parts_loaded[b], 16 * TABLES * (i + 1))
                wait_if(pe, x1_ready, g - 1)
                half = TG // 2
                for t0 in range(0, tiles, half):
                    for j in range(TABLES):
                        last = nc.tensor.matmul(sum_ps[b][:, t0:t0 + half, :], lhsT=ident[:], rhs=parts[:, b, j, t0:t0 + half, :],
                                                start=(j == 0), stop=(j == TABLES - 1))
                last.then_inc(parts_summed, 1)

            add_tables(0, 0)
            add_tables(0, 1)
            with pe.Fori(1, GROUPS // 2) as i:
                add_tables(i, 0)
                add_tables(i, 1)
            add_tables(GROUPS // 2, 0, TAIL)

        @block.scalar
        def _(act):
            def root_and_store(i, b, tiles=TG):
                g = 2 * i + b
                act.wait_ge(mv_ready, g + 1)
                act.activation(std[:, 0:tiles], mv[:, 0:tiles, 1], ACT.Sqrt, bias=v["eps"][:]).then_inc(std_ready, 1)
                act.wait_ge(xn_ready, g + 1)
                act.dma_start(tile_rows(xn_dram, g, tiles), xn[:, b, 0:tiles, :]).then_inc(xn_stored[b], 16)

            root_and_store(0, 0)
            root_and_store(0, 1)
            with act.Fori(1, GROUPS // 2) as i:
                root_and_store(i, 0)
                root_and_store(i, 1)
            root_and_store(GROUPS // 2, 0, TAIL)
            act.wait_ge(xn_stored[0], 16 * (GROUPS // 2 + 1))
            act.wait_ge(xn_stored[1], 16 * (GROUPS // 2))

        @block.gpsimd
        def _(pool):
            def add_bias(i, b, tiles=TG):
                pool.wait_ge(x_loaded[b], 16 * (i + 1) + (0 if tiles == TG else 16))
                nc.gpsimd.tensor_tensor(xb[:, b, 0:tiles, :], xb[:, b, 0:tiles, :],
                                        bias_sb[:].unsqueeze(1).to_broadcast([P, tiles, D]), ALU.add).then_inc(bias_added, 1)

            def keep_base(i, b, tiles=TG):
                g = 2 * i + b
                pool.wait_ge(xn_ready, g + 1)
                nc.gpsimd.tensor_tensor(base[:, bass.ds(g * TG, tiles), :], x1[:, b, 0:tiles, :], xn[:, b, 0:tiles, :],
                                        ALU.add).then_inc(base_ready, 1)

            pool.wait_ge(v["weights_loaded"], 16 * 7)
            add_bias(0, 0)
            add_bias(0, 1)
            keep_base(0, 0)
            with pool.Fori(1, GROUPS // 2) as i:
                add_bias(i, 0)
                keep_base(i - 1, 1)
                add_bias(i, 1)
                keep_base(i, 0)
            add_bias(GROUPS // 2, 0, TAIL)
            keep_base(GROUPS // 2 - 1, 1)
            keep_base(GROUPS // 2, 0, TAIL)

        @block.vector
        def _(dve):
            vec = nc.vector
            st = Steps(dve, step)
            dve.wait_ge(v["weights_loaded"], 16 * 7)
            vec.memset(wts[:], float("-inf"))

            def group(i, b, tiles=TG):
                g = 2 * i + b
                dve.wait_ge(parts_summed, g + 1)
                dve.wait_ge(bias_added, g + 1)
                wait_if(dve, base_ready, g - 1)
                vec.tensor_tensor(x1[:, b, 0:tiles, :], sum_ps[b][:, 0:tiles, :], xb[:, b, 0:tiles, :],
                                  ALU.add).then_inc(x1_ready, 1)
                dve.wait_ge(x1_ready, g + 1)
                for t in range(tiles):
                    last = vec.bn_stats(stats[:, t, :], x1[:, b, t, :])
                st.wait(last)
                hold(dve)
                for t in range(tiles):
                    last = vec.bn_aggr(mv[:, t, :], stats[:, t, :])
                last.then_inc(mv_ready, 1)
                dve.wait_ge(std_ready, g + 1)
                st.wait(vec.reciprocal(std[:, 0:tiles], std[:, 0:tiles]))
                wait_if(dve, xn_stored[b], 16 * i)
                for t in range(tiles):
                    last = vec.tensor_scalar(xn[:, b, t, :], x1[:, b, t, :], mv[:, t, 0:1], std[:, t:t + 1],
                                             ALU.subtract, ALU.mult)
                last.then_inc(xn_ready, 1)
                dve.wait_ge(xn_ready, g + 1)
                for t in range(tiles):
                    last = vec.tensor_tensor_reduce(out=junk[:, t, :], in0=xn[:, b, t, :], in1=wr_sb[:], scale=1.0, scalar=0.0,
                                                    op0=ALU.mult, op1=ALU.add, accum_out=wcur[:, t:t + 1])
                st.wait(last)
                if tiles == TG:
                    vec.tensor_scalar(wts[:, bass.ds(g * TG, TG)], wcur[:], br_sb[:], None, ALU.add)
                else:
                    vec.tensor_scalar(wts[:, NT - tiles:NT - 1], wcur[:, 0:tiles - 1], br_sb[:], None, ALU.add)
                    vec.tensor_scalar(wts[0:LAST, NT - 1:NT], wcur[0:LAST, tiles - 1:tiles], br_sb[0:LAST, :], None, ALU.add)

            group(0, 0)
            group(0, 1)
            a_step = st.k
            with dve.Fori(1, GROUPS // 2) as i:
                st.rebase(i * a_step)
                group(i, 0)
                group(i, 1)
            st.rebase((GROUPS // 2) * a_step)
            group(GROUPS // 2, 0, TAIL)


def choose(nc, v):
    (out, sem, sb, base, wts, kept_row, consts) = (v[n] for n in "out sem sb base wts kept_row consts".split())
    N, D, NT, LAST, KEPT, SLOTS, base_stored = (v[n] for n in "N D NT LAST KEPT SLOTS base_stored".split())
    before, ones, row, col = (consts[n] for n in ("before", "ones", "row", "col"))
    DIGITS = 8
    PART = 14
    assert NT % PART == 0
    with ExitStack() as c:
        def ps(name, shape):
            return c.enter_context(nc.psum_tensor(name, shape, F32))

        half_i = [sb(c, f"half_i{i}", [P, NT], I32) for i in range(2)]
        key = [sb(c, f"key{i}", [P, NT]) for i in range(2)]
        neg = sb(c, "neg", [P, NT])
        tmp = sb(c, "tmp", [P, NT])
        junk = sb(c, "junk2", [P, 3, NT])
        cand = sb(c, "cand", [P, 3])
        found = sb(c, "found", [P, 1])
        unit = sb(c, "unit", [P, 1])
        digit = sb(c, "digit", [P, 1])
        reached = sb(c, "reached", [P, 3])
        cnt = sb(c, "cnt", [P, 3])
        tied_left = sb(c, "tied_left", [P, 1])
        above = sb(c, "above", [P, NT], BF16)
        tied = sb(c, "tied", [P, NT], BF16)
        chosen = sb(c, "chosen", [P, NT], BF16)
        ones_b = sb(c, "ones_b", [P, P], BF16)
        total_b = sb(c, "total_b", [NT, P], BF16)
        rank = sb(c, "rank", [P, NT])
        rank_i = sb(c, "rank_i", [P, NT], I32)
        part_i = [sb(c, f"part_i{i}", [P, NT], I32) for i in range(2)]
        part = [sb(c, f"part{i}", [P, NT]) for i in range(2)]
        in_slot = sb(c, "in_slot", [P, 2, PART, P], BF16)
        in_tile = sb(c, "in_tile", [P, 2, PART, SLOTS], BF16)
        number = sb(c, "number", [P, 2, PART, 2, SLOTS], BF16)
        number_f = sb(c, "number_f", [P, 2, SLOTS])
        tot_ps = ps("tot_ps", [P, 3])
        all_ps = ps("all_ps", [P, NT])
        col_ps = ps("col_ps", [NT, 1])
        rank_ps = ps("rank_ps", [P, NT])
        num_ps = ps("num_ps", [P, 2, SLOTS])
        step = sem("choose_dve_step")
        counted = sem("counted")
        totalled = sem("totalled")
        ready = sem("mask_ready")
        summed = sem("mask_summed")
        spread = sem("totals_spread")
        ranked = sem("ranked")
        hot = sem("hot_ready")
        packed = sem("packed")
        tile_placed = sem("tile_placed")
        place_ready = sem("place_ready")
        block = c.enter_context(nc.Block())

        @block.sync
        def _(sp):
            sp.dma_start(out[0:N - LAST, :].rearrange("(t p) d -> p t d", p=P), base[:, 0:NT - 1, :]).then_inc(base_stored, 16)
            sp.dma_start(out[N - LAST:N, :], base[0:LAST, NT - 1, :]).then_inc(base_stored, 16)
            sp.wait_ge(base_stored, 32)

        @block.gpsimd
        def _(pool):
            for n in range(NT // PART):
                pool.wait_ge(tile_placed, n + 1)
                nc.gpsimd.tensor_scalar(number[:, n % 2, :, 1, :], in_tile[:, n % 2, :, :], col[:], None, ALU.mult).then_inc(place_ready, 1)

        @block.tensor
        def _(pe):
            t = nc.tensor

            def total(n):
                pe.wait_ge(counted, n + 1)
                t.matmul(tot_ps[:], lhsT=ones[:], rhs=cnt[:], start=True, stop=True).then_inc(totalled, 1)

            with pe.Fori(0, 2 * DIGITS) as n:
                total(n)
            pe.wait_ge(ready, 1)
            t.matmul(all_ps[:], lhsT=ones_b[:], rhs=above[:], start=True, stop=True)
            for n, mask in enumerate((tied, chosen)):
                pe.wait_ge(ready, n + 1)
                t.matmul(col_ps[:], lhsT=mask[:], rhs=ones_b[:, 0:1], start=True, stop=True).then_inc(summed, 1)
                pe.wait_ge(spread, n + 1)
                t.matmul(rank_ps[:], lhsT=before[:], rhs=mask[:], start=True, stop=False)
                t.matmul(rank_ps[:], lhsT=total_b[:], rhs=before[0:NT, 0:NT], start=False, stop=True).then_inc(ranked, 1)
            for n in range(NT // PART):
                pe.wait_ge(hot, n + 1)
                pe.wait_ge(place_ready, n + 1)
                for j in range(PART):
                    last = t.matmul(num_ps[:], lhsT=in_slot[:, n % 2, j, :], rhs=number[:, n % 2, j, :, :],
                                    start=(n == 0 and j == 0), stop=(n == NT // PART - 1 and j == PART - 1))
                last.then_inc(packed, 1)

        @block.vector
        def _(dve):
            vec = nc.vector
            st = Steps(dve, step)
            bits = wts[:].bitcast(I32)
            vec.memset(ones_b[:], 1.0)
            vec.tensor_scalar(half_i[0][:], bits, 16, None, ALU.logical_shift_right)
            st.wait(vec.tensor_scalar(half_i[1][:], bits, 0xFFFF, None, ALU.bitwise_and))
            vec.tensor_copy(key[1][:], half_i[1][:])
            st.wait(vec.tensor_copy(key[0][:], half_i[0][:]))
            vec.tensor_scalar(neg[:], key[0][:], 32768.0, None, ALU.is_ge)
            st.wait(vec.tensor_scalar(tmp[:], key[0][:], -2.0, 32767.0, ALU.mult, ALU.add))
            st.wait(vec.tensor_tensor(tmp[:], tmp[:], neg[:], ALU.mult))
            st.wait(vec.scalar_tensor_tensor(out=key[0][:], in0=key[0][:], scalar=32768.0, in1=tmp[:], op0=ALU.add, op1=ALU.add))
            st.wait(vec.tensor_scalar(tmp[:], key[1][:], -2.0, 65535.0, ALU.mult, ALU.add))
            st.wait(vec.tensor_tensor(tmp[:], tmp[:], neg[:], ALU.mult))
            st.wait(vec.tensor_tensor(key[1][:], key[1][:], tmp[:], ALU.add))
            for half in range(2):
                if half:
                    st.wait(vec.tensor_scalar(tmp[:], key[0][:], found[:], 65536.0, ALU.subtract, ALU.mult))
                    st.wait(vec.tensor_tensor(key[1][:], key[1][:], tmp[:], ALU.add))
                vec.memset(found[:], 0.0)
                vec.memset(unit[:], float(4 ** (DIGITS - 1)))
                st.wait(vec.tensor_scalar(cand[:], row[:, 1:4], float(4 ** (DIGITS - 1)), None, ALU.mult))
                first = st.base + st.k
                with dve.Fori(0, DIGITS) as i:
                    st.rebase(first + i * 4)
                    for j in range(3):
                        last = vec.tensor_scalar(junk[:, j, :], key[half][:], cand[:, j:j + 1], 0.0, ALU.is_ge, ALU.add,
                                                 accum_out=cnt[:, j:j + 1])
                    last.then_inc(counted, 1)
                    dve.wait_ge(totalled, i + (DIGITS * half + 1))
                    st.wait(vec.tensor_scalar(reached[:], tot_ps[:], float(KEPT), 0.0, ALU.is_ge, ALU.add, accum_out=digit[:]))
                    st.wait(vec.scalar_tensor_tensor(out=found[:], in0=digit[:], scalar=unit[:], in1=found[:],
                                                     op0=ALU.mult, op1=ALU.add))
                    st.wait(vec.tensor_scalar(unit[:], unit[:], 0.25, None, ALU.mult))
                    st.wait(vec.tensor_scalar(cand[:], row[:, 1:4], unit[:], found[:], ALU.mult, ALU.add))
                st.rebase(first + DIGITS * 4)
            top = found
            vec.tensor_scalar(above[:], key[1][:], top[:], None, ALU.is_gt)
            vec.tensor_scalar(tied[:], key[1][:], top[:], None, ALU.is_equal).then_inc(ready, 1)

            def spread_totals(n):
                dve.wait_ge(summed, n + 1)
                vec.tensor_copy(total_b[:], col_ps[:].to_broadcast([NT, P])).then_inc(spread, 1)
                dve.wait_ge(ranked, n + 1)

            spread_totals(0)
            st.wait(vec.tensor_reduce(digit[:], all_ps[:], op=ALU.add, axis=AX.X))
            st.wait(vec.tensor_scalar(tied_left[:], digit[:], -1.0, float(KEPT), ALU.mult, ALU.add))
            st.wait(vec.tensor_scalar(tmp[:], rank_ps[:], tied_left[:], None, ALU.is_lt))
            st.wait(vec.tensor_tensor(tmp[:], tmp[:], tied[:], ALU.mult))
            vec.tensor_tensor(chosen[:], tmp[:], above[:], ALU.add).then_inc(ready, 1)
            spread_totals(1)
            st.wait(vec.scalar_tensor_tensor(out=rank[:], in0=rank_ps[:], scalar=1.0, in1=chosen[:], op0=ALU.add, op1=ALU.mult))
            st.wait(vec.tensor_scalar(rank_i[:], rank[:], -1.0, None, ALU.add))
            vec.tensor_scalar(part_i[0][:], rank_i[:], 7, None, ALU.arith_shift_right)
            st.wait(vec.tensor_scalar(part_i[1][:], rank_i[:], P - 1, None, ALU.bitwise_and))
            vec.tensor_copy(part[0][:], part_i[0][:])
            st.wait(vec.tensor_copy(part[1][:], part_i[1][:]))
            for n in range(NT // PART):
                r, t0 = n % 2, n * PART
                wait_if(dve, packed, n - 1)
                st.wait(vec.tensor_tensor(in_tile[:, r, :, :], part[0][:, t0:t0 + PART].unsqueeze(2).to_broadcast([P, PART, SLOTS]),
                                          row[:, 0:SLOTS].unsqueeze(1).to_broadcast([P, PART, SLOTS]), ALU.is_equal))
                for j in range(PART):
                    last = vec.tensor_scalar(number[:, r, j, 0, :], in_tile[:, r, j, :], float(t0 + j), None, ALU.mult)
                last.then_inc(tile_placed, 1)
                vec.tensor_tensor(in_slot[:, r, :, :], part[1][:, t0:t0 + PART].unsqueeze(2).to_broadcast([P, PART, P]),
                                  row[:].unsqueeze(1).to_broadcast([P, PART, P]), ALU.is_equal).then_inc(hot, 1)
            dve.wait_ge(packed, NT // PART)
            st.wait(vec.tensor_copy(number_f[:], num_ps[:]))
            vec.memset(kept_row[:, SLOTS:], 0)
            vec.scalar_tensor_tensor(out=kept_row[:, 0:SLOTS], in0=number_f[:, 0, :], scalar=float(P), in1=number_f[:, 1, :],
                                     op0=ALU.mult, op1=ALU.add)


def ffn(nc, v):
    hold = v['hold']
    (out, xn_dram, sem, sb, kept_row, consts, w1_parts, w2_parts, b1_sb, b2_sb, wr_sb, br_sb) = (
        v[n] for n in "out xn_dram sem sb kept_row consts w1_parts w2_parts b1_sb b2_sb wr_sb br_sb".split())
    N, D, NT, KD, KH, KEPT, SLOTS, SG = (v[n] for n in "N D NT KD KH KEPT SLOTS SG".split())
    ident = consts["ident"]
    LAST_SLOTS = KEPT - (SLOTS - 1) * P
    with ExitStack() as c:
        def ps(name, shape):
            return c.enter_context(nc.psum_tensor(name, shape, F32))

        from_row = sb(c, "from_row", [P, 2, TG], I32)
        to_row = sb(c, "to_row", [P, 2, TG], I32)
        xg = sb(c, "xg", [P, 2, TG, D])
        xgT = sb(c, "xgT", [P, 2, 2, KD, TG * P], F32R)
        act_out = sb(c, "act_out", [P, 2, TG * P])
        hidden = sb(c, "hidden", [P, 2, KH, TG * P], F32R)
        route = sb(c, "route", [P, 2, TG])
        route_in = sb(c, "route_in", [P, 2, TG])
        junk = sb(c, "junk3", [P, TG, D])
        y1 = sb(c, "y1", [P, TG, D])
        y = sb(c, "y", [P, 2, TG, D])
        xt_ps = ps("xgt_ps", [P, KD, TG * P])
        up_ps = [ps(f"up_ps{i}", [P, TG * P]) for i in range(2)]
        y_ps = [ps(f"y_ps{i}", [P, TG, D]) for i in range(2)]
        from_ready = sem("from_ready")
        xg_loaded = [sem(f"xg_loaded{i}") for i in range(2)]
        xg_turned = sem("xg_turned")
        xgT_ready = sem("xgT_ready")
        routed = sem("routed")
        up_done = sem("up_done")
        gelu_done = sem("gelu_done")
        hidden_ready = sem("hidden_ready")
        down_done = sem("down_done")
        y_ready = sem("y_ready")
        y_added = [sem(f"y_added{i}") for i in range(2)]
        step = sem("ffn_dve_step")
        block = c.enter_context(nc.Block())
        HALF = SG // 2

        @block.gpsimd
        def _(pool):
            def gather(i, b, tiles=TG):
                g = 2 * i + b
                pool.wait_ge(from_ready, g + 1)
                wait_if(pool, xg_turned, g - 1)
                wait_if(pool, routed, g - 1)
                for k in range(tiles):
                    hold(pool)
                    pool.indirect_dma_start(
                        out=xg[:, b, k, :], out_offset=None, in_=xn_dram,
                        in_offset=bass.IndirectOffsetOnAxis(ap=from_row[:, b, k:k + 1], axis=0)).then_inc(xg_loaded[b], 16)

            def add(i, b, tiles=TG):
                g = 2 * i + b
                pool.wait_ge(y_ready, g + 1)
                for k in range(tiles):
                    n = P if tiles == TG else LAST_SLOTS
                    hold(pool)
                    pool.indirect_dma_start(
                        out=out, out_offset=bass.IndirectOffsetOnAxis(ap=to_row[0:n, b, k:k + 1], axis=0),
                        in_=y[0:n, b, k, :], in_offset=None,
                        compute_op=ALU.add).then_inc(y_added[b], 16)

            gather(0, 0)
            gather(0, 1)
            with pool.Fori(1, HALF) as i:
                for b in range(2):
                    gather(i, b)
                    add(i - 1, b)
            gather(HALF, 0, 1)
            add(HALF - 1, 0)
            add(HALF - 1, 1)
            add(HALF, 0, 1)
            pool.wait_ge(y_added[0], 16 * (TG * HALF + 1))
            pool.wait_ge(y_added[1], 16 * TG * HALF)

        @block.vector
        def _(dve):
            vec = nc.vector
            st = Steps(dve, step)

            a_step = 2 * (2 + 1 + KH)

            def take_from(i, b):
                vec.tensor_copy(from_row[:, b, :], kept_row[:, bass.ds((2 * i + b) * TG, TG)]).then_inc(from_ready, 1)

            def turn(i, b, tiles=TG):
                g = 2 * i + b
                dve.wait_ge(xg_turned, g + 1)
                wait_if(dve, up_done, KH * (g - 1))
                cols = slice(0, tiles * P)
                st.wait(vec.tensor_copy(xgT[:, b, 0, :, cols], xt_ps[:, :, cols]))
                vec.tensor_tensor(xgT[:, b, 1, :, cols], xt_ps[:, :, cols], xgT[:, b, 0, :, cols].bitcast(F32),
                                  ALU.subtract).then_inc(xgT_ready, 1)
                for k in range(tiles):
                    last = vec.tensor_tensor_reduce(out=junk[:, k, :], in0=xg[:, b, k, :], in1=wr_sb[:], scale=1.0, scalar=0.0,
                                                    op0=ALU.mult, op1=ALU.add, accum_out=route_in[:, b, k:k + 1])
                st.wait(last)
                vec.tensor_scalar(route[:, b, 0:tiles], route_in[:, b, 0:tiles], br_sb[:], None, ALU.add).then_inc(routed, 1)

            def split_hidden(i, b, tiles=TG):
                g = 2 * i + b
                cols = slice(0, tiles * P)
                wait_if(dve, down_done, g)
                for m in range(KH):
                    dve.wait_ge(gelu_done, KH * g + m + 1)
                    st.wait(vec.tensor_copy(hidden[:, 0, m, cols], act_out[:, m % 2, cols]))
                    vec.tensor_tensor(hidden[:, 1, m, cols], act_out[:, m % 2, cols], hidden[:, 0, m, cols].bitcast(F32),
                                      ALU.subtract).then_inc(hidden_ready, 1)

            def scale(i, b, tiles=TG):
                g = 2 * i + b
                dve.wait_ge(down_done, g + 1)
                wait_if(dve, y_ready, g)
                wait_if(dve, y_added[b], 16 * TG * i)
                vec.tensor_copy(to_row[:, b, 0:tiles], kept_row[:, bass.ds(g * TG, tiles)])
                st.wait(vec.tensor_tensor(y1[:, 0:tiles, :], y_ps[b][:, 0:tiles, :],
                                          b2_sb[:].unsqueeze(1).to_broadcast([P, tiles, D]), ALU.add))
                for k in range(tiles):
                    last = vec.tensor_scalar(y[:, b, k, :], y1[:, k, :], route[:, b, k:k + 1], None, ALU.mult)
                last.then_inc(y_ready, 1)

            take_from(0, 0)
            take_from(0, 1)
            turn(0, 0)
            take_from(1, 0)
            split_hidden(0, 0)
            turn(0, 1)
            take_from(1, 1)
            first = st.k
            with dve.Fori(1, HALF) as i:
                st.rebase(first + (i - 1) * a_step)
                split_hidden(i - 1, 1)
                scale(i - 1, 0)
                turn(i, 0)
                take_from(i + 1, 0)
                split_hidden(i, 0)
                scale(i - 1, 1)
                turn(i, 1)
                take_from(i + 1, 1)
                assert st.k == a_step
            st.rebase(first + (HALF - 1) * a_step)
            split_hidden(HALF - 1, 1)
            scale(HALF - 1, 0)
            turn(HALF, 0, 1)
            split_hidden(HALF, 0, 1)
            scale(HALF - 1, 1)
            scale(HALF, 0, 1)

        @block.tensor
        def _(pe):
            t = nc.tensor

            def turn(i, b, tiles=TG):
                g = 2 * i + b
                pe.wait_ge(xg_loaded[b], 16 * (TG * i + tiles))
                wait_if(pe, xgT_ready, g)
                for j in range(tiles):
                    for k in range(KD):
                        last = t.transpose(xt_ps[:, k, j * P:(j + 1) * P], xg[:, b, j, k * P:(k + 1) * P], ident[:])
                last.then_inc(xg_turned, 1)

            def up(i, b, tiles=TG):
                g = 2 * i + b
                pe.wait_ge(xgT_ready, g + 1)
                for m in range(KH):
                    wait_if(pe, gelu_done, KH * g + m - 1)
                    for n, (k, (pw, px)) in enumerate((k, p) for k in range(KD) for p in PAIRS):
                        last = t.matmul(up_ps[m % 2][:, 0:tiles * P], lhsT=w1_parts[:, pw, k, m * P:(m + 1) * P],
                                        rhs=xgT[:, b, px, k, 0:tiles * P], start=(n == 0), stop=(n == KD * len(PAIRS) - 1))
                    last.then_inc(up_done, 1)

            def down(i, b, tiles=TG):
                g = 2 * i + b
                pe.wait_ge(hidden_ready, KH * (g + 1))
                wait_if(pe, y_ready, g - 1)
                for j in range(tiles):
                    for n, (m, (pw, px)) in enumerate((m, p) for m in range(KH) for p in PAIRS):
                        last = t.matmul(y_ps[b][:, j, :], lhsT=hidden[:, px, m, j * P:(j + 1) * P],
                                        rhs=w2_parts[:, pw, m, :], start=(n == 0), stop=(n == KH * len(PAIRS) - 1))
                last.then_inc(down_done, 1)

            turn(0, 0)
            up(0, 0)
            turn(0, 1)
            down(0, 0)
            with pe.Fori(1, HALF) as i:
                up(i - 1, 1)
                turn(i, 0)
                down(i - 1, 1)
                up(i, 0)
                turn(i, 1)
                down(i, 0)
            up(HALF - 1, 1)
            turn(HALF, 0, 1)
            down(HALF - 1, 1)
            up(HALF, 0, 1)
            down(HALF, 0, 1)

        @block.scalar
        def _(act):
            def gelu(i, b, tiles=TG):
                g = 2 * i + b
                for m in range(KH):
                    act.wait_ge(up_done, KH * g + m + 1)
                    wait_if(act, hidden_ready, KH * g + m - 1)
                    act.activation(act_out[:, m % 2, 0:tiles * P], up_ps[m % 2][:, 0:tiles * P], ACT.Gelu_apprx_tanh,
                                   bias=b1_sb[:, m:m + 1]).then_inc(gelu_done, 1)

            gelu(0, 0)
            gelu(0, 1)
            with act.Fori(1, HALF) as i:
                gelu(i, 0)
                gelu(i, 1)
            gelu(HALF, 0, 1)


_INS = ["x", "src", "dst", "edge_weight", "L0_gnn_W", "L0_gnn_bias", "L0_ffn_wr", "L0_ffn_br", "L0_ffn_w1",
        "L0_ffn_b1", "L0_ffn_w2", "L0_ffn_b2"]
_OUTS = [((12500, 256), "float32")]


def kernel(**inputs):
    import numpy as _np
    import concourse.bacc as _bacc
    from concourse import mybir as _mybir
    from concourse.bass_utils import run_bass_kernel_spmd as _run

    nc = _bacc.Bacc("TRN2", target_bir_lowering=False, num_devices=1)
    arrays, args = {}, []
    for name in _INS:
        a = _np.ascontiguousarray(inputs[name])
        arrays[f"in_{name}"] = a
        args.append(nc.dram_tensor(f"in_{name}", a.shape, _mybir.dt.from_np(a.dtype), kind="ExternalInput").ap())
    for i, (shape, dtype) in enumerate(_OUTS):
        args.append(nc.dram_tensor(f"out_{i}", shape, _mybir.dt.from_np(_np.dtype(dtype)), kind="ExternalOutput").ap())
    build(nc, *args)
    r = _run(nc, [arrays], core_ids=[0])
    return r.results[0]["out_0"]
```

```python
from contextlib import ExitStack

import concourse.bass as bass
from concourse import mybir

P = 128
F32 = mybir.dt.float32
F32R = mybir.dt.float32r
BF16 = mybir.dt.bfloat16
I32 = mybir.dt.int32
ALU = mybir.AluOpType
ACT = mybir.ActivationFunctionType
AX = mybir.AxisListType

EPS = 1e-5
TABLES = 4
EARLY = 1
CLEAR_ROWS = 11
RUN_EDGES = 1024
CH = RUN_EDGES // P
STEP_RUNS = 2
BATCH = 4
TG = 4
WEIGHTS = 8
CONSTS = 11
NFIELD = 5
SRC, REL, WGT, SPARE, DST = range(NFIELD)
PAIRS = ((0, 0), (0, 1), (1, 0))


class Kit:
    pass


def is_zero(value):
    return isinstance(value, int) and value == 0


def hold(kit, engine):
    engine.sem_inc(kit.held, 1)


class Steps:

    def __init__(self, engine, sem):
        self.engine, self.sem, self.base, self.k = engine, sem, 0, 0

    def rebase(self, base):
        self.base, self.k = base, 0

    def wait(self, instruction):
        instruction.then_inc(self.sem, 1)
        self.k += 1
        self.engine.wait_ge(self.sem, self.base + self.k)


def wait_if(engine, sem, value):
    if not isinstance(value, int) or value > 0:
        engine.wait_ge(sem, value)


def build_constants(nc, kit):
    g = nc.gpsimd
    st = Steps(g, kit.consts_ready)
    st.wait(g.memset(kit.ident[:], 0.0))
    st.wait(g.affine_select(out=kit.ident[:], in_=kit.ident[:], compare_op=ALU.not_equal, fill=1.0,
                            base=0, pattern=[[-1, P]], channel_multiplier=1))
    st.wait(g.memset(kit.lower[:], 1.0))
    st.wait(g.affine_select(out=kit.lower[:], in_=kit.lower[:], compare_op=ALU.is_gt, fill=0.0,
                            base=0, pattern=[[-1, P]], channel_multiplier=1))
    st.wait(g.memset(kit.before[:], 1.0))
    st.wait(g.affine_select(out=kit.before[:], in_=kit.before[:], compare_op=ALU.is_gt, fill=0.0,
                            base=0, pattern=[[1, P]], channel_multiplier=-1))
    st.wait(g.memset(kit.ones[:], 1.0))
    st.wait(g.iota(kit.row[:], pattern=[[1, P]], base=0, channel_multiplier=0,
                   allow_small_or_imprecise_dtypes=True))
    st.wait(g.iota(kit.col[:], pattern=[[0, 1]], base=0, channel_multiplier=1,
                   allow_small_or_imprecise_dtypes=True))
    st.wait(g.memset(kit.eps[:], EPS))
    st.wait(g.memset(kit.zero[:], 0.0))
    assert st.k == CONSTS


def build(nc, x, src, dst, wgt, W, bias, wr, br, w1, b1, w2, b2, out):
    N, D = x.shape
    E = src.shape[0]
    H = w1.shape[1]
    KD, KH = D // P, H // P
    NT = -(-N // P)
    LAST = N - (NT - 1) * P
    GROUPS = NT // TG
    TAIL = NT - GROUPS * TG
    S = -(-E // RUN_EDGES)
    S += S % STEP_RUNS
    Q = S // STEP_RUNS
    OVER = S * RUN_EDGES - E
    BATCHES = STEP_RUNS * CH // BATCH
    KEPT = max(1, int(0.5 * N)) - 1
    SLOTS = -(-KEPT // P)
    SG = SLOTS // TG
    STAIL = SLOTS - SG * TG
    assert Q <= P and OVER < RUN_EDGES and GROUPS % 2 == 0 and TAIL and SG % 2 == 0 and STAIL == 1
    CLEARS = -(-(N + P) // (P * CLEAR_ROWS))
    ROWS = CLEARS * P * CLEAR_ROWS
    assert ROWS >= N + P and ROWS >= NT * P

    kit = Kit()
    kit.x, kit.src, kit.dst, kit.wgt, kit.out = x, src, dst, wgt, out
    kit.W, kit.bias, kit.wr, kit.br, kit.w1, kit.b1, kit.w2, kit.b2 = W, bias, wr, br, w1, b1, w2, b2
    kit.N, kit.D, kit.H, kit.KD, kit.KH = N, D, H, KD, KH
    kit.NT, kit.LAST, kit.GROUPS, kit.TAIL = NT, LAST, GROUPS, TAIL
    kit.Q, kit.OVER, kit.BATCHES, kit.CLEARS = Q, OVER, BATCHES, CLEARS
    kit.KEPT, kit.SLOTS, kit.SG = KEPT, SLOTS, SG
    kit.xn_dram = nc.dram_tensor("xn_rows", [NT * P, D], F32, kind="Internal").ap()
    kit.tables = [nc.dram_tensor(f"aggregate{i}", [ROWS, D], F32, kind="Internal").ap() for i in range(TABLES)]

    with ExitStack() as whole:
        def sem(name):
            return whole.enter_context(nc.semaphore(name))

        def sb(ctx, name, shape, dt=F32):
            return ctx.enter_context(nc.sbuf_tensor(name, shape, dt))

        kit.sem, kit.sb = sem, sb
        kit.ident = sb(whole, "ident", [P, P])
        kit.lower = sb(whole, "lower", [P, P])
        kit.before = sb(whole, "before", [P, P], BF16)
        kit.ones = sb(whole, "ones", [P, P])
        kit.row = sb(whole, "row", [P, P])
        kit.col = sb(whole, "col", [P, 1])
        kit.eps = sb(whole, "eps", [P, 1])
        kit.w1_parts = sb(whole, "w1_parts", [P, 2, KD, H], F32R)
        kit.w2_parts = sb(whole, "w2_parts", [P, 2, KH, D], F32R)
        kit.b1_sb = sb(whole, "b1_sb", [P, KH])
        kit.b2_sb = sb(whole, "b2_sb", [P, D])
        kit.wr_sb = sb(whole, "wr_sb", [P, D])
        kit.br_sb = sb(whole, "br_sb", [P, 1])
        kit.bias_sb = sb(whole, "bias_sb", [P, D])
        kit.W_sb = sb(whole, "W_sb", [P, KD, D])

        kit.consts_ready = sem("consts_ready")
        kit.weights_loaded = sem("weights_loaded")
        kit.table_cleared = [sem(f"table_cleared{i}") for i in range(TABLES)]
        kit.table_added = [sem(f"table_added{i}") for i in range(TABLES)]
        kit.held = sem("held")

        with ExitStack() as edge_ctx:
            kit.zero = sb(edge_ctx, "zero", [P, CLEAR_ROWS * D])
            kit.edges = sb(edge_ctx, "edges", [P, Q + 1, STEP_RUNS, NFIELD, CH])
            kit.window_row = sb(edge_ctx, "window_row", [1, Q + 1, STEP_RUNS], I32)
            kit.flag = sb(edge_ctx, "flag", [1, 1], I32)
            prepare(nc, kit)
            edge_sums(nc, kit)
        with ExitStack() as late:
            kit.kept_row = sb(late, "kept_row", [P, (SG + 2) * TG], I32)
            with ExitStack() as middle:
                kit.base = sb(middle, "base", [P, NT, D])
                kit.wts = sb(middle, "wts", [P, NT])
                combine(nc, kit)
                choose(nc, kit)
            ffn(nc, kit)


def tile_rows(a, g, tiles=TG):
    return a[bass.ds(g * (TG * P), tiles * P), :].rearrange("(t p) d -> p t d", p=P)


def clear(sp, kit, t, z):
    rows = P * CLEAR_ROWS
    sp.dma_start(kit.tables[t][z * rows:(z + 1) * rows, :].rearrange("(p r) d -> p (r d)", r=CLEAR_ROWS),
                 kit.zero[:]).then_inc(kit.table_cleared[t], 16)


def prepare(nc, kit):
    src, dst, wgt, edges, window_row, flag = kit.src, kit.dst, kit.wgt, kit.edges, kit.window_row, kit.flag
    sem, sb = kit.sem, kit.sb
    N, D, Q, OVER, KD = kit.N, kit.D, kit.Q, kit.OVER, kit.KD
    ident, col = kit.ident, kit.col
    consts_ready, weights_loaded = kit.consts_ready, kit.weights_loaded
    E1 = RUN_EDGES
    with ExitStack() as c:
        src_i = sb(c, "src_i", [Q, STEP_RUNS, E1], I32)
        dst_i = sb(c, "dst_i", [Q, STEP_RUNS, E1], I32)
        lists = [sb(c, n, [Q, STEP_RUNS, E1]) for n in ("src_f", "rel_f", "wgt_f", "dst_f")]
        src_f, rel_f, wgt_f, dst_f = lists
        fields = (SRC, REL, WGT, DST)
        lo = sb(c, "lo", [Q, STEP_RUNS])
        hi = sb(c, "hi", [Q, STEP_RUNS])
        spread = sb(c, "spread", [Q, STEP_RUNS])
        first = sb(c, "first", [Q, STEP_RUNS])
        wide = sb(c, "wide", [Q, STEP_RUNS])
        wide_row = sb(c, "wide_row", [1, STEP_RUNS, Q])
        any_wide = sb(c, "any_wide", [1, 1])
        spare = sb(c, "spare", [P, 1])
        w1_sb = sb(c, "w1_sb", [P, KD, kit.H])
        w2_sb = sb(c, "w2_sb", [P, kit.KH, D])
        BANKS = 4
        turn_ps = [c.enter_context(nc.psum_tensor(f"turn_ps{i}", [P, 4, P], F32)) for i in range(BANKS)]

        src_loaded = sem("src_loaded")
        dst_loaded = sem("dst_loaded")
        wgt_loaded = sem("wgt_loaded")
        lists_ready = sem("lists_ready")
        rel_ready = sem("rel_ready")
        turned = sem("turned")
        turn_copied = sem("turn_copied")
        meta_turned = sem("meta_turned")
        meta_read = sem("meta_read")
        split_step = sem("split_step")
        dve_step = sem("prepare_dve_step")
        NTURN = len(lists) * STEP_RUNS * (CH // 4)
        LIST_DMAS = 4

        block = c.enter_context(nc.Block())

        @block.gpsimd
        def _(pool):
            build_constants(nc, kit)
            pool.wait_ge(weights_loaded, 16 * WEIGHTS)
            for n, (w, parts) in enumerate(((w1_sb, kit.w1_parts), (w2_sb, kit.w2_parts))):
                nc.gpsimd.tensor_copy(parts[:, 0, :, :], w[:]).then_inc(split_step, 1)
                pool.wait_ge(split_step, n + 1)
                nc.gpsimd.tensor_tensor(parts[:, 1, :, :], w[:], parts[:, 0, :, :].bitcast(F32), ALU.subtract)

        @block.sync
        def _(sp):
            for a, t, loaded in ((dst, dst_i, dst_loaded), (src, src_i, src_loaded), (wgt, wgt_f, wgt_loaded)):
                sp.dma_start(t[0:1, 0, :], a[0:E1].rearrange("(o e) -> o e", o=1)).then_inc(loaded, 16)
                sp.dma_start(t[0:1, 1, :], a[E1 - OVER:2 * E1 - OVER].rearrange("(o e) -> o e", o=1)).then_inc(loaded, 16)
                for q0, q1 in ((1, 8), (8, Q)):
                    sp.dma_start(t[q0:q1, :, :], a[q0 * STEP_RUNS * E1 - OVER:q1 * STEP_RUNS * E1 - OVER]
                                 .rearrange("(q g e) -> q g e", g=STEP_RUNS, e=E1)).then_inc(loaded, 16)
            sp.wait_ge(consts_ready, CONSTS)
            for z in range(kit.CLEARS):
                clear(sp, kit, 0, z)

        @block.scalar
        def _(act):
            for a, t in ((kit.w1.rearrange("(k p) n -> p k n", p=P), w1_sb),
                         (kit.w2.rearrange("(k p) n -> p k n", p=P), w2_sb),
                         (kit.W.rearrange("(k p) n -> p k n", p=P), kit.W_sb),
                         (kit.b2.partition_broadcast(P), kit.b2_sb),
                         (kit.wr.rearrange("n o -> (n o)").partition_broadcast(P), kit.wr_sb),
                         (kit.br.partition_broadcast(P), kit.br_sb),
                         (kit.bias.partition_broadcast(P), kit.bias_sb)):
                act.dma_start(t[:], a).then_inc(weights_loaded, 16)
            with nc.allow_non_contiguous_dma(reason="the bias of the first product, once"):
                act.dma_start(kit.b1_sb[:], kit.b1.rearrange("(c p) -> p c", p=P)).then_inc(weights_loaded, 16)
            for n in range(NTURN):
                f, g, half = n // (STEP_RUNS * 2), n // 2 % STEP_RUNS, n % 2
                act.wait_ge(turned, n + 1)
                act.activation(edges[:, 0:Q, g, fields[f], 4 * half:4 * half + 4],
                               turn_ps[n % BANKS][:, :, 0:Q].rearrange("p k q -> p q k"), ACT.Copy).then_inc(turn_copied, 1)

        @block.vector
        def _(dve):
            st = Steps(dve, dve_step)
            vec = nc.vector
            vec.memset(edges[:, Q, :, :, :], 0.0)
            vec.memset(window_row[0:1, Q:Q + 1, :], 0)
            dve.wait_ge(dst_loaded, 16 * LIST_DMAS)
            st.wait(vec.tensor_copy(dst_f[:], dst_i[:]))
            vec.tensor_reduce(lo[:], dst_f[:], op=ALU.min, axis=AX.X)
            st.wait(vec.tensor_reduce(hi[:], dst_f[:], op=ALU.max, axis=AX.X))
            st.wait(vec.tensor_scalar(first[:], lo[:], float(N - P), None, ALU.min))
            st.wait(vec.tensor_tensor(spread[:], hi[:], first[:], ALU.subtract))
            vec.tensor_scalar(wide[:], spread[:], float(P), None, ALU.is_ge).then_inc(lists_ready, 1)
            for g in range(STEP_RUNS):
                last = vec.tensor_scalar(rel_f[:, g, :], dst_f[:, g, :], first[:, g:g + 1], None, ALU.subtract)
            last.then_inc(rel_ready, 1)
            dve.wait_ge(src_loaded, 16 * LIST_DMAS)
            vec.tensor_copy(src_f[:], src_i[:]).then_inc(rel_ready, 1)
            dve.wait_ge(wgt_loaded, 16 * LIST_DMAS)
            vec.memset(wgt_f[0:1, 0, E1 - OVER:E1], 0.0).then_inc(rel_ready, 1)
            dve.wait_ge(meta_turned, 1)
            vec.tensor_copy(window_row[0:1, 0:Q, :].rearrange("o q g -> o g q"), turn_ps[0][0:1, 0:STEP_RUNS, 0:Q])
            vec.tensor_copy(wide_row[:], turn_ps[1][0:1, 0:STEP_RUNS, 0:Q]).then_inc(meta_read, 1)
            dve.wait_ge(meta_read, 1)
            st.wait(vec.tensor_reduce(any_wide[:], wide_row[:].rearrange("o g q -> o (g q)"), op=ALU.max, axis=AX.X))
            vec.tensor_copy(flag[:], any_wide[:])
            dve.wait_ge(consts_ready, CONSTS)
            st.wait(vec.tensor_scalar(spare[:], col[:], float(N), None, ALU.add))
            dve.wait_ge(turn_copied, NTURN)
            for g in range(STEP_RUNS):
                vec.tensor_scalar(edges[:, 0:Q, g, SPARE, :], edges[:, 0:Q, g, SRC, :], -1.0, spare[:], ALU.mult, ALU.add)

        @block.tensor
        def _(pe):
            t = nc.tensor
            pe.wait_ge(consts_ready, CONSTS)
            pe.wait_ge(lists_ready, 1)
            for g in range(STEP_RUNS):
                t.transpose(turn_ps[0][0:1, g, 0:Q], first[:, g:g + 1], ident[0:Q, 0:Q])
                last = t.transpose(turn_ps[1][0:1, g, 0:Q], wide[:, g:g + 1], ident[0:Q, 0:Q])
            last.then_inc(meta_turned, 1)
            pe.wait_ge(rel_ready, 3)
            pe.wait_ge(meta_read, 1)
            for n in range(NTURN):
                f, g, half = n // (STEP_RUNS * 2), n // 2 % STEP_RUNS, n % 2
                wait_if(pe, turn_copied, n + 1 - BANKS)
                for k in range(4):
                    e0 = (4 * half + k) * P
                    last = t.transpose(turn_ps[n % BANKS][:, k, 0:Q], lists[f][:, g, e0:e0 + P], ident[0:Q, 0:Q])
                last.then_inc(turned, 1)


def edge_sums(nc, kit):
    x, edges, window_row, flag, sem, sb = kit.x, kit.edges, kit.window_row, kit.flag, kit.sem, kit.sb
    tables, table_cleared, table_added = kit.tables, kit.table_cleared, kit.table_added
    N, D, Q, BATCHES, CLEARS = kit.N, kit.D, kit.Q, kit.BATCHES, kit.CLEARS
    ident, lower, row = kit.ident, kit.lower, kit.row
    RUN_BATCHES = CH // BATCH
    with ExitStack() as c:
        def ps(name, shape):
            return c.enter_context(nc.psum_tensor(name, shape, F32))

        cur = sb(c, "cur", [P, STEP_RUNS, NFIELD, CH])
        same = sb(c, "same", [P, 2, BATCH, P])
        earlier = sb(c, "earlier", [P, BATCH, P])
        dups = sb(c, "dups", [P, BATCH])
        moved = sb(c, "moved", [P, BATCH])
        pick = sb(c, "pick", [P, 2, BATCH, P])
        mix_sb = sb(c, "mix_sb", [P, 2, BATCH, P])
        raw = sb(c, "raw", [P, STEP_RUNS, D])
        window = sb(c, "window", [P, STEP_RUNS, D])
        stats = sb(c, "stats", [P, BATCH, 6])
        mv = sb(c, "mv", [P, BATCH, 2])
        std = sb(c, "std", [P, BATCH])
        gathered = sb(c, "gathered", [P, STEP_RUNS, CH, D])
        target = sb(c, "target", [P, STEP_RUNS, CH], I32)
        put_row = sb(c, "put_row", [P, STEP_RUNS * CH], I32)
        msg = sb(c, "msg", [P, 2 * BATCH, D])
        src_ps = [ps(f"src_ps{i}", [P, BATCH, P]) for i in range(2)]
        mix_ps = [ps(f"mix_ps{i}", [P, BATCH, P]) for i in range(2)]
        msg_ps = [ps(f"msg_ps{i}", [P, 2, D]) for i in range(4)]

        cur_ready = sem("cur_ready")
        src_turned = sem("src_turned")
        picked = sem("picked")
        rows_ready = sem("rows_ready")
        mix_done = sem("mix_done")
        mix_copied = sem("mix_copied")
        msg_done = sem("msg_done")
        msg_copied = sem("msg_copied")
        window_loaded = [sem(f"window_loaded{i}") for i in range(STEP_RUNS)]
        target_ready = sem("target_ready")
        window_ready = sem("window_ready")
        mv_ready = sem("mv_ready")
        std_ready = sem("std_ready")
        rows_gathered = [sem(f"rows_gathered{i}") for i in range(STEP_RUNS)]
        edge_step = sem("edge_dve_step")

        block = c.enter_context(nc.Block())

        def steps(engine, body, first=0):
            for q in range(first, EARLY + 1):
                body(q)
            with engine.Fori(EARLY + 1, Q) as q:
                body(q)

        def place(t, j):
            if isinstance(t, int) and t < EARLY * BATCHES:
                return j % (TABLES // 2), 2 * t + j // (TABLES // 2)
            return j, t + (EARLY * BATCHES if j < TABLES // 2 else -EARLY * BATCHES)

        def wait_added(engine, t, j):
            table, adds = place(t, j)
            engine.wait_ge(table_added[table], 16 * (adds + 1))

        def vector_body(dve, general):
            vec = nc.vector
            st = Steps(dve, edge_step)

            def window_stats(q, g):
                dve.wait_ge(window_loaded[g], 16 * (q + 1))
                return vec.bn_stats(stats[:, 0, :], raw[:, g, :])

            def window_norm(q, g):
                wait_if(dve, msg_done, 2 * RUN_BATCHES * (STEP_RUNS * q + g - 1))
                vec.tensor_scalar(window[:, g, :], raw[:, g, :], mv[:, 0, 0:1], std[:, 0:1],
                                  ALU.subtract, ALU.mult).then_inc(window_ready, 1)

            def norm_gathered(q, g, hb):
                t = RUN_BATCHES * (STEP_RUNS * q + g) + hb
                if hb == 0:
                    dve.wait_ge(rows_gathered[g], 16 * CH * (q + 1))
                rows = gathered[:, g, hb * BATCH:(hb + 1) * BATCH, :]
                for k in range(BATCH):
                    last = vec.bn_stats(stats[:, k, :], rows[:, k, :])
                st.wait(last)
                hold(kit, dve)
                for k in range(BATCH):
                    last = vec.bn_aggr(mv[:, k, :], stats[:, k, :])
                last.then_inc(mv_ready, 1)
                dve.wait_ge(std_ready, t + 1)
                st.wait(vec.reciprocal(std[:], std[:]))
                for k in range(BATCH):
                    last = vec.tensor_scalar(rows[:, k, :], rows[:, k, :], mv[:, k, 0:1], std[:, k:k + 1],
                                             ALU.subtract, ALU.mult)
                last.then_inc(window_ready, 1)

            def body(q):
                for g in range(STEP_RUNS):
                    dve.wait_ge(cur_ready, STEP_RUNS * q + g + 1)
                    nq, ng = (q, 1) if g == 0 else (q + 1, 0)
                    if general:
                        wait_if(dve, rows_gathered[g], 16 * CH * q)
                        vec.tensor_copy(target[:, g, :], cur[:, g, DST, :]).then_inc(target_ready, 1)
                    for hb in range(RUN_BATCHES):
                        t = BATCHES * q + RUN_BATCHES * g + hb
                        r = hb % 2
                        if general:
                            norm_gathered(q, g, hb)
                        k0 = hb * BATCH
                        dve.wait_ge(src_turned, t + 1)
                        if not general:
                            wait_if(dve, mix_done, t - 1)
                        s4 = cur[:, g, SRC, k0:k0 + BATCH]
                        vec.tensor_tensor(same[:, r, :, :], src_ps[r][:],
                                          s4.unsqueeze(2).to_broadcast([P, BATCH, P]), ALU.is_equal)
                        for k in range(BATCH):
                            last = vec.scalar_tensor_tensor(out=earlier[:, k, :], in0=src_ps[r][:, k, :],
                                                            scalar=cur[:, g, SRC, k0 + k:k0 + k + 1], in1=lower[:],
                                                            op0=ALU.is_equal, op1=ALU.mult, accum_out=dups[:, k:k + 1])
                        if not general and hb == 0:
                            dve.wait_ge(std_ready, STEP_RUNS * q + g + 1)
                            last = vec.reciprocal(std[:, 0:1], std[:, 0:1])
                        if not general and hb == 1:
                            last = window_stats(nq, ng)
                        st.wait(last)
                        moved_ready = vec.scalar_tensor_tensor(out=moved[:], in0=dups[:], scalar=1.0,
                                                               in1=cur[:, g, SPARE, k0:k0 + BATCH], op0=ALU.min, op1=ALU.mult)
                        if not general and hb == 0:
                            window_norm(q, g)
                        if not general and hb == 1:
                            hold(kit, dve)
                            vec.bn_aggr(mv[:, 0, :], stats[:, 0, :]).then_inc(mv_ready, 1)
                        st.wait(moved_ready)
                        slot = g * CH + k0
                        for j in range(BATCH):
                            if not is_zero(q):
                                wait_added(dve, t - BATCHES, j)
                        vec.tensor_tensor(put_row[:, slot:slot + BATCH], moved[:], s4, ALU.add).then_inc(rows_ready, 1)
                        if general:
                            wait_if(dve, msg_done, 2 * t - 2)
                        for k in range(BATCH):
                            last = vec.tensor_scalar(
                                pick[:, r, k, :], src_ps[r][:, k, :] if general else row[:],
                                cur[:, g, SRC if general else REL, k0 + k:k0 + k + 1],
                                cur[:, g, WGT, k0 + k:k0 + k + 1], ALU.is_equal, ALU.mult)
                        last.then_inc(picked, 1)
                        if not general and hb == 0:
                            dve.wait_ge(window_ready, STEP_RUNS * q + g + 1)

            a_step = (4 if general else 2) * BATCHES
            if not general:
                st.wait(window_stats(0, 0))
                vec.bn_aggr(mv[:, 0, :], stats[:, 0, :]).then_inc(mv_ready, 1)
            first = st.k
            for q in range(EARLY + 1):
                body(q)
                assert st.k == first + (q + 1) * a_step
            with dve.Fori(EARLY + 1, Q) as q:
                st.rebase(first + q * a_step)
                body(q)

        @block.vector
        def _(dve):
            wide = dve.value_load(flag[0:1, 0:1], min_val=0, max_val=1)
            with dve.If(wide):
                vector_body(dve, True)
            with dve.Else():
                vector_body(dve, False)

        def tensor_body(pe, general):
            t_ = nc.tensor

            def sources(q, bt):
                t, g, hb = BATCHES * q + bt, bt // RUN_BATCHES, bt % RUN_BATCHES
                pe.wait_ge(cur_ready, STEP_RUNS * q + g + 1)
                wait_if(pe, picked, t - 1)
                for k in range(BATCH):
                    col_ap = cur[:, g, SRC, hb * BATCH + k:hb * BATCH + k + 1]
                    last = t_.transpose(src_ps[bt % 2][:, k, :], col_ap.to_broadcast([P, P]), ident[:])
                last.then_inc(src_turned, 1)

            def mix(t, bt):
                pe.wait_ge(picked, t + 1)
                wait_if(pe, mix_copied, t - 1)
                for k in range(BATCH):
                    last = t_.matmul(mix_ps[bt % 2][:, k, :], lhsT=pick[:, bt % 2, k, :], rhs=same[:, bt % 2, k, :],
                                     start=True, stop=True)
                last.then_inc(mix_done, 1)

            def message(t, q, bt):
                g, hb = bt // RUN_BATCHES, bt % RUN_BATCHES
                if general:
                    pe.wait_ge(picked, t + 1)
                    pe.wait_ge(window_ready, t + 1)
                else:
                    pe.wait_ge(mix_copied, t + 1)
                    pe.wait_ge(window_ready, STEP_RUNS * q + g + 1)
                for half in range(2):
                    wait_if(pe, msg_copied, 2 * t + half - 3)
                    for k in range(2):
                        kk = 2 * half + k
                        last = t_.matmul(msg_ps[(2 * bt + half) % 4][:, k, :],
                                         lhsT=pick[:, bt % 2, kk, :] if general else mix_sb[:, bt % 2, kk, :],
                                         rhs=gathered[:, g, hb * BATCH + kk, :] if general else window[:, g, :],
                                         start=True, stop=True)
                    last.then_inc(msg_done, 1)

            def body(q):
                first = is_zero(q)
                for bt in range(BATCHES):
                    t = BATCHES * q + bt
                    sources(q, bt)
                    if general:
                        if not (first and bt < 1):
                            message(t - 1, q if bt >= 1 else q - 1, (bt - 1) % BATCHES)
                        continue
                    if not (first and bt < 1):
                        mix(t - 1, (bt - 1) % BATCHES)
                    if not (first and bt < 2):
                        message(t - 2, q if bt >= 2 else q - 1, (bt - 2) % BATCHES)

            steps(pe, body)
            end = BATCHES * Q
            if general:
                message(end - 1, Q - 1, BATCHES - 1)
            else:
                mix(end - 1, BATCHES - 1)
                message(end - 2, Q - 1, BATCHES - 2)
                message(end - 1, Q - 1, BATCHES - 1)

        @block.tensor
        def _(pe):
            wide = pe.value_load(flag[0:1, 0:1], min_val=0, max_val=1)
            with pe.If(wide):
                tensor_body(pe, True)
            with pe.Else():
                tensor_body(pe, False)

        def scalar_body(act, general):
            def mix_copy(t, bt):
                act.wait_ge(mix_done, t + 1)
                wait_if(act, msg_done, 2 * t - 2)
                act.activation(mix_sb[:, bt % 2, :, :], mix_ps[bt % 2][:], ACT.Copy).then_inc(mix_copied, 1)

            def msg_copy(t, bt):
                for half in range(2):
                    act.wait_ge(msg_done, 2 * t + half + 1)
                    if not (isinstance(t, int) and t < 2):
                        for j in (2 * half, 2 * half + 1):
                            wait_added(act, t - 2, j)
                    k0 = (bt % 2) * BATCH + 2 * half
                    act.activation(msg[:, k0:k0 + 2, :], msg_ps[(2 * bt + half) % 4][:], ACT.Copy).then_inc(msg_copied, 1)

            def next_fields(q, g):
                wait_if(act, picked, RUN_BATCHES * (STEP_RUNS * q + g))
                wait_if(act, rows_ready, RUN_BATCHES * (STEP_RUNS * q + g))
                nq, ng = (q, 1) if g == 0 else (q + 1, 0)
                act.activation(cur[:, ng, :, :], edges[:, bass.ds(nq, 1), ng, :, :]
                               .rearrange("p o f k -> p (o f) k"), ACT.Copy).then_inc(cur_ready, 1)

            def root(n, k):
                act.wait_ge(mv_ready, n + 1)
                act.activation(std[:, 0:k], mv[:, 0:k, 1], ACT.Sqrt, bias=kit.eps[:]).then_inc(std_ready, 1)

            def body(q):
                first = is_zero(q)
                for bt in range(BATCHES):
                    t = BATCHES * q + bt
                    if bt % RUN_BATCHES == 0:
                        next_fields(q, bt // RUN_BATCHES)
                    if general:
                        root(t, BATCH)
                        msg_copy(t, bt)
                        continue
                    if bt % RUN_BATCHES == 1:
                        root(STEP_RUNS * q + bt // RUN_BATCHES + 1, 1)
                    mix_copy(t, bt)
                    if not (first and bt < 1):
                        msg_copy(t - 1, (bt - 1) % BATCHES)

            act.activation(cur[:, 0, :, :], edges[:, 0, 0, :, :], ACT.Copy).then_inc(cur_ready, 1)
            if not general:
                root(0, 1)
            steps(act, body)
            if not general:
                msg_copy(BATCHES * Q - 1, BATCHES - 1)

        @block.scalar
        def _(act):
            wide = act.value_load(flag[0:1, 0:1], min_val=0, max_val=1)
            with act.If(wide):
                scalar_body(act, True)
            with act.Else():
                scalar_body(act, False)

        @block.sync
        def _(sp):
            def clear_second():
                for t in range(1, TABLES // 2):
                    for z in range(CLEARS):
                        clear(sp, kit, t, z)

            def clear_rest(first, end):
                for z in range(first, end):
                    for t in range(TABLES // 2, TABLES):
                        wait_if(sp, table_cleared[t], 16 * z)
                        clear(sp, kit, t, z)

            wide = sp.value_load(flag[0:1, 0:1], min_val=0, max_val=1)
            with sp.If(wide):
                clear_second()
                clear_rest(0, CLEARS)
            with sp.Else():
                def load_window(q, g):
                    wait_if(sp, window_ready, STEP_RUNS * (q - 1) + g + 1)
                    r0 = sp.value_load(window_row[0:1, bass.ds(q, 1), g], min_val=0, max_val=N - P)
                    sp.dma_start(raw[:, g, :], x[bass.ds(r0, P), :]).then_inc(window_loaded[g], 16)

                def body(q):
                    load_window(q, 1)
                    load_window(q + 1, 0)

                load_window(0, 0)
                load_window(0, 1)
                clear_second()
                load_window(1, 0)
                clear_rest(0, CLEARS // 2)
                load_window(1, 1)
                clear_rest(CLEARS // 2, CLEARS)
                load_window(2, 0)
                steps(sp, body, 2)

        def add_to_table(pool, q, bt):
            t = BATCHES * q + bt
            pool.wait_ge(rows_ready, t + 1)
            for j in range(BATCH):
                if j % 2 == 0:
                    pool.wait_ge(msg_copied, 2 * t + j // 2 + 1)
                table, adds = place(t, j)
                if is_zero(adds):
                    pool.wait_ge(table_cleared[table], 16 * CLEARS)
                wait_if(pool, table_added[table], 16 * adds)
                slot = bt * BATCH + j
                hold(kit, pool)
                pool.indirect_dma_start(
                    out=tables[table], out_offset=bass.IndirectOffsetOnAxis(ap=put_row[:, slot:slot + 1], axis=0),
                    in_=msg[:, (bt % 2) * BATCH + j, :], in_offset=None,
                    compute_op=ALU.add).then_inc(table_added[table], 16)

        def gather_rows(pool, q, g):
            pool.wait_ge(target_ready, STEP_RUNS * q + g + 1)
            wait_if(pool, msg_done, 2 * RUN_BATCHES * (STEP_RUNS * (q - 1) + g + 1))
            for k in range(CH):
                hold(kit, pool)
                pool.indirect_dma_start(
                    out=gathered[:, g, k, :], out_offset=None, in_=x,
                    in_offset=bass.IndirectOffsetOnAxis(ap=target[:, g, k:k + 1], axis=0)).then_inc(rows_gathered[g], 16)

        @block.gpsimd
        def _(pool):
            wide = pool.value_load(flag[0:1, 0:1], min_val=0, max_val=1)
            with pool.If(wide):
                def general_body(q):
                    for g in range(STEP_RUNS):
                        gather_rows(pool, q, g)
                        for hb in range(RUN_BATCHES):
                            if g == 0 and not is_zero(q):
                                add_to_table(pool, q - 1, (STEP_RUNS - 1) * RUN_BATCHES + hb)
                            elif g > 0:
                                add_to_table(pool, q, (g - 1) * RUN_BATCHES + hb)

                steps(pool, general_body)
                for hb in range(RUN_BATCHES):
                    add_to_table(pool, Q - 1, (STEP_RUNS - 1) * RUN_BATCHES + hb)
            with pool.Else():
                def body(q):
                    for bt in range(BATCHES):
                        add_to_table(pool, q, bt)

                steps(pool, body)
            for j in range(BATCH):
                wait_added(pool, (Q - 1) * BATCHES + BATCHES - 1, j)


def combine(nc, kit):
    x, xn_dram, tables, sem, sb, base = kit.x, kit.xn_dram, kit.tables, kit.sem, kit.sb, kit.base
    wts, wr_sb = kit.wts, kit.wr_sb
    br_sb, bias_sb = kit.br_sb, kit.bias_sb
    N, D, GROUPS, TAIL, LAST, NT = kit.N, kit.D, kit.GROUPS, kit.TAIL, kit.LAST, kit.NT
    KD, W_sb = kit.KD, kit.W_sb
    ident = kit.ident
    with ExitStack() as c:
        parts = sb(c, "parts", [P, 2, TABLES, TG, D])
        xb = sb(c, "xb", [P, 2, TG, D])
        x1 = sb(c, "x1", [P, 2, TG, D])
        xn = sb(c, "xn1", [P, 2, TG, D])
        stats = sb(c, "stats1", [P, TG, 6])
        mv = sb(c, "mv1", [P, 2, TG, 2])
        std = sb(c, "std1", [P, 2, TG])
        junk = sb(c, "junk", [P, TG, D])
        wcur = sb(c, "wcur", [P, TG])
        aggT = sb(c, "aggT", [P, 2, KD, TG * P])
        aggT_ps = [c.enter_context(nc.psum_tensor(f"aggT_ps{i}", [P, KD, TG * P], F32)) for i in range(2)]
        sum_ps = [c.enter_context(nc.psum_tensor(f"sum_ps{i}", [P, TG, D], F32)) for i in range(2)]
        parts_loaded = [sem(f"parts_loaded{i}") for i in range(2)]
        x_loaded = [sem(f"x1_loaded{i}") for i in range(2)]
        sums_turned = sem("sums_turned")
        bias_added = sem("bias_added")
        pair_added = sem("pair_added")
        sums_ready = sem("sums_ready")
        PAIRS_OF_GROUPS = GROUPS // 2
        aggT_copied = sem("aggT_copied")
        product_done = sem("product_done")
        x1_ready = sem("x1_ready")
        xn_ready = sem("xn_ready")
        base_ready = sem("base_ready")
        xn_stored = [sem(f"xn_stored{i}") for i in range(2)]
        step = sem("combine_dve_step")
        mv_ready = sem("mv1_ready")
        std_ready = sem("std1_ready")
        block = c.enter_context(nc.Block())

        @block.sync
        def _(sp):
            def load_parts(i, b, tiles=TG):
                wait_if(sp, sums_turned, 2 * i + b - 1)
                for j in range(TABLES):
                    sp.dma_start(parts[:, b, j, 0:tiles, :], tile_rows(tables[j], 2 * i + b, tiles)).then_inc(parts_loaded[b], 16)

            def load_x(i, b, tiles=TG):
                wait_if(sp, x1_ready, 2 * i + b - 1)
                if tiles == TG:
                    sp.dma_start(xb[:, b, :, :], tile_rows(x, 2 * i + b)).then_inc(x_loaded[b], 16)
                else:
                    n0 = GROUPS * TG * P
                    sp.dma_start(xb[:, b, 0:tiles - 1, :], x[n0:n0 + (tiles - 1) * P, :]
                                 .rearrange("(t p) d -> p t d", p=P)).then_inc(x_loaded[b], 16)
                    sp.dma_start(xb[0:LAST, b, tiles - 1, :], x[N - LAST:N, :]).then_inc(x_loaded[b], 16)

            def body(i):
                load_parts(i + 1, 0)
                load_x(i, 1)
                load_parts(i + 1, 1)
                load_x(i + 1, 0)

            load_parts(0, 0)
            load_x(0, 0)
            load_parts(0, 1)
            body(0)
            with sp.Fori(1, PAIRS_OF_GROUPS - 1) as i:
                body(i)
            load_parts(PAIRS_OF_GROUPS, 0, TAIL)
            load_x(PAIRS_OF_GROUPS - 1, 1)
            load_x(PAIRS_OF_GROUPS, 0, TAIL)

        @block.tensor
        def _(pe):
            def turn_sums(i, b, tiles=TG):
                g = 2 * i + b
                pe.wait_ge(sums_ready, g + 1)
                wait_if(pe, aggT_copied, g - 1)
                for t in range(tiles):
                    for k in range(KD):
                        last = nc.tensor.transpose(aggT_ps[b][:, k, t * P:(t + 1) * P], parts[:, b, 0, t, k * P:(k + 1) * P],
                                                   ident[:])
                last.then_inc(sums_turned, 1)

            def product(i, b, tiles=TG):
                g = 2 * i + b
                pe.wait_ge(aggT_copied, g + 1)
                wait_if(pe, x1_ready, g - 1)
                for t in range(tiles):
                    for k in range(KD):
                        last = nc.tensor.matmul(sum_ps[b][:, t, :], lhsT=aggT[:, b, k, t * P:(t + 1) * P], rhs=W_sb[:, k, :],
                                                start=(k == 0), stop=(k == KD - 1))
                last.then_inc(product_done, 1)

            turn_sums(0, 0)
            turn_sums(0, 1)
            product(0, 0)
            with pe.Fori(1, GROUPS // 2) as i:
                turn_sums(i, 0)
                product(i - 1, 1)
                turn_sums(i, 1)
                product(i, 0)
            turn_sums(GROUPS // 2, 0, TAIL)
            product(GROUPS // 2 - 1, 1)
            product(GROUPS // 2, 0, TAIL)

        @block.scalar
        def _(act):
            def root(i, b, tiles=TG):
                act.wait_ge(mv_ready, 2 * i + b + 1)
                act.activation(std[:, b, 0:tiles], mv[:, b, 0:tiles, 1], ACT.Sqrt, bias=kit.eps[:]).then_inc(std_ready, 1)

            def store(i, b, tiles=TG):
                act.wait_ge(xn_ready, 2 * i + b + 1)
                act.dma_start(tile_rows(xn_dram, 2 * i + b, tiles), xn[:, b, 0:tiles, :]).then_inc(xn_stored[b], 16)

            def aggT_copy(i, b, tiles=TG):
                g = 2 * i + b
                act.wait_ge(sums_turned, g + 1)
                wait_if(act, product_done, g - 1)
                act.activation(aggT[:, b, :, 0:tiles * P], aggT_ps[b][:, :, 0:tiles * P], ACT.Copy).then_inc(aggT_copied, 1)

            def body(i):
                aggT_copy(i, 1)
                root(i, 0)
                if not isinstance(i, int):
                    store(i - 1, 1)
                aggT_copy(i + 1, 0)
                root(i, 1)
                store(i, 0)

            aggT_copy(0, 0)
            body(0)
            with act.Fori(1, PAIRS_OF_GROUPS - 1) as i:
                body(i)
            last = PAIRS_OF_GROUPS - 1
            aggT_copy(last, 1)
            root(last, 0)
            store(last - 1, 1)
            aggT_copy(last + 1, 0, TAIL)
            root(last, 1)
            store(last, 0)
            root(last + 1, 0, TAIL)
            store(last, 1)
            store(last + 1, 0, TAIL)
            act.wait_ge(xn_stored[0], 16 * (GROUPS // 2 + 1))
            act.wait_ge(xn_stored[1], 16 * (GROUPS // 2))

        @block.gpsimd
        def _(pool):
            def add_pair(i, b, tiles=TG):
                pool.wait_ge(parts_loaded[b], 16 * TABLES * (i + 1))
                nc.gpsimd.tensor_tensor(parts[:, b, 2, 0:tiles, :], parts[:, b, 2, 0:tiles, :], parts[:, b, 3, 0:tiles, :],
                                        ALU.add).then_inc(pair_added, 1)

            def add_bias(i, b, tiles=TG):
                pool.wait_ge(x_loaded[b], 16 * (i + 1) + (0 if tiles == TG else 16))
                nc.gpsimd.tensor_tensor(xb[:, b, 0:tiles, :], xb[:, b, 0:tiles, :],
                                        bias_sb[:].unsqueeze(1).to_broadcast([P, tiles, D]), ALU.add).then_inc(bias_added, 1)

            def keep_base(i, b, tiles=TG):
                g = 2 * i + b
                pool.wait_ge(xn_ready, g + 1)
                nc.gpsimd.tensor_tensor(base[:, bass.ds(g * TG, tiles), :], x1[:, b, 0:tiles, :], xn[:, b, 0:tiles, :],
                                        ALU.add).then_inc(base_ready, 1)

            pool.wait_ge(kit.weights_loaded, 16 * WEIGHTS)
            add_pair(0, 0)
            add_bias(0, 0)
            add_pair(0, 1)

            def body(i):
                add_pair(i + 1, 0)
                if not isinstance(i, int):
                    keep_base(i - 1, 0)
                add_bias(i, 1)
                add_pair(i + 1, 1)
                if not isinstance(i, int):
                    keep_base(i - 1, 1)
                add_bias(i + 1, 0)

            body(0)
            with pool.Fori(1, PAIRS_OF_GROUPS - 1) as i:
                body(i)
            last = PAIRS_OF_GROUPS - 1
            add_pair(last + 1, 0, TAIL)
            keep_base(last - 1, 0)
            add_bias(last, 1)
            keep_base(last - 1, 1)
            add_bias(last + 1, 0, TAIL)
            keep_base(last, 0)
            keep_base(last, 1)
            keep_base(last + 1, 0, TAIL)

        @block.vector
        def _(dve):
            vec = nc.vector
            st = Steps(dve, step)
            dve.wait_ge(kit.weights_loaded, 16 * WEIGHTS)
            vec.memset(wts[:], float("-inf"))

            def add_parts(i, b, tiles=TG):
                g = 2 * i + b
                dve.wait_ge(parts_loaded[b], 16 * TABLES * (i + 1))
                part = parts[:, b, :, 0:tiles, :]
                st.wait(vec.tensor_tensor(part[:, 0], part[:, 0], part[:, 1], ALU.add))
                dve.wait_ge(pair_added, g + 1)
                vec.tensor_tensor(part[:, 0], part[:, 0], part[:, 2], ALU.add).then_inc(sums_ready, 1)

            def statistics(i, b, tiles=TG):
                g = 2 * i + b
                dve.wait_ge(product_done, g + 1)
                dve.wait_ge(bias_added, g + 1)
                wait_if(dve, base_ready, g - 1)
                vec.tensor_tensor(x1[:, b, 0:tiles, :], sum_ps[b][:, 0:tiles, :], xb[:, b, 0:tiles, :],
                                  ALU.add).then_inc(x1_ready, 1)
                dve.wait_ge(x1_ready, g + 1)
                for t in range(tiles):
                    last = vec.bn_stats(stats[:, t, :], x1[:, b, t, :])
                st.wait(last)
                hold(kit, dve)
                for t in range(tiles):
                    last = vec.bn_aggr(mv[:, b, t, :], stats[:, t, :])
                last.then_inc(mv_ready, 1)

            def normalise(i, b, tiles=TG):
                g = 2 * i + b
                dve.wait_ge(std_ready, g + 1)
                st.wait(vec.reciprocal(std[:, b, 0:tiles], std[:, b, 0:tiles]))
                wait_if(dve, xn_stored[b], 16 * i)
                for t in range(tiles):
                    last = vec.tensor_scalar(xn[:, b, t, :], x1[:, b, t, :], mv[:, b, t, 0:1], std[:, b, t:t + 1],
                                             ALU.subtract, ALU.mult)
                last.then_inc(xn_ready, 1)
                dve.wait_ge(xn_ready, g + 1)
                for t in range(tiles):
                    last = vec.tensor_tensor_reduce(out=junk[:, t, :], in0=xn[:, b, t, :], in1=wr_sb[:], scale=1.0, scalar=0.0,
                                                    op0=ALU.mult, op1=ALU.add, accum_out=wcur[:, t:t + 1])
                st.wait(last)
                if tiles == TG:
                    vec.tensor_scalar(wts[:, bass.ds(g * TG, TG)], wcur[:], br_sb[:], None, ALU.add)
                else:
                    vec.tensor_scalar(wts[:, NT - tiles:NT - 1], wcur[:, 0:tiles - 1], br_sb[:], None, ALU.add)
                    vec.tensor_scalar(wts[0:LAST, NT - 1:NT], wcur[0:LAST, tiles - 1:tiles], br_sb[0:LAST, :], None, ALU.add)

            def body(i):
                add_parts(i + 1, 0)
                statistics(i, 0)
                if not isinstance(i, int):
                    normalise(i - 1, 1)
                add_parts(i + 1, 1)
                statistics(i, 1)
                normalise(i, 0)

            add_parts(0, 0)
            add_parts(0, 1)
            body(0)
            first, a_step = st.k, 6 + 2
            with dve.Fori(1, PAIRS_OF_GROUPS - 1) as i:
                st.rebase(first + (i - 1) * a_step)
                body(i)
                assert st.k == a_step
            last_pair = PAIRS_OF_GROUPS - 1
            st.rebase(first + (last_pair - 1) * a_step)
            add_parts(last_pair + 1, 0, TAIL)
            statistics(last_pair, 0)
            normalise(last_pair - 1, 1)
            statistics(last_pair, 1)
            normalise(last_pair, 0)
            statistics(last_pair + 1, 0, TAIL)
            normalise(last_pair, 1)
            normalise(last_pair + 1, 0, TAIL)


def choose(nc, kit):
    out, sem, sb, base, wts, kept_row = kit.out, kit.sem, kit.sb, kit.base, kit.wts, kit.kept_row
    N, D, NT, LAST, KEPT, SLOTS = kit.N, kit.D, kit.NT, kit.LAST, kit.KEPT, kit.SLOTS
    before, ones, row, col = kit.before, kit.ones, kit.row, kit.col
    DIGITS, RADIX = 8, 4
    PART = 14
    assert NT % PART == 0
    with ExitStack() as c:
        def ps(name, shape):
            return c.enter_context(nc.psum_tensor(name, shape, F32))

        half_i = [sb(c, f"half_i{i}", [P, NT], I32) for i in range(2)]
        key = [sb(c, f"key{i}", [P, NT]) for i in range(2)]
        neg = sb(c, "neg", [P, NT])
        tmp = sb(c, "tmp", [P, NT])
        junk = sb(c, "junk2", [P, RADIX - 1, NT])
        cand = sb(c, "cand", [P, RADIX - 1])
        steps = sb(c, "steps", [P, RADIX - 1])
        found = [sb(c, f"found{i}", [P, 1]) for i in range(2)]
        unit = [sb(c, f"unit{i}", [P, 1]) for i in range(2)]
        digit = sb(c, "digit", [P, 1])
        reached = sb(c, "reached", [P, RADIX - 1])
        cnt = sb(c, "cnt", [P, RADIX - 1])
        tied_left = sb(c, "tied_left", [P, 1])
        above = sb(c, "above", [P, NT], BF16)
        tied = sb(c, "tied", [P, NT], BF16)
        chosen = sb(c, "chosen", [P, NT], BF16)
        ones_b = sb(c, "ones_b", [P, P], BF16)
        total_b = sb(c, "total_b", [NT, P], BF16)
        rank = sb(c, "rank", [P, NT])
        rank_i = sb(c, "rank_i", [P, NT], I32)
        part_i = [sb(c, f"part_i{i}", [P, NT], I32) for i in range(2)]
        part = [sb(c, f"part{i}", [P, NT], BF16) for i in range(2)]
        row_b = sb(c, "row_b", [P, P], BF16)
        in_slot = sb(c, "in_slot", [P, 2, PART, P], BF16)
        in_tile = sb(c, "in_tile", [P, 2, PART, SLOTS], BF16)
        number = sb(c, "number", [P, 2, PART, 2, SLOTS], BF16)
        number_f = sb(c, "number_f", [P, 2, SLOTS])
        tot_ps = ps("tot_ps", [P, RADIX - 1])
        all_ps = ps("all_ps", [P, NT])
        col_ps = ps("col_ps", [NT, 1])
        rank_ps = ps("rank_ps", [P, NT])
        num_ps = ps("num_ps", [P, 2, SLOTS])
        base_stored = sem("base_stored")
        step = sem("choose_dve_step")
        counted = sem("counted")
        totalled = sem("totalled")
        ready = sem("mask_ready")
        summed = sem("mask_summed")
        spread = sem("totals_spread")
        ranked = sem("ranked")
        hot = sem("hot_ready")
        packed = sem("packed")
        tile_placed = sem("tile_placed")
        place_ready = sem("place_ready")
        tile_numbered = sem("tile_numbered")
        block = c.enter_context(nc.Block())

        @block.sync
        def _(sp):
            sp.dma_start(out[0:N - LAST, :].rearrange("(t p) d -> p t d", p=P), base[:, 0:NT - 1, :]).then_inc(base_stored, 16)
            sp.dma_start(out[N - LAST:N, :], base[0:LAST, NT - 1, :]).then_inc(base_stored, 16)
            sp.wait_ge(base_stored, 32)

        @block.gpsimd
        def _(pool):
            for n in range(NT // PART):
                pool.wait_ge(tile_placed, n + 1)
                nc.gpsimd.tensor_scalar(number[:, n % 2, :, 1, :], in_tile[:, n % 2, :, :], col[:], None,
                                        ALU.mult).then_inc(place_ready, 1)

        @block.scalar
        def _(act):
            for n in range(NT // PART):
                act.wait_ge(tile_placed, n + 1)
                for j in range(PART):
                    last = act.activation(number[:, n % 2, j, 0, :], in_tile[:, n % 2, j, :], ACT.Copy,
                                          scale=float(n * PART + j))
                last.then_inc(tile_numbered, 1)

        @block.tensor
        def _(pe):
            t = nc.tensor

            with pe.Fori(0, 2 * DIGITS) as n:
                pe.wait_ge(counted, n + 1)
                t.matmul(tot_ps[:], lhsT=ones[:], rhs=cnt[:], start=True, stop=True).then_inc(totalled, 1)
            pe.wait_ge(ready, 1)
            t.matmul(all_ps[:], lhsT=ones_b[:], rhs=above[:], start=True, stop=True)
            for n, mask in enumerate((tied, chosen)):
                pe.wait_ge(ready, n + 1)
                t.matmul(col_ps[:], lhsT=mask[:], rhs=ones_b[:, 0:1], start=True, stop=True).then_inc(summed, 1)
                pe.wait_ge(spread, n + 1)
                t.matmul(rank_ps[:], lhsT=before[:], rhs=mask[:], start=True, stop=False)
                t.matmul(rank_ps[:], lhsT=total_b[:], rhs=before[0:NT, 0:NT], start=False, stop=True).then_inc(ranked, 1)
            for n in range(NT // PART):
                pe.wait_ge(hot, n + 1)
                pe.wait_ge(place_ready, n + 1)
                pe.wait_ge(tile_numbered, n + 1)
                for j in range(PART):
                    last = t.matmul(num_ps[:], lhsT=in_slot[:, n % 2, j, :], rhs=number[:, n % 2, j, :, :],
                                    start=(n == 0 and j == 0), stop=(n == NT // PART - 1 and j == PART - 1))
                last.then_inc(packed, 1)

        @block.vector
        def _(dve):
            vec = nc.vector
            st = Steps(dve, step)
            bits = wts[:].bitcast(I32)
            vec.memset(ones_b[:], 1.0)
            vec.tensor_scalar(half_i[0][:], bits, 16, None, ALU.logical_shift_right)
            st.wait(vec.tensor_scalar(half_i[1][:], bits, 0xFFFF, None, ALU.bitwise_and))
            vec.tensor_copy(key[1][:], half_i[1][:])
            st.wait(vec.tensor_copy(key[0][:], half_i[0][:]))
            vec.tensor_scalar(neg[:], key[0][:], 32768.0, None, ALU.is_ge)
            st.wait(vec.tensor_scalar(tmp[:], key[0][:], -2.0, 32767.0, ALU.mult, ALU.add))
            st.wait(vec.tensor_tensor(tmp[:], tmp[:], neg[:], ALU.mult))
            st.wait(vec.scalar_tensor_tensor(out=key[0][:], in0=key[0][:], scalar=32768.0, in1=tmp[:], op0=ALU.add, op1=ALU.add))
            st.wait(vec.tensor_scalar(tmp[:], key[1][:], -2.0, 65535.0, ALU.mult, ALU.add))
            st.wait(vec.tensor_tensor(tmp[:], tmp[:], neg[:], ALU.mult))
            st.wait(vec.tensor_tensor(key[1][:], key[1][:], tmp[:], ALU.add))
            for half in range(2):
                if half:
                    st.wait(vec.tensor_scalar(tmp[:], key[0][:], found[0][:], 65536.0, ALU.subtract, ALU.mult))
                    st.wait(vec.tensor_tensor(key[1][:], key[1][:], tmp[:], ALU.add))
                vec.memset(found[0][:], 0.0)
                vec.memset(unit[0][:], float(RADIX ** (DIGITS - 1)))
                st.wait(vec.tensor_scalar(cand[:], row[:, 1:RADIX], float(RADIX ** (DIGITS - 1)), None, ALU.mult))
                first = st.base + st.k
                with dve.Fori(0, DIGITS // 4) as i:
                    st.rebase(first + i * 12)
                    for n in range(4):
                        old, new = n % 2, 1 - n % 2
                        for j in range(RADIX - 1):
                            last = vec.tensor_scalar(junk[:, j, :], key[half][:], cand[:, j:j + 1], 0.0, ALU.is_ge, ALU.add,
                                                     accum_out=cnt[:, j:j + 1])
                        last.then_inc(counted, 1)
                        st.wait(vec.tensor_scalar(unit[new][:], unit[old][:], 1.0 / RADIX, None, ALU.mult))
                        vec.tensor_scalar(steps[:], row[:, 1:RADIX], unit[new][:], found[old][:], ALU.mult, ALU.add)
                        dve.wait_ge(totalled, 4 * i + (DIGITS * half + n + 1))
                        st.wait(vec.tensor_scalar(reached[:], tot_ps[:], float(KEPT), 0.0, ALU.is_ge, ALU.add, accum_out=digit[:]))
                        vec.scalar_tensor_tensor(out=found[new][:], in0=digit[:], scalar=unit[old][:], in1=found[old][:],
                                                 op0=ALU.mult, op1=ALU.add)
                        st.wait(vec.scalar_tensor_tensor(out=cand[:], in0=digit[:].to_broadcast([P, RADIX - 1]),
                                                         scalar=unit[old][:], in1=steps[:], op0=ALU.mult, op1=ALU.add))
                st.rebase(first + DIGITS * 3)
            top = found[0]
            vec.tensor_scalar(above[:], key[1][:], top[:], None, ALU.is_gt)
            vec.tensor_scalar(tied[:], key[1][:], top[:], None, ALU.is_equal).then_inc(ready, 1)

            def spread_totals(n):
                dve.wait_ge(summed, n + 1)
                vec.tensor_copy(total_b[:], col_ps[:].to_broadcast([NT, P])).then_inc(spread, 1)
                dve.wait_ge(ranked, n + 1)

            spread_totals(0)
            st.wait(vec.tensor_reduce(digit[:], all_ps[:], op=ALU.add, axis=AX.X))
            st.wait(vec.tensor_scalar(tied_left[:], digit[:], -1.0, float(KEPT), ALU.mult, ALU.add))
            st.wait(vec.tensor_scalar(tmp[:], rank_ps[:], tied_left[:], None, ALU.is_lt))
            st.wait(vec.tensor_tensor(tmp[:], tmp[:], tied[:], ALU.mult))
            vec.tensor_tensor(chosen[:], tmp[:], above[:], ALU.add).then_inc(ready, 1)
            spread_totals(1)
            st.wait(vec.scalar_tensor_tensor(out=rank[:], in0=rank_ps[:], scalar=1.0, in1=chosen[:], op0=ALU.add, op1=ALU.mult))
            st.wait(vec.tensor_scalar(rank_i[:], rank[:], -1.0, None, ALU.add))
            vec.tensor_scalar(part_i[0][:], rank_i[:], 7, None, ALU.arith_shift_right)
            st.wait(vec.tensor_scalar(part_i[1][:], rank_i[:], P - 1, None, ALU.bitwise_and))
            vec.tensor_copy(row_b[:], row[:])
            vec.tensor_copy(part[0][:], part_i[0][:])
            st.wait(vec.tensor_copy(part[1][:], part_i[1][:]))
            for n in range(NT // PART):
                r, t0 = n % 2, n * PART
                wait_if(dve, packed, n - 1)
                vec.tensor_tensor(in_tile[:, r, :, :], part[0][:, t0:t0 + PART].unsqueeze(2).to_broadcast([P, PART, SLOTS]),
                                  row_b[:, 0:SLOTS].unsqueeze(1).to_broadcast([P, PART, SLOTS]),
                                  ALU.is_equal).then_inc(tile_placed, 1)
                vec.tensor_tensor(in_slot[:, r, :, :], part[1][:, t0:t0 + PART].unsqueeze(2).to_broadcast([P, PART, P]),
                                  row_b[:].unsqueeze(1).to_broadcast([P, PART, P]), ALU.is_equal).then_inc(hot, 1)
            dve.wait_ge(packed, NT // PART)
            st.wait(vec.tensor_copy(number_f[:], num_ps[:]))
            vec.memset(kept_row[:, SLOTS:], 0)
            vec.scalar_tensor_tensor(out=kept_row[:, 0:SLOTS], in0=number_f[:, 0, :], scalar=float(P), in1=number_f[:, 1, :],
                                     op0=ALU.mult, op1=ALU.add)


def ffn(nc, kit):
    out, xn_dram, sem, sb, kept_row, w1_parts = kit.out, kit.xn_dram, kit.sem, kit.sb, kit.kept_row, kit.w1_parts
    w2_parts, b1_sb, b2_sb, wr_sb, br_sb = kit.w2_parts, kit.b1_sb, kit.b2_sb, kit.wr_sb, kit.br_sb
    D, KD, KH, KEPT, SLOTS, SG = kit.D, kit.KD, kit.KH, kit.KEPT, kit.SLOTS, kit.SG
    ident = kit.ident
    LAST_SLOTS = KEPT - (SLOTS - 1) * P
    with ExitStack() as c:
        def ps(name, shape):
            return c.enter_context(nc.psum_tensor(name, shape, F32))

        from_row = sb(c, "from_row", [P, 2, TG], I32)
        to_row = sb(c, "to_row", [P, 2, TG], I32)
        xg = sb(c, "xg", [P, 2, TG, D])
        xgT = sb(c, "xgT", [P, 2, 2, KD, TG * P], F32R)
        act_out = sb(c, "act_out", [P, 2, TG * P])
        hidden = sb(c, "hidden", [P, 2, KH, TG * P], F32R)
        route = sb(c, "route", [P, 2, TG])
        route_in = sb(c, "route_in", [P, 2, TG])
        junk = sb(c, "junk3", [P, TG, D])
        y1 = sb(c, "y1", [P, TG, D])
        y = sb(c, "y", [P, 2, TG, D])
        xt_ps = ps("xgt_ps", [P, KD, TG * P])
        up_ps = [ps(f"up_ps{i}", [P, TG * P]) for i in range(2)]
        y_ps = [ps(f"y_ps{i}", [P, TG, D]) for i in range(2)]
        from_ready = sem("from_ready")
        xg_loaded = [sem(f"xg_loaded{i}") for i in range(2)]
        xg_turned = sem("xg_turned")
        xgT_ready = sem("xgT_ready")
        routed = sem("routed")
        up_done = sem("up_done")
        gelu_done = sem("gelu_done")
        hidden_ready = sem("hidden_ready")
        down_done = sem("down_done")
        y_ready = sem("y_ready")
        y_added = [sem(f"y_added{i}") for i in range(2)]
        step = sem("ffn_dve_step")
        block = c.enter_context(nc.Block())
        HALF = SG // 2

        @block.gpsimd
        def _(pool):
            def gather(i, b, tiles=TG):
                g = 2 * i + b
                pool.wait_ge(from_ready, g + 1)
                wait_if(pool, xg_turned, g - 1)
                wait_if(pool, routed, g - 1)
                for k in range(tiles):
                    hold(kit, pool)
                    pool.indirect_dma_start(
                        out=xg[:, b, k, :], out_offset=None, in_=xn_dram,
                        in_offset=bass.IndirectOffsetOnAxis(ap=from_row[:, b, k:k + 1], axis=0)).then_inc(xg_loaded[b], 16)

            def add(i, b, tiles=TG):
                g = 2 * i + b
                pool.wait_ge(y_ready, g + 1)
                for k in range(tiles):
                    n = P if tiles == TG else LAST_SLOTS
                    hold(kit, pool)
                    pool.indirect_dma_start(
                        out=out, out_offset=bass.IndirectOffsetOnAxis(ap=to_row[0:n, b, k:k + 1], axis=0),
                        in_=y[0:n, b, k, :], in_offset=None,
                        compute_op=ALU.add).then_inc(y_added[b], 16)

            gather(0, 0)
            gather(0, 1)
            with pool.Fori(1, HALF) as i:
                for b in range(2):
                    gather(i, b)
                    add(i - 1, b)
            gather(HALF, 0, 1)
            add(HALF - 1, 0)
            add(HALF - 1, 1)
            add(HALF, 0, 1)
            pool.wait_ge(y_added[0], 16 * (TG * HALF + 1))
            pool.wait_ge(y_added[1], 16 * TG * HALF)

        @block.vector
        def _(dve):
            vec = nc.vector
            st = Steps(dve, step)

            a_step = 2 * (2 + 1 + KH)

            def take_from(i, b):
                vec.tensor_copy(from_row[:, b, :], kept_row[:, bass.ds((2 * i + b) * TG, TG)]).then_inc(from_ready, 1)

            def turn(i, b, tiles=TG):
                g = 2 * i + b
                dve.wait_ge(xg_turned, g + 1)
                wait_if(dve, up_done, KH * (g - 1))
                cols = slice(0, tiles * P)
                st.wait(vec.tensor_copy(xgT[:, b, 0, :, cols], xt_ps[:, :, cols]))
                vec.tensor_tensor(xgT[:, b, 1, :, cols], xt_ps[:, :, cols], xgT[:, b, 0, :, cols].bitcast(F32),
                                  ALU.subtract).then_inc(xgT_ready, 1)
                for k in range(tiles):
                    last = vec.tensor_tensor_reduce(out=junk[:, k, :], in0=xg[:, b, k, :], in1=wr_sb[:], scale=1.0, scalar=0.0,
                                                    op0=ALU.mult, op1=ALU.add, accum_out=route_in[:, b, k:k + 1])
                st.wait(last)
                vec.tensor_scalar(route[:, b, 0:tiles], route_in[:, b, 0:tiles], br_sb[:], None, ALU.add).then_inc(routed, 1)

            def split_hidden(i, b, tiles=TG):
                g = 2 * i + b
                cols = slice(0, tiles * P)
                wait_if(dve, down_done, g)
                for m in range(KH):
                    dve.wait_ge(gelu_done, KH * g + m + 1)
                    st.wait(vec.tensor_copy(hidden[:, 0, m, cols], act_out[:, m % 2, cols]))
                    vec.tensor_tensor(hidden[:, 1, m, cols], act_out[:, m % 2, cols], hidden[:, 0, m, cols].bitcast(F32),
                                      ALU.subtract).then_inc(hidden_ready, 1)

            def scale(i, b, tiles=TG):
                g = 2 * i + b
                dve.wait_ge(down_done, g + 1)
                wait_if(dve, y_ready, g)
                wait_if(dve, y_added[b], 16 * TG * i)
                vec.tensor_copy(to_row[:, b, 0:tiles], kept_row[:, bass.ds(g * TG, tiles)])
                st.wait(vec.tensor_tensor(y1[:, 0:tiles, :], y_ps[b][:, 0:tiles, :],
                                          b2_sb[:].unsqueeze(1).to_broadcast([P, tiles, D]), ALU.add))
                for k in range(tiles):
                    last = vec.tensor_scalar(y[:, b, k, :], y1[:, k, :], route[:, b, k:k + 1], None, ALU.mult)
                last.then_inc(y_ready, 1)

            take_from(0, 0)
            take_from(0, 1)
            turn(0, 0)
            take_from(1, 0)
            split_hidden(0, 0)
            turn(0, 1)
            take_from(1, 1)
            first = st.k
            with dve.Fori(1, HALF) as i:
                st.rebase(first + (i - 1) * a_step)
                split_hidden(i - 1, 1)
                scale(i - 1, 0)
                turn(i, 0)
                take_from(i + 1, 0)
                split_hidden(i, 0)
                scale(i - 1, 1)
                turn(i, 1)
                take_from(i + 1, 1)
                assert st.k == a_step
            st.rebase(first + (HALF - 1) * a_step)
            split_hidden(HALF - 1, 1)
            scale(HALF - 1, 0)
            turn(HALF, 0, 1)
            split_hidden(HALF, 0, 1)
            scale(HALF - 1, 1)
            scale(HALF, 0, 1)

        @block.tensor
        def _(pe):
            t = nc.tensor

            def turn(i, b, tiles=TG):
                g = 2 * i + b
                pe.wait_ge(xg_loaded[b], 16 * (TG * i + tiles))
                wait_if(pe, xgT_ready, g)
                for j in range(tiles):
                    for k in range(KD):
                        last = t.transpose(xt_ps[:, k, j * P:(j + 1) * P], xg[:, b, j, k * P:(k + 1) * P], ident[:])
                last.then_inc(xg_turned, 1)

            def up(i, b, tiles=TG):
                g = 2 * i + b
                pe.wait_ge(xgT_ready, g + 1)
                for m in range(KH):
                    wait_if(pe, gelu_done, KH * g + m - 1)
                    for n, (k, (pw, px)) in enumerate((k, p) for k in range(KD) for p in PAIRS):
                        last = t.matmul(up_ps[m % 2][:, 0:tiles * P], lhsT=w1_parts[:, pw, k, m * P:(m + 1) * P],
                                        rhs=xgT[:, b, px, k, 0:tiles * P], start=(n == 0), stop=(n == KD * len(PAIRS) - 1))
                    last.then_inc(up_done, 1)

            def down(i, b, tiles=TG):
                g = 2 * i + b
                wait_if(pe, y_ready, g - 1)
                for j in range(tiles):
                    for n, (m, (pw, px)) in enumerate((m, p) for m in range(KH) for p in PAIRS):
                        if j == 0 and n % len(PAIRS) == 0:
                            pe.wait_ge(hidden_ready, KH * g + m + 1)
                        last = t.matmul(y_ps[b][:, j, :], lhsT=hidden[:, px, m, j * P:(j + 1) * P],
                                        rhs=w2_parts[:, pw, m, :], start=(n == 0), stop=(n == KH * len(PAIRS) - 1))
                last.then_inc(down_done, 1)

            turn(0, 0)
            up(0, 0)
            turn(0, 1)
            down(0, 0)
            with pe.Fori(1, HALF) as i:
                up(i - 1, 1)
                turn(i, 0)
                down(i - 1, 1)
                up(i, 0)
                turn(i, 1)
                down(i, 0)
            up(HALF - 1, 1)
            turn(HALF, 0, 1)
            down(HALF - 1, 1)
            up(HALF, 0, 1)
            down(HALF, 0, 1)

        @block.scalar
        def _(act):
            def gelu(i, b, tiles=TG):
                g = 2 * i + b
                for m in range(KH):
                    act.wait_ge(up_done, KH * g + m + 1)
                    wait_if(act, hidden_ready, KH * g + m - 1)
                    act.activation(act_out[:, m % 2, 0:tiles * P], up_ps[m % 2][:, 0:tiles * P], ACT.Gelu_apprx_tanh,
                                   bias=b1_sb[:, m:m + 1]).then_inc(gelu_done, 1)

            gelu(0, 0)
            gelu(0, 1)
            with act.Fori(1, HALF) as i:
                gelu(i, 0)
                gelu(i, 1)
            gelu(HALF, 0, 1)


_INS = ["x", "src", "dst", "edge_weight", "L0_gnn_W", "L0_gnn_bias", "L0_ffn_wr", "L0_ffn_br", "L0_ffn_w1",
        "L0_ffn_b1", "L0_ffn_w2", "L0_ffn_b2"]
_OUTS = [((12500, 256), "float32")]


def kernel(**inputs):
    import numpy as _np
    import concourse.bacc as _bacc
    from concourse import mybir as _mybir
    from concourse.bass_utils import run_bass_kernel_spmd as _run

    nc = _bacc.Bacc("TRN2", target_bir_lowering=False, num_devices=1)
    arrays, args = {}, []
    for name in _INS:
        a = _np.ascontiguousarray(inputs[name])
        arrays[f"in_{name}"] = a
        args.append(nc.dram_tensor(f"in_{name}", a.shape, _mybir.dt.from_np(a.dtype), kind="ExternalInput").ap())
    for i, (shape, dtype) in enumerate(_OUTS):
        args.append(nc.dram_tensor(f"out_{i}", shape, _mybir.dt.from_np(_np.dtype(dtype)), kind="ExternalOutput").ap())
    build(nc, *args)
    r = _run(nc, [arrays], core_ids=[0])
    return r.results[0]["out_0"]
```
